# Optimizing a Trainium2 kernel written in Bass

```python
import numpy as np
import jax
import jax.numpy as jnp

def _softmax(x, axis=-1):
    return jax.nn.softmax(x, axis=axis)

def _gelu(x):
    return jax.nn.gelu(x, approximate=True)

def _silu(x):
    return jax.nn.silu(x)

def _sigmoid(x):
    return jax.nn.sigmoid(x)

def _layernorm(x, axis=-1, eps=1e-05):
    m = jnp.mean(x, axis=axis, keepdims=True)
    v = jnp.var(x, axis=axis, keepdims=True)
    return (x - m) / jnp.sqrt(v + eps)

def _scatter_add(tgt, idx, src, axis=0):
    return tgt.at[idx].add(src)

def _segment_sum(src, seg, n):
    return jax.ops.segment_sum(src, seg, n)
kernel_name = 'mk_macaron_d1_jaxref_r4_932f1e'

def setup_inputs(seed: int=0):
    np.random.seed(seed)
    _w = jnp.asarray

    def _L0_attn_setup():
        import jax, jax.numpy as jnp
        from jax import lax
        import numpy as np
        INPUT_DIM, STATE_DIM, CONV_K, EXPAND = (256, 16, 4, 2)
        INNER = INPUT_DIM * EXPAND
        BATCH, SEQ = (2, 512)
        key = jax.random.key(seed)
        ks = jax.random.split(key, 6)
        x = jax.random.normal(ks[0], (BATCH, SEQ, INPUT_DIM), jnp.float32)
        W_in = jax.random.normal(ks[1], (2 * INNER, INPUT_DIM), jnp.float32) * 0.02
        conv_w = jax.random.normal(ks[2], (INNER, 1, CONV_K), jnp.float32) * 0.1
        conv_b = jnp.zeros((INNER,), jnp.float32)
        A_log = jax.random.normal(ks[3], (INNER, STATE_DIM), jnp.float32)
        D = jnp.ones((INNER,), jnp.float32)
        W_out = jax.random.normal(ks[4], (INPUT_DIM, INNER), jnp.float32) * 0.02
        return {'x': x, 'W_in': W_in, 'conv_w': conv_w, 'conv_b': conv_b, 'A_log': A_log, 'D': D, 'W_out': W_out}
    _L0_attn_in = _L0_attn_setup()

    def _L0_ffn_setup():
        import jax, jax.numpy as jnp
        import numpy as np
        SINKHORN_ITERS = 8
        TEMPERATURE = 1.0
        EPS = 1e-06

        def sinkhorn(t):
            t = jnp.log(jnp.clip(t, EPS)) / TEMPERATURE
            for _ in range(SINKHORN_ITERS):
                t = t - jax.nn.logsumexp(t, axis=-2, keepdims=True)
                t = t - jax.nn.logsumexp(t, axis=-1, keepdims=True)
            return jnp.exp(t)
        key = jax.random.key(seed)
        k1, k2, k3 = jax.random.split(key, 3)
        B, N, D, E = (4, 1024, 256, 8)
        x = jax.random.normal(k1, (B, N, D), dtype=jnp.float32)
        gate_w = jax.random.normal(k2, (D, E), dtype=jnp.float32) * D ** (-0.5)
        experts = jax.random.normal(k3, (E, D, D), dtype=jnp.float32) * D ** (-0.5)
        return {'x': x, 'gate_w': gate_w, 'experts': experts}
    _L0_ffn_in = _L0_ffn_setup()
    _d = {'L0_attn_x': _L0_attn_in['x'], 'L0_attn_W_in': _L0_attn_in['W_in'], 'L0_attn_conv_w': _L0_attn_in['conv_w'], 'L0_attn_conv_b': _L0_attn_in['conv_b'], 'L0_attn_A_log': _L0_attn_in['A_log'], 'L0_attn_D': _L0_attn_in['D'], 'L0_attn_W_out': _L0_attn_in['W_out'], 'L0_ffn_gate_w': _L0_ffn_in['gate_w'], 'L0_ffn_experts': _L0_ffn_in['experts']}
    _x0 = _d['L0_attn_x']
    _d['L0_attn_x'] = jax.random.normal(jax.random.fold_in(jax.random.key(seed), 1), (8, 2048, 256), dtype=_x0.dtype)
    del _x0
    return _d

def reference(L0_attn_x, L0_attn_W_in, L0_attn_conv_w, L0_attn_conv_b, L0_attn_A_log, L0_attn_D, L0_attn_W_out, L0_ffn_gate_w, L0_ffn_experts):

    def _L0_attn_ref(x, W_in, conv_w, conv_b, A_log, D, W_out):
        import jax, jax.numpy as jnp
        from jax import lax
        import numpy as np
        INPUT_DIM, STATE_DIM, CONV_K, EXPAND = (256, 16, 4, 2)
        INNER = INPUT_DIM * EXPAND
        BATCH, SEQ = (2, 512)
        b, s, _ = x.shape
        inner = W_in.shape[0] // 2
        K = conv_w.shape[-1]
        state = A_log.shape[1]
        xr = x @ W_in.T
        x_ssm, res = (xr[..., :inner], xr[..., inner:])
        xc = jnp.transpose(x_ssm, (0, 2, 1))
        xc = jnp.pad(xc, ((0, 0), (0, 0), (K - 1, 0)))
        xc = lax.conv_general_dilated(xc, conv_w, (1,), 'VALID', feature_group_count=inner, dimension_numbers=('NCH', 'OIH', 'NCH'))
        x_conv = jax.nn.silu(jnp.transpose(xc, (0, 2, 1)) + conv_b)
        delta = jax.nn.softplus(x_conv)
        A = -jnp.exp(A_log)
        A_d = jnp.exp(delta[..., None] * A)
        Bx = x_conv * x_conv

        def step(h, inp):
            a_t, bx_t, c_t = inp
            h = a_t * h + bx_t[..., None]
            y = c_t * jnp.sum(h, axis=-1)
            return (h, y)
        h0 = jnp.zeros((b, inner, state), x.dtype)
        _, ys = lax.scan(step, h0, (jnp.moveaxis(A_d, 1, 0), jnp.moveaxis(Bx, 1, 0), jnp.moveaxis(x_conv, 1, 0)))
        y_ssm = jnp.moveaxis(ys, 0, 1)
        y = y_ssm * jax.nn.silu(res) + D * x_conv
        return y @ W_out.T

    def _L0_ffn_ref(x, gate_w, experts):
        import jax, jax.numpy as jnp
        import numpy as np
        SINKHORN_ITERS = 8
        TEMPERATURE = 1.0
        EPS = 1e-06

        def sinkhorn(t):
            t = jnp.log(jnp.clip(t, EPS)) / TEMPERATURE
            for _ in range(SINKHORN_ITERS):
                t = t - jax.nn.logsumexp(t, axis=-2, keepdims=True)
                t = t - jax.nn.logsumexp(t, axis=-1, keepdims=True)
            return jnp.exp(t)
        B, N, D = x.shape
        E = gate_w.shape[-1]
        M = N // E
        gate_logits = jnp.einsum('bnd,de->bne', x, gate_w)
        competitive_gates = sinkhorn(gate_logits)
        vals, idx = jax.lax.top_k(jnp.swapaxes(competitive_gates, -1, -2), M)
        gate_values = jnp.swapaxes(vals, -1, -2)
        routed_indices = jnp.swapaxes(idx, -1, -2)
        b_idx = jnp.arange(B)[:, None, None]
        routed = x[b_idx, routed_indices]
        routed = jnp.transpose(routed, (2, 0, 1, 3))
        outputs = jnp.einsum('ebmd,edf->ebmf', routed, experts)
        outputs = outputs * jnp.transpose(gate_values, (2, 0, 1))[..., None]
        vals_bmed = jnp.transpose(outputs, (1, 2, 0, 3))
        routed_back = jnp.zeros_like(x).at[b_idx, routed_indices].set(vals_bmed)
        return routed_back
    x = L0_attn_x
    x = x + 0.5 * _L0_ffn_ref(_layernorm(x, axis=-1), L0_ffn_gate_w, L0_ffn_experts)
    x = x + _L0_attn_ref(_layernorm(x, axis=-1), L0_attn_W_in, L0_attn_conv_w, L0_attn_conv_b, L0_attn_A_log, L0_attn_D, L0_attn_W_out)
    x = x + 0.5 * _L0_ffn_ref(_layernorm(x, axis=-1), L0_ffn_gate_w, L0_ffn_experts)
    return x

_drawn_inputs = setup_inputs


def setup_inputs(seed=0):
    import zlib

    import numpy as np

    out = dict(_drawn_inputs(seed))
    spreads = {'L0_attn_conv_b': (0.0, 0.1), 'L0_attn_D': (1.0, 0.592)}
    factors = {'L0_attn_A_log': 7.58}
    for name, (base, spread) in spreads.items():
        noise = np.random.default_rng([zlib.crc32(name.encode()), seed]).standard_normal(out[name].shape)
        drawn = base * np.exp(spread * noise) if base else spread * noise
        out[name] = jnp.asarray(drawn.astype(out[name].dtype))
    for name, factor in factors.items():
        out[name] = (out[name] * factor).astype(out[name].dtype)
    return out
```

```python
from contextlib import ExitStack

import numpy as np

import concourse.bass as bass
from concourse import mybir

ALU = mybir.AluOpType
ACT = mybir.ActivationFunctionType
F32 = mybir.dt.float32
BF16 = mybir.dt.bfloat16
I32 = mybir.dt.int32
U32 = mybir.dt.uint32
AX = mybir.AxisListType

P = 128
NB = 8
NT = 2048
D = 256
KD = D // P
T = NT // P
E = 8
M = NT // E
NH = M // P
SL = E * NH
R = NB * E
YR = E * (M + 1)
ITERS = 8
INNER = 512
J = INNER // P
N = 16
KC = 4
CH = 512
C = NT // CH
LN_EPS = 1e-5
CLIP = 1e-6


class Bag:
    pass


def count(value):
    return max(value, 0) if isinstance(value, int) else value


def constants(nc, g, w, ctx):

    def sb(name, shape, dt=F32):
        return ctx.enter_context(nc.sbuf_tensor(name, shape, dt))

    g.ident = sb("ident", [P, P])
    g.ones = sb("ones", [P, P])
    g.iota_col = sb("iota_col", [P, P])
    g.rank_of = sb("rank_of", [P, NH])
    g.expert_of = sb("expert_of", [P, R])
    g.token_base = sb("token_base", [P, NB])
    g.gate_w = sb("gate_w", [P, KD, E])
    g.w_in = sb("w_in", [P, KD, 2 * INNER])
    g.w_out = sb("w_out", [P, J, D])
    g.conv_w = sb("conv_w", [P, J, KC])
    g.conv_b = sb("conv_b", [P, J])
    g.skip = sb("skip", [P, J])
    g.neg_a = sb("neg_a", [P, J, N])
    g.slot_token = sb("slot_token", [P, NB, SL], I32)
    g.slot_gate = sb("slot_gate", [P, NB, SL])
    g.token_row = sb("token_row", [P, NB, T], I32)

    g.passed_dve, g.passed_pool, g.passed_sp = (
        ctx.enter_context(nc.semaphore(n)) for n in ("passed_dve", "passed_pool", "passed_sp"))

    with ExitStack() as c2:
        zrow = c2.enter_context(nc.sbuf_tensor("zero_row", [E, D], F32))
        zeroed = c2.enter_context(nc.semaphore("zeroed"))
        loaded = ctx.enter_context(nc.semaphore("weights_loaded"))
        a_loaded = c2.enter_context(nc.semaphore("a_log_loaded"))
        a_exp = c2.enter_context(nc.semaphore("a_exp_done"))
        zero_stored = c2.enter_context(nc.semaphore("zero_rows_stored"))
        block = c2.enter_context(nc.Block())

        @block.gpsimd
        def _(pool):
            nc.gpsimd.memset(zrow[:], 0.0).then_inc(zeroed, 1)
            nc.gpsimd.memset(g.ident[:], 0.0).then_inc(zeroed, 1)
            nc.gpsimd.memset(g.ones[:], 1.0)
            pool.wait_ge(zeroed, 2)
            nc.gpsimd.affine_select(out=g.ident[:], in_=g.ident[:], compare_op=ALU.not_equal, fill=1.0,
                                    base=0, pattern=[[-1, P]], channel_multiplier=1)
            for out, pattern, base, mult in (
                (g.iota_col[:], [[1, P]], 0, 0),
                (g.rank_of[:], [[P, NH]], 1, 1),
                (g.expert_of[:], [[0, NB], [1, E]], 0, 0),
                (g.token_base[:], [[NT, NB]], 0, 0),
            ):
                nc.gpsimd.iota(out, pattern, base=base, channel_multiplier=mult,
                               allow_small_or_imprecise_dtypes=True)

        @block.sync
        def _(sp):
            sp.dma_start(g.neg_a[:], w.A_log.rearrange("(j p) n -> p j n", p=P)).then_inc(a_loaded, 16)
            sp.dma_start(g.gate_w[:], w.gate_w.rearrange("(k p) e -> p k e", p=P)).then_inc(loaded, 16)
            sp.dma_start(g.w_in[:], w.w_in_t.rearrange("(k p) c -> p k c", p=P)).then_inc(loaded, 16)
            sp.dma_start(g.w_out[:], w.w_out_t.rearrange("(j p) d -> p j d", p=P)).then_inc(loaded, 16)
            sp.dma_start(g.conv_w[:], w.conv_w.rearrange("(j p) k -> p j k", p=P)).then_inc(loaded, 16)
            sp.dma_start(g.conv_b[:], w.conv_b_t).then_inc(loaded, 16)
            sp.dma_start(g.skip[:], w.skip_t).then_inc(loaded, 16)
            sp.wait_ge(zeroed, 1)
            for table in g.routed:
                sp.dma_start(table[0:E, :], zrow[:]).then_inc(zero_stored, 16)
            sp.wait_ge(loaded, 6 * 16)
            sp.wait_ge(zero_stored, 2 * 16)

        @block.scalar
        def _(act):
            act.wait_ge(a_loaded, 16)
            flat = g.neg_a[:].rearrange("p j n -> p (j n)")
            nc.scalar.activation(flat, flat, ACT.Exp).then_inc(a_exp, 1)
            act.wait_ge(a_exp, 1)
            nc.scalar.mul(flat, flat, -1.0)


def route(nc, g, x, tag):
    x_in = x.rearrange("b (p t) d -> b p t d", t=T)
    xn_out = g.normed.rearrange("(b p t) d -> b p t d", p=P, t=T)
    with ExitStack() as ctx:
        def sb(name, shape, dt=F32):
            return ctx.enter_context(nc.sbuf_tensor(f"{name}_{tag}", shape, dt))

        def sem(name):
            return ctx.enter_context(nc.semaphore(f"{name}_{tag}"))

        probs = sb("probs", [P, T, NB, E])
        with ExitStack() as c1:
            logits_stage(nc, g, x_in, xn_out, probs, tag, c1)
        with ExitStack() as c1:
            rows = sinkhorn_stage(nc, g, probs, tag, ctx, c1)
        with ExitStack() as c1:
            top_stage(nc, g, rows, tag, c1)


def logits_stage(nc, g, x_in, xn_out, probs, tag, ctx):
    def sb(name, shape, dt=F32):
        return ctx.enter_context(nc.sbuf_tensor(f"{name}_{tag}", shape, dt))

    def sem(name):
        return ctx.enter_context(nc.semaphore(f"{name}_{tag}"))

    U = 2
    rows_ = [sb(f"rows{u}", [P, T, D]) for u in range(U)]
    stats = [sb(f"stats{u}", [P, T, 6]) for u in range(U)]
    moments = [sb(f"moments{u}", [P, T, 2]) for u in range(U)]
    std = [sb(f"std{u}", [P, T]) for u in range(U)]
    rstd = [sb(f"rstd{u}", [P, T]) for u in range(U)]
    shift = [sb(f"shift{u}", [P, T]) for u in range(U)]
    eps = sb("eps", [P, 1])
    turned = [sb(f"turned{u}", [P, KD, P]) for u in range(2)]
    ps_turn = [ctx.enter_context(nc.psum_tensor(f"ps_turn{u}_{tag}", [P, CH], F32)) for u in range(2)]
    ps_logit = [ctx.enter_context(nc.psum_tensor(f"ps_logit{u}_{tag}", [P, CH], F32)) for u in range(2)]

    def turns(eng, turn):
        turn(0)
        with eng.Fori(1, NB // U) as it:
            turn(it)

    row_in = [sem(f"row_in{u}") for u in range(U)]
    row_out = [sem(f"row_out{u}") for u in range(U)]
    eps_set, stats_done, moments_done, std_done, rstd_done, shift_done = (
        sem(n) for n in ("eps_set", "stats_done", "moments_done", "std_done", "rstd_done", "shift_done"))
    normed, turns_done, turned_copied, logits_done, probs_done = (
        sem(n) for n in ("normed", "turns_done", "turned_copied", "logits_done", "probs_done"))
    block = ctx.enter_context(nc.Block())

    @block.sync
    def _(sp):
        def turn(it):
            for u in range(U):
                b = it * U + u
                sp.wait_ge(row_out[u], it * 16)
                sp.sem_inc(g.passed_sp, 1)
                sp.wait_ge(logits_done, count((b - U + 1) * T))
                sp.dma_start(rows_[u][:], x_in[bass.ds(b, 1)].rearrange("a p t d -> p (a t) d")
                             ).then_inc(row_in[u], 16)
            for u in range(U):
                b = it * U + u
                sp.wait_ge(normed, (b + 1) * T)
                sp.dma_start(xn_out[bass.ds(b, 1)].rearrange("a p t d -> p (a t) d"), rows_[u][:]
                             ).then_inc(row_out[u], 16)

        turns(sp, turn)
        for u in range(U):
            sp.wait_ge(row_out[u], 16 * NB // U)

    @block.vector
    def _(dve):
        def turn(it):
            for u in range(U):
                b = it * U + u
                dve.wait_ge(row_in[u], (it + 1) * 16)
                for t in range(T):
                    nc.vector.bn_stats(stats[u][:, t, :], rows_[u][:, t, :]).then_inc(stats_done, 1)
                dve.wait_ge(stats_done, (b + 1) * T)
                dve.sem_inc(g.passed_dve, 1)
                for t in range(T):
                    nc.vector.bn_aggr(moments[u][:, t, :], stats[u][:, t, :]).then_inc(moments_done, 1)
                dve.wait_ge(std_done, b + 1)
                nc.vector.reciprocal(rstd[u][:], std[u][:]).then_inc(rstd_done, 1)
                dve.wait_ge(rstd_done, b + 1)
                nc.vector.scalar_tensor_tensor(shift[u][:], moments[u][:, :, 0], -1.0, rstd[u][:],
                                               ALU.mult, ALU.mult).then_inc(shift_done, 1)
                for t in range(T):
                    dve.wait_ge(turns_done, b * T + t + 1)
                    if t >= 2:
                        dve.wait_ge(logits_done, count(b * T + t - 1))
                    nc.vector.tensor_copy(turned[t % 2][:].rearrange("p k n -> p (k n)"),
                                          ps_turn[t % 2][:, 0:KD * P]).then_inc(turned_copied, 1)
                dve.wait_ge(logits_done, (b + 1) * T)
                nc.vector.tensor_scalar(
                    probs[:, :, bass.ds(b, 1), :].rearrange("p t a e -> p t (a e)"),
                    ps_logit[u][:, 0:T * E].rearrange("p (t e) -> p t e", e=E),
                    CLIP, None, ALU.max).then_inc(probs_done, 1)

        nc.vector.memset(eps[:], LN_EPS).then_inc(eps_set, 1)
        turns(dve, turn)

    @block.scalar
    def _(act):
        def turn(it):
            for u in range(U):
                b = it * U + u
                act.wait_ge(moments_done, (b + 1) * T)
                nc.scalar.activation(std[u][:], moments[u][:, :, 1], ACT.Sqrt, bias=eps[:, 0:1]
                                     ).then_inc(std_done, 1)
                act.wait_ge(shift_done, b + 1)
                for t in range(T):
                    nc.scalar.activation(rows_[u][:, t, :], rows_[u][:, t, :], ACT.Identity,
                                         bias=shift[u][:, t:t + 1], scale=rstd[u][:, t:t + 1]
                                         ).then_inc(normed, 1)

        act.wait_ge(eps_set, 1)
        turns(act, turn)

    @block.tensor
    def _(pe):
        def transpose(b, u, t):
            pe.wait_ge(normed, b * T + t + 1)
            if t >= 2:
                pe.wait_ge(turned_copied, count(b * T + t - 1))
            for k in range(KD):
                mm = nc.tensor.transpose(ps_turn[t % 2][:, k * P:(k + 1) * P],
                                         rows_[u][:, t, k * P:(k + 1) * P], g.ident[:])
            mm.then_inc(turns_done, 1)

        def logit(b, u, t):
            pe.wait_ge(turned_copied, b * T + t + 1)
            if t == 0:
                pe.wait_ge(probs_done, count(b - U + 1))
            for k in range(KD):
                mm = nc.tensor.matmul(ps_logit[u][:, t * E:(t + 1) * E], turned[t % 2][:, k, :],
                                      g.gate_w[:, k, :], start=(k == 0), stop=(k == KD - 1))
            mm.then_inc(logits_done, 1)

        def turn(it):
            for u in range(U):
                b = it * U + u
                transpose(b, u, 0)
                for t in range(T):
                    if t + 1 < T:
                        transpose(b, u, t + 1)
                    logit(b, u, t)

        turns(pe, turn)


def sinkhorn_stage(nc, g, probs, tag, outer, ctx):
    def sb(name, shape, dt=F32, c=ctx):
        return c.enter_context(nc.sbuf_tensor(f"{name}_{tag}", shape, dt))

    def sem(name):
        return ctx.enter_context(nc.semaphore(f"{name}_{tag}"))

    rows = sb("gate_rows", [R, NT], c=outer)
    r = sb("token_scale", [P, T * NB])
    c_ = sb("expert_scale", [P, R])
    token_sum = sb("token_sum", [P, T * NB])
    scaled = sb("scaled", [P, T * NB, E])
    weighted = sb("weighted", [P, T, R])
    ps_sum = ctx.enter_context(nc.psum_tensor(f"ps_sum_{tag}", [P, CH], F32))
    ps_rows = [ctx.enter_context(nc.psum_tensor(f"ps_rows{i}_{tag}", [P, CH], F32)) for i in range(4)]
    weighted_done, sums_done, c_done, scaled_done, token_sums_done, r_done, gates_done, turned, copied = (
        sem(n) for n in ("weighted", "expert_sums", "expert_scale", "scaled", "token_sums", "token_scale",
                         "gates", "gates_turned", "gates_copied"))
    block = ctx.enter_context(nc.Block())
    flat = probs[:].rearrange("p t b e -> p (t b) e")

    @block.vector
    def _(dve):
        nc.vector.memset(r[:], 1.0).then_inc(r_done, 1)
        for i in range(ITERS):
            dve.wait_ge(r_done, i + 1)
            nc.vector.tensor_tensor(weighted[:].rearrange("p t (b e) -> p (t b) e", e=E), flat,
                                    r[:].unsqueeze(2).to_broadcast([P, T * NB, E]), ALU.mult
                                    ).then_inc(weighted_done, 1)
            dve.wait_ge(sums_done, i + 1)
            nc.vector.reciprocal(c_[:], ps_sum[:, 0:R]).then_inc(c_done, 1)
            dve.wait_ge(c_done, i + 1)
            nc.vector.tensor_tensor(scaled[:].rearrange("p (t b) e -> p t (b e)", b=NB),
                                    probs[:].rearrange("p t b e -> p t (b e)"),
                                    c_[:].unsqueeze(1).to_broadcast([P, T, R]), ALU.mult
                                    ).then_inc(scaled_done, 1)
            dve.wait_ge(scaled_done, i + 1)
            nc.vector.tensor_reduce(token_sum[:], scaled[:], AX.X, ALU.add).then_inc(token_sums_done, 1)
            dve.wait_ge(token_sums_done, i + 1)
            nc.vector.reciprocal(r[:], token_sum[:]).then_inc(r_done, 1)
        dve.wait_ge(r_done, ITERS + 1)
        nc.vector.tensor_tensor(weighted[:].rearrange("p t (b e) -> p (t b) e", e=E), scaled[:],
                                r[:].unsqueeze(2).to_broadcast([P, T * NB, E]), ALU.mult
                                ).then_inc(gates_done, 1)
        for i in range(4):
            dve.wait_ge(turned, 4 * (i + 1))
            nc.vector.tensor_copy(rows[:].rearrange("r (p t) -> r t p", t=T)[:, 4 * i:4 * i + 4, :],
                                  ps_rows[i][0:R, :].rearrange("r (t p) -> r t p", p=P)).then_inc(copied, 1)

    @block.tensor
    def _(pe):
        for i in range(ITERS):
            pe.wait_ge(weighted_done, i + 1)
            if i:
                pe.wait_ge(c_done, i)
            for t in range(T):
                mm = nc.tensor.matmul(ps_sum[:, 0:R], g.ones[:], weighted[:, t, :],
                                      start=(t == 0), stop=(t == T - 1))
            mm.then_inc(sums_done, 1)
        pe.wait_ge(gates_done, 1)
        for t in range(T):
            nc.tensor.transpose(ps_rows[t // 4][0:R, (t % 4) * P:(t % 4 + 1) * P], weighted[:, t, :],
                                g.ident[:]).then_inc(turned, 1)
    return rows


def top_stage(nc, g, rows, tag, ctx):
    def sb(name, shape, dt=F32):
        return ctx.enter_context(nc.sbuf_tensor(f"{name}_{tag}", shape, dt))

    def sem(name):
        return ctx.enter_context(nc.semaphore(f"{name}_{tag}"))

    vals = sb("top_vals", [R, M])
    idx = sb("top_idx", [R, M], U32)
    idx_f = sb("top_idx_f", [R, M])
    token_f = sb("token_f", [P, R, NH])
    token_i = sb("token_i", [P, R * NH], I32)
    part_i = sb("part_i", [P, R * NH], I32)
    tile_i = sb("tile_i", [P, R * NH], I32)
    part_f = sb("part_f", [P, R * NH])
    tile_f = sb("tile_f", [P, R * NH])
    at_tile = sb("at_tile", [P, R * NH, T], BF16)
    NU = 4
    at_part = [sb(f"at_part{i}", [P, P], BF16) for i in range(NU)]
    key = sb("key", [P, R, T])
    won = sb("won", [P, NB, T])
    ps_t = ctx.enter_context(nc.psum_tensor(f"ps_t_{tag}", [P, CH], F32))
    ps_v = ctx.enter_context(nc.psum_tensor(f"ps_v_{tag}", [P, CH], F32))
    ps_rank = ctx.enter_context(nc.psum_tensor(f"ps_rank_{tag}", [P, R * T], F32))
    maxed, indexed, replaced, idx_conv, moved, tok_copied, chain, gate_copied = (
        sem(n) for n in ("maxed", "indexed", "replaced", "idx_converted", "slots_turned",
                         "tokens_copied", "index_step", "gates_copied2"))
    part_built, part_used = sem("part_built"), sem("part_used")
    block = ctx.enter_context(nc.Block())

    @block.vector
    def _(dve):
        for k in range(M // 8):
            s = slice(8 * k, 8 * k + 8)
            if k:
                dve.wait_ge(replaced, k)
            nc.vector.max(vals[:, s], rows[:]).then_inc(maxed, 1)
            dve.wait_ge(maxed, k + 1)
            nc.vector.max_index(idx[:, s], vals[:, s], rows[:]).then_inc(indexed, 1)
            if k + 1 < M // 8:
                dve.wait_ge(indexed, k + 1)
                nc.vector.match_replace(rows[:], vals[:, s], rows[:], -1.0).then_inc(replaced, 1)
        dve.wait_ge(indexed, M // 8)
        nc.vector.tensor_copy(idx_f[:], idx[:]).then_inc(idx_conv, 1)
        dve.wait_ge(moved, 1)
        nc.vector.tensor_copy(token_f[:], ps_t[:, 0:R * NH].rearrange("p (h r) -> p r h", h=NH)
                              ).then_inc(tok_copied, 1)
        n_chain = [0]

        def step(ins):
            n_chain[0] += 1
            ins.then_inc(chain, 1)
            dve.wait_ge(chain, n_chain[0])

        dve.wait_ge(tok_copied, 1)
        flat = token_f[:].rearrange("p r h -> p (r h)")
        step(nc.vector.tensor_copy(token_i[:], flat))
        step(nc.vector.tensor_scalar(part_i[:], token_i[:], 4, None, ALU.logical_shift_right))
        step(nc.vector.tensor_scalar(tile_i[:], token_i[:], T - 1, None, ALU.bitwise_and))
        step(nc.vector.tensor_copy(part_f[:], part_i[:]))
        step(nc.vector.tensor_copy(tile_f[:], tile_i[:]))
        nc.vector.tensor_tensor(g.slot_token[:], token_f[:].rearrange("p (b e) h -> p b (e h)", b=NB),
                                g.token_base[:].unsqueeze(2).to_broadcast([P, NB, SL]), ALU.add)
        step(nc.vector.tensor_tensor(at_tile[:], tile_f[:].unsqueeze(2).to_broadcast([P, R * NH, T]),
                                     g.iota_col[:, 0:T].unsqueeze(1).to_broadcast([P, R * NH, T]),
                                     ALU.is_equal))
        for q in range(R * NH):
            if q >= NU:
                dve.wait_ge(part_used, count(q - NU + 1))
            nc.vector.tensor_scalar(at_part[q % NU][:], g.iota_col[:], part_f[:, q:q + 1],
                                    g.rank_of[:, q % NH:q % NH + 1], ALU.is_equal, ALU.mult
                                    ).then_inc(part_built, 1)
        dve.wait_ge(part_used, R * NH)
        ranks = ps_rank[:].rearrange("p (r t) -> p r t", t=T)
        step(nc.vector.scalar_tensor_tensor(key[:], ranks, float(E),
                                            g.expert_of[:].unsqueeze(2).to_broadcast([P, R, T]),
                                            ALU.mult, ALU.add))
        step(nc.vector.scalar_tensor_tensor(key[:], ranks, 0.0, key[:], ALU.is_gt, ALU.mult))
        step(nc.vector.tensor_reduce(won[:], key[:].rearrange("p (b e) t -> p b t e", e=E), AX.X, ALU.max))
        nc.vector.tensor_copy(g.token_row[:], won[:])

    @block.scalar
    def _(act):
        act.wait_ge(moved, 2)
        nc.scalar.mul(g.slot_gate[:].rearrange("p b (e h) -> p (b e) h", h=NH),
                      ps_v[:, 0:R * NH].rearrange("p (h r) -> p r h", h=NH), 0.5).then_inc(gate_copied, 1)

    @block.tensor
    def _(pe):
        pe.wait_ge(idx_conv, 1)
        for src, dst in ((idx_f, ps_t), (vals, ps_v)):
            for h in range(NH):
                mm = nc.tensor.transpose(dst[:, h * R:(h + 1) * R], src[:, h * P:(h + 1) * P],
                                         g.ident[0:R, 0:R])
            mm.then_inc(moved, 1)
        for q in range(R * NH):
            row = q // NH
            pe.wait_ge(part_built, q + 1)
            nc.tensor.matmul(ps_rank[:, row * T:(row + 1) * T], at_part[q % NU][:], at_tile[:, q, :],
                             start=(q % NH == 0), stop=(q % NH == NH - 1)).then_inc(part_used, 1)


def mixer(nc, g, x, ctx):
    def sb(name, shape, dt=F32):
        return ctx.enter_context(nc.sbuf_tensor(name, shape, dt))

    def sem(name):
        return ctx.enter_context(nc.semaphore(name))

    def ps(name):
        return ctx.enter_context(nc.psum_tensor(name, [P, CH], F32))

    NA, NHB, NX, NY, NRES = 2, 4, 3, 2, 4
    LEAD = NHB
    FFN = 2
    decay = [sb(f"decay{i}", [P, NT]) for i in range(NA)]
    state = [sb(f"state{i}", [P, NT]) for i in range(NHB)]
    conv_in = sb("conv_in", [P, KC - 1 + NT])
    xc = [sb(f"xc{i}", [P, NT]) for i in range(J + 1)]
    res = sb("res", [P, NT])
    delta = [sb(f"delta{i}", [P, NT]) for i in range(2)]
    drive = [sb(f"drive{i}", [P, NT]) for i in range(2)]
    x1 = sb("x1", [P, T, D])
    x1t = sb("x1t", [P, KD, NT])
    resid = [sb(f"resid{i}", [P, 2, D]) for i in range(NRES)]
    picked = [sb(f"picked{i}", [P, D]) for i in range(NX)]
    picked_t = [sb(f"picked_t{i}", [P, KD, P]) for i in range(2)]
    routed = [sb(f"routed{i}", [P, D]) for i in range(NY)]
    back = [sb(f"back{i}", [P, D]) for i in range(NY)]
    expert = [sb(f"expert{i}", [P, KD, D]) for i in range(2)]
    slot_now = sb("slot_now", [P, SL], I32)
    gate_now = sb("gate_now", [P, SL])
    row_now = sb("row_now", [P, T], I32)
    stats = sb("m_stats", [P, T, 6])
    moments = sb("m_moments", [P, T, 2])
    std = sb("m_std", [P, T])
    rstd = sb("m_rstd", [P, T])
    shift = sb("m_shift", [P, T])
    eps = sb("m_eps", [P, 1])
    ps_sum = [ps(f"ps_states{c}") for c in range(C)]
    ps_proj = [ps(f"ps_proj{i}") for i in range(2)]
    ps_misc = [ps(f"ps_misc{i}") for i in range(2)]

    decay_ready = sem("decay_ready")
    state_ready = sem("state_ready")
    state_used = [sem(f"state_used{i}") for i in range(NHB)]
    setup = sem("m_setup")
    ssm_done, ssm_copied, conv_step, conv_done = (sem(n) for n in ("ssm_done", "ssm_copied", "conv_step", "conv_done"))
    res_done, res_gated, xc_done, soft_step, soft_done, drive_done, delta_done = (
        sem(n) for n in ("res_done", "res_gated", "xc_done", "soft_step", "soft_done", "drive_done", "delta_done"))
    gated, y_done, out_done, out_added = (sem(n) for n in ("gated", "y_done", "out_done", "out_added"))
    now_set = sem("now_set")
    picked_in = [sem(f"picked_in{i}") for i in range(NX)]
    pick_turned, pick_copied, expert_done, routed_scaled = (
        sem(n) for n in ("pick_turned", "pick_copied", "expert_done", "routed_scaled"))
    expert_in = [sem(f"expert_in{i}") for i in range(2)]
    routed_out = [sem(f"routed_out{i}") for i in range(NY)]
    back_in = [sem(f"back_in{i}") for i in range(NY)]
    x_in, x1_added, x1_stored = sem("m_x_in"), sem("x1_added"), sem("x1_stored")
    stats_done, moments_done, std_done, rstd_done, shift_done, normed, x1_turned, x1t_copied = (
        sem(n) for n in ("m_stats_done", "m_moments_done", "m_std_done", "m_rstd_done", "m_shift_done",
                         "m_normed", "x1_turned", "x1t_copied"))
    resid_in = [sem(f"resid_in{i}") for i in range(NRES)]
    x2_out = [sem(f"x2_out{i}") for i in range(NRES)]

    x_v = x.rearrange("b (p t) d -> b p t d", t=T)
    x1_v = g.x1.rearrange("(b p t) d -> b p t d", p=P, t=T)
    x2_v = g.x2.rearrange("b (p t) d -> b p t d", t=T)
    routed_v = g.routed[0].rearrange("(m e) d -> e m d", e=E)
    G2 = T // 2

    def xc_of(j):
        return xc[J] if j == 0 else xc[j]

    def batches(eng, body):
        body(0, True, False)
        with eng.Fori(1, NB - 1) as b:
            body(b, False, False)
        body(NB - 1, False, True)

    block = ctx.enter_context(nc.Block())

    @block.sync
    def _(sp):
        def load_expert(nb, e):
            sp.wait_ge(expert_done, count(nb * SL + (e - 2) * NH + NH if e >= 2 else nb * SL))
            sp.dma_start(expert[e % 2][:], g.experts[e].rearrange("(k p) f -> p k f", p=P)
                         ).then_inc(expert_in[e % 2], 16)

        def load_next(nb):
            sp.wait_ge(x1_turned, nb * T)
            sp.wait_ge(x1_stored, nb * 16)
            sp.dma_start(x1[:], x_v[bass.ds(nb, 1)].rearrange("a p t d -> p (a t) d")).then_inc(x_in, 16)
            load_expert(nb, 0)
            load_expert(nb, 1)

        def side(nb):
            for i in range(NY):
                sp.wait_ge(back_in[i], nb * 16 * (T // NY))
                sp.sem_inc(g.passed_sp, 1)
            for s in range(SL):
                e, h = s // NH, s % NH
                sp.wait_ge(routed_scaled, nb * SL + s + 1)
                sp.dma_start(routed_v[e, 1 + h * P:1 + (h + 1) * P, :],
                             routed[s % NY][:]).then_inc(routed_out[s % NY], 16)
                if h == NH - 1 and e + 2 < E:
                    load_expert(nb, e + 2)
            sp.wait_ge(x1_added, (nb + 1) * T)
            sp.dma_start(x1_v[bass.ds(nb, 1)].rearrange("a p t d -> p (a t) d"), x1[:]).then_inc(x1_stored, 16)

        def load_resid(b, r):
            sp.dma_start(resid[r % NRES][:], x1_v[bass.ds(b, 1), :, 2 * r:2 * r + 2, :].rearrange("a p t d -> p (a t) d")
                         ).then_inc(resid_in[r % NRES], 16)

        def load_resids(b):
            for r in range(NRES):
                sp.wait_ge(x2_out[r], b * 16 * (G2 // NRES))
                load_resid(b, r)

        def store_results(b):
            for r in range(G2):
                sp.wait_ge(out_added, b * T + 2 * r + 2)
                sp.dma_start(x2_v[bass.ds(b, 1), :, 2 * r:2 * r + 2, :].rearrange("a p t d -> p (a t) d"), resid[r % NRES][:]
                             ).then_inc(x2_out[r % NRES], 16)
                if r >= 1 and r + NRES - 1 < G2:
                    sp.wait_ge(x2_out[(r - 1) % NRES], (b * (G2 // NRES) + (r - 1) // NRES + 1) * 16)
                    load_resid(b, r + NRES - 1)

        def body(b, first, last):
            if not last:
                load_next(b + 1)
            if not first:
                store_results(b - 1)
            if not last:
                side(b + 1)
            load_resids(b)

        load_next(0)
        side(0)
        sp.wait_ge(x1_stored, 16)
        batches(sp, body)
        store_results(NB - 1)
        for r in range(NRES):
            sp.wait_ge(x2_out[r], NB * 16 * (G2 // NRES))

    @block.gpsimd
    def _(pool):
        def side(nb):
            pool.wait_ge(now_set, (nb + 1) * 3)
            for s in range(SL):
                pool.wait_ge(pick_turned, nb * SL + (s - NX + 1 if s >= NX else 0))
                pool.sem_inc(g.passed_pool, 1)
                nc.gpsimd.indirect_dma_start(
                    out=picked[s % NX][:], out_offset=None, in_=g.normed,
                    in_offset=bass.IndirectOffsetOnAxis(ap=slot_now[:, s:s + 1].bitcast(U32), axis=0)
                ).then_inc(picked_in[s % NX], 16)
            for i in range(NY):
                pool.wait_ge(routed_out[i], (nb + 1) * 16 * (SL // NY))
            for t in range(T):
                pool.wait_ge(x1_added, nb * T + (t - NY + 1 if t >= NY else 0))
                pool.sem_inc(g.passed_pool, 1)
                nc.gpsimd.indirect_dma_start(
                    out=back[t % NY][:], out_offset=None, in_=g.routed[0],
                    in_offset=bass.IndirectOffsetOnAxis(ap=row_now[:, t:t + 1].bitcast(U32), axis=0)
                ).then_inc(back_in[t % NY], 16)

        side(0)
        side(1)
        with pool.Fori(2, NB) as b:
            side(b)

    @block.vector
    def _(dve):
        def set_now(nb):
            for i in range(NY):
                dve.wait_ge(back_in[i], nb * 16 * (T // NY))
            nc.vector.tensor_copy(slot_now[:], g.slot_token[:, bass.ds(nb, 1), :].rearrange("p a s -> p (a s)")).then_inc(now_set, 1)
            dve.wait_ge(routed_scaled, nb * SL)
            nc.vector.tensor_copy(gate_now[:], g.slot_gate[:, bass.ds(nb, 1), :].rearrange("p a s -> p (a s)")).then_inc(now_set, 1)
            nc.vector.tensor_copy(row_now[:], g.token_row[:, bass.ds(nb, 1), :].rearrange("p a s -> p (a s)")).then_inc(now_set, 1)

        def add_routed(nb, t):
            if t == 0:
                dve.wait_ge(x_in, (nb + 1) * 16)
            dve.wait_ge(back_in[t % NY], (nb * (T // NY) + t // NY + 1) * 16)
            nc.vector.tensor_tensor(x1[:, t, :], x1[:, t, :], back[t % NY][:], ALU.add).then_inc(x1_added, 1)
            dve.wait_ge(x1_added, nb * T + t + 1)
            nc.vector.bn_stats(stats[:, t, :], x1[:, t, :]).then_inc(stats_done, 1)

        def aggregate(nb):
            dve.wait_ge(stats_done, (nb + 1) * T)
            dve.sem_inc(g.passed_dve, 1)
            for t in range(T):
                nc.vector.bn_aggr(moments[:, t, :], stats[:, t, :]).then_inc(moments_done, 1)

        def scales(nb):
            dve.wait_ge(std_done, nb + 1)
            dve.wait_ge(moments_done, (nb + 1) * T)
            nc.vector.reciprocal(rstd[:], std[:]).then_inc(rstd_done, 1)
            dve.wait_ge(rstd_done, nb + 1)
            nc.vector.scalar_tensor_tensor(shift[:], moments[:, :, 0], -1.0, rstd[:], ALU.mult, ALU.mult
                                           ).then_inc(shift_done, 1)

        def normalise(nb, t):
            if t == 0:
                dve.wait_ge(shift_done, nb + 1)
                dve.wait_ge(x1_stored, (nb + 1) * 16)
            nc.vector.tensor_scalar(x1[:, t, :], x1[:, t, :], rstd[:, t:t + 1], shift[:, t:t + 1],
                                    ALU.mult, ALU.add).then_inc(normed, 1)

        def conv(b, j, taps):
            u = b * J + j
            v = delta[j % 2]
            for i in taps:
                k = KC - 1 - i
                if i == 0:
                    dve.wait_ge(ssm_copied, (u + 1) * C)
                    ins = nc.vector.tensor_scalar(v[:], conv_in[:, k:k + NT], g.conv_w[:, j, k:k + 1], None, ALU.mult)
                else:
                    dve.wait_ge(conv_step, u * (KC - 1) + i)
                    ins = nc.vector.scalar_tensor_tensor(v[:], conv_in[:, k:k + NT], g.conv_w[:, j, k:k + 1], v[:],
                                                         ALU.mult, ALU.add)
                ins.then_inc(conv_step if i < KC - 1 else conv_done, 1)

        def step_size(b, j):
            u = b * J + j
            dve.wait_ge(soft_done, u + 1)
            nc.vector.scalar_tensor_tensor(delta[j % 2][:], xc_of(j)[:], 0.0, delta[j % 2][:], ALU.max, ALU.add
                                           ).then_inc(delta_done, 1)

        def combine(b, j):
            u = b * J + j
            dve.wait_ge(state_used[NHB - 1], b * (J * N // NHB) + (j + 1) * (N // NHB))
            dve.wait_ge(res_gated, (u + 1) * C)
            for c in range(C):
                s = slice(c * CH, (c + 1) * CH)
                nc.vector.tensor_tensor(res[:, s], ps_sum[c][:], res[:, s], ALU.mult).then_inc(gated, 1)
            dve.wait_ge(gated, (u + 1) * C)
            if j == 0:
                dve.wait_ge(out_done, b * T)
            nc.vector.scalar_tensor_tensor(xc[j][:], res[:], g.skip[:, j:j + 1], xc_of(j)[:], ALU.add, ALU.mult
                                           ).then_inc(y_done, 1)

        def add_out(b, t):
            r = t // 2
            dve.wait_ge(out_done, b * T + t + 1)
            dve.wait_ge(resid_in[r % NRES], (b * (G2 // NRES) + r // NRES + 1) * 16)
            nc.vector.tensor_tensor(resid[r % NRES][:, t % 2, :], ps_misc[t % 2][:, 0:D], resid[r % NRES][:, t % 2, :],
                                    ALU.add).then_inc(out_added, 1)

        def finish(b, n):
            if n == 0:
                combine(b, J - 1)
            for t in range(G2 * n, G2 * n + G2):
                add_out(b, t)

        def body(b, first, last):
            if not last:
                set_now(b + 1)
            for j in range(J):
                for n in range(N):
                    q = j * N + n
                    if n == 0:
                        dve.wait_ge(drive_done, b * J + j + 1)
                    dve.wait_ge(decay_ready, b * J * N + q + 1)
                    dve.wait_ge(state_used[q % NHB], b * (J * N // NHB) + q // NHB)
                    nc.vector.tensor_tensor_scan(state[q % NHB][:], decay[q % NA][:], drive[j % 2][:], 0.0,
                                                 ALU.mult, ALU.add).then_inc(state_ready, 1)
                    if j and n == 0:
                        combine(b, j - 1)
                    if not first and q < 2:
                        finish(b - 1, n)
                    if j < J - 1:
                        if n == 6:
                            conv(b, j + 1, (0, 1))
                        if n == 7:
                            conv(b, j + 1, (2, 3))
                        if n == 13:
                            step_size(b, j + 1)
                    if last:
                        continue
                    if j == 1 and 6 <= n < 14:
                        add_routed(b + 1, 2 * (n - 6))
                        add_routed(b + 1, 2 * (n - 6) + 1)
                    if j == 1 and n == 14:
                        aggregate(b + 1)
                    if j == 2 and n == 11:
                        scales(b + 1)
                    if j == 2 and n >= 12:
                        for t in range(4 * (n - 12), 4 * (n - 11)):
                            normalise(b + 1, t)
                    if j == 3 and n == 11:
                        conv(b + 1, 0, (0, 1))
                    if j == 3 and n == 12:
                        conv(b + 1, 0, (2, 3))
                    if j == 3 and n == 15:
                        step_size(b + 1, 0)

        nc.vector.memset(conv_in[:, 0:KC - 1], 0.0).then_inc(setup, 1)
        nc.vector.memset(eps[:], LN_EPS).then_inc(setup, 1)
        set_now(0)
        for t in range(T):
            add_routed(0, t)
        aggregate(0)
        scales(0)
        for t in range(T):
            normalise(0, t)
        dve.wait_ge(setup, 2)
        conv(0, 0, range(KC))
        step_size(0, 0)
        batches(dve, body)
        for n in range(2):
            finish(NB - 1, n)

    @block.scalar
    def _(act):
        def copy_pick(nb, s):
            act.wait_ge(pick_turned, nb * SL + s + 1)
            act.wait_ge(expert_done, count(nb * SL + s - 1 if s >= 2 else nb * SL))
            nc.scalar.copy(picked_t[s % 2][:].rearrange("p k n -> p (k n)"), ps_misc[0][:, 0:KD * P]
                           ).then_inc(pick_copied, 1)

        def scale_routed(nb, s):
            act.wait_ge(expert_done, nb * SL + s + 1)
            if s == 0:
                act.wait_ge(now_set, (nb + 1) * 3)
            act.wait_ge(routed_out[s % NY], (nb * (SL // NY) + s // NY) * 16)
            nc.scalar.activation(routed[s % NY][:], ps_misc[1][:, 0:D], ACT.Identity, scale=gate_now[:, s:s + 1]
                                 ).then_inc(routed_scaled, 1)

        def deviation(nb):
            act.wait_ge(moments_done, (nb + 1) * T)
            nc.scalar.activation(std[:], moments[:, :, 1], ACT.Sqrt, bias=eps[:, 0:1]).then_inc(std_done, 1)

        def copy_turned(nb, t):
            act.wait_ge(x1_turned, nb * T + t + 1)
            nc.scalar.copy(x1t[:].rearrange("p k (n t) -> p k n t", t=T)[:, :, :, t],
                           ps_misc[t % 2][:, 0:KD * P].rearrange("p (k n) -> p k n", k=KD)).then_inc(x1t_copied, 1)

        def copy_ssm(b, j, c):
            u = b * J + j
            act.wait_ge(ssm_done, u * C + c + 1)
            if c == 0:
                act.wait_ge(conv_done, u)
            nc.scalar.copy(conv_in[:, KC - 1 + c * CH:KC - 1 + (c + 1) * CH], ps_proj[c % 2][:]).then_inc(ssm_copied, 1)

        def gate_res(b, j, c):
            u = b * J + j
            act.wait_ge(res_done, u * C + c + 1)
            if c == 0:
                act.wait_ge(y_done, u)
            nc.scalar.activation(res[:, c * CH:(c + 1) * CH], ps_proj[c % 2][:], ACT.Silu).then_inc(res_gated, 1)

        def activate(b, j):
            u = b * J + j
            act.wait_ge(conv_done, u + 1)
            if j:
                act.wait_ge(out_done, b * T)
            nc.scalar.activation(xc_of(j)[:], delta[j % 2][:], ACT.Silu, bias=g.conv_b[:, j:j + 1]).then_inc(xc_done, 1)

        def magnitude(b, j):
            u = b * J + j
            act.wait_ge(xc_done, u + 1)
            nc.scalar.activation(delta[j % 2][:], xc_of(j)[:], ACT.Abs).then_inc(soft_step, 1)
            nc.scalar.activation(drive[j % 2][:], xc_of(j)[:], ACT.Square).then_inc(drive_done, 1)

        def soft_exp(b, j):
            u = b * J + j
            act.wait_ge(soft_step, 2 * u + 1)
            nc.scalar.activation(delta[j % 2][:], delta[j % 2][:], ACT.Exp, scale=-1.0).then_inc(soft_step, 1)

        def soft_log(b, j):
            u = b * J + j
            act.wait_ge(soft_step, 2 * u + 2)
            nc.scalar.activation(delta[j % 2][:], delta[j % 2][:], ACT.Ln, bias=1.0).then_inc(soft_done, 1)

        def both_tables():
            nc.scalar.preload_act_table_set("natural_log_exp_and_others")

        def body(b, first, last):
            for j in range(J):
                for n in range(N):
                    q = j * N + n
                    if n == 0:
                        act.wait_ge(delta_done, b * J + j + 1)
                    act.wait_ge(state_ready, count(b * J * N + q - NA + 1))
                    nc.scalar.activation(decay[q % NA][:], delta[j % 2][:], ACT.Exp, scale=g.neg_a[:, j, n:n + 1]
                                         ).then_inc(decay_ready, 1)
                    if not last and FFN <= q < FFN + SL:
                        copy_pick(b + 1, q - FFN)
                    if not last and FFN < q <= FFN + SL:
                        scale_routed(b + 1, q - FFN - 1)
                    if j < J - 1:
                        if 2 <= n < 2 + C:
                            copy_ssm(b, j + 1, n - 2)
                        if n == 9:
                            if j == 2 and not last:
                                deviation(b + 1)
                            for c in range(C):
                                gate_res(b, j, c)
                            activate(b, j + 1)
                            both_tables()
                        if n == 10:
                            magnitude(b, j + 1)
                        if n == 11:
                            soft_exp(b, j + 1)
                        if n == 12:
                            soft_log(b, j + 1)
                    elif n == 2:
                        for c in range(C):
                            gate_res(b, j, c)
                        both_tables()
                    if j == J - 1 and not last:
                        if 4 <= n < 8:
                            for t in range(4 * (n - 4), 4 * (n - 3)):
                                copy_turned(b + 1, t)
                        if 8 <= n < 8 + C:
                            copy_ssm(b + 1, 0, n - 8)
                        if n == 13:
                            activate(b + 1, 0)
                            both_tables()
                        if n == 14:
                            magnitude(b + 1, 0)
                        if n == 15:
                            soft_exp(b + 1, 0)
                            soft_log(b + 1, 0)

        for s in range(SL):
            copy_pick(0, s)
            scale_routed(0, s)
        act.wait_ge(setup, 2)
        deviation(0)
        for t in range(T):
            copy_turned(0, t)
        for c in range(C):
            copy_ssm(0, 0, c)
        activate(0, 0)
        both_tables()
        magnitude(0, 0)
        soft_exp(0, 0)
        soft_log(0, 0)
        batches(act, body)

    @block.tensor
    def _(pe):
        def turn_pick(nb, s):
            full = [len([v for v in range(SL) if v % NX == i]) for i in range(NX)]
            pe.wait_ge(picked_in[s % NX], (nb * full[s % NX] + s // NX + 1) * 16)
            if s:
                pe.wait_ge(pick_copied, nb * SL + s)
            else:
                pe.wait_ge(x1t_copied, nb * T)
                pe.wait_ge(out_added, count((nb - 1) * T))
            for k in range(KD):
                mm = nc.tensor.transpose(ps_misc[0][:, k * P:(k + 1) * P], picked[s % NX][:, k * P:(k + 1) * P], g.ident[:])
            mm.then_inc(pick_turned, 1)

        def apply_expert(nb, s):
            e = s // NH
            pe.wait_ge(pick_copied, nb * SL + s + 1)
            pe.wait_ge(expert_in[e % 2], (nb * (E // 2) + e // 2 + 1) * 16)
            if s:
                pe.wait_ge(routed_scaled, nb * SL + s)
            for k in range(KD):
                mm = nc.tensor.matmul(ps_misc[1][:, 0:D], picked_t[s % 2][:, k, :], expert[e % 2][:, k, :],
                                      start=(k == 0), stop=(k == KD - 1))
            mm.then_inc(expert_done, 1)

        def turn_x1(nb, t):
            pe.wait_ge(normed, nb * T + t + 1)
            if t >= 2:
                pe.wait_ge(x1t_copied, count(nb * T + t - 1))
            elif t == 0:
                pe.wait_ge(pick_copied, (nb + 1) * SL)
            else:
                pe.wait_ge(routed_scaled, (nb + 1) * SL)
            for k in range(KD):
                mm = nc.tensor.transpose(ps_misc[t % 2][:, k * P:(k + 1) * P], x1[:, t, k * P:(k + 1) * P], g.ident[:])
            mm.then_inc(x1_turned, 1)

        def project(bank, col, c):
            for k in range(KD):
                mm = nc.tensor.matmul(ps_proj[bank][:], g.w_in[:, k, col:col + P], x1t[:, k, c * CH:(c + 1) * CH],
                                      start=(k == 0), stop=(k == KD - 1))
            return mm

        def project_ssm(b, j, c):
            u = b * J + j
            if c == 0:
                pe.wait_ge(x1t_copied, (b + 1) * T)
            if c >= 2:
                pe.wait_ge(ssm_copied, count(u * C + c - 1))
            else:
                if j == 1:
                    pe.wait_ge(ssm_copied, u * C)
                elif j > 1:
                    pe.wait_ge(res_gated, count((u - 1) * C))
                else:
                    pe.wait_ge(res_gated, u * C)
            project(c % 2, j * P, c).then_inc(ssm_done, 1)

        def project_res(b, j, c):
            u = b * J + j
            if c >= 2:
                pe.wait_ge(res_gated, count(u * C + c - 1))
            elif j < J - 1:
                pe.wait_ge(ssm_copied, (u + 2) * C)
            else:
                pe.wait_ge(res_gated, u * C)
            project(c % 2, INNER + j * P, c).then_inc(res_done, 1)

        def project_out(b, last):
            for t in range(T):
                if t >= 2:
                    pe.wait_ge(out_added, b * T + t - 1)
                elif t == 0:
                    pe.wait_ge(y_done, (b + 1) * J)
                    pe.wait_ge(x1t_copied, NB * T if last else (b + 2) * T)
                for j in range(J):
                    mm = nc.tensor.matmul(ps_misc[t % 2][:, 0:D], xc[j][:].rearrange("p (n t) -> p n t", t=T)[:, :, t],
                                          g.w_out[:, j, :], start=(j == 0), stop=(j == J - 1))
                mm.then_inc(out_done, 1)

        def beside(b, v, last):
            j, n = v // N, v % N
            if not last and FFN <= v < FFN + SL:
                turn_pick(b + 1, v - FFN)
            if not last and FFN < v <= FFN + SL:
                apply_expert(b + 1, v - FFN - 1)
            if j < J - 1:
                if 2 <= n < 2 + C:
                    project_ssm(b, j + 1, n - 2)
                if n == 8:
                    project_res(b, j, 0)
                    project_res(b, j, 1)
                if n == 9:
                    project_res(b, j, 2)
                    project_res(b, j, 3)
            elif n == 3:
                for c in range(C):
                    project_res(b, j, c)
            if j == J - 1 and not last:
                if 4 <= n < 8:
                    for t in range(4 * (n - 4), 4 * (n - 3)):
                        turn_x1(b + 1, t)
                if 8 <= n < 8 + C:
                    project_ssm(b + 1, 0, n - 8)

        def body(b, first, last):
            if not first:
                project_out(b - 1, False)
            for v in range(LEAD):
                beside(b, v, last)
            for j in range(J):
                for n in range(N):
                    q = j * N + n
                    for c in range(C):
                        if c == 0:
                            pe.wait_ge(state_ready, b * J * N + q + 1)
                        if n == 0:
                            pe.wait_ge(gated, count((b * J + j - 1) * C + c + 1))
                        mm = nc.tensor.matmul(ps_sum[c][:], g.ident[:], state[q % NHB][:, c * CH:(c + 1) * CH],
                                              start=(n == 0), stop=(n == N - 1))
                    mm.then_inc(state_used[q % NHB], 1)
                    if q + LEAD < J * N:
                        beside(b, q + LEAD, last)

        for s in range(SL):
            turn_pick(0, s)
            apply_expert(0, s)
        for t in range(T):
            turn_x1(0, t)
        for c in range(C):
            project_ssm(0, 0, c)
        batches(pe, body)
        project_out(NB - 1, True)


def ffn(nc, g, x, out, ctx):
    def sb(name, shape, dt=F32):
        return ctx.enter_context(nc.sbuf_tensor(name, shape, dt))

    def sem(name):
        return ctx.enter_context(nc.semaphore(name))

    def ps(name):
        return ctx.enter_context(nc.psum_tensor(name, [P, CH], F32))

    NX = NY = NK = 4
    expert = sb("f_expert", [P, E, KD, D])
    slot_now = [sb(f"f_slot_now{i}", [P, SL], I32) for i in range(2)]
    row_now = sb("f_row_now", [P, T], I32)
    picked = [sb(f"f_picked{i}", [P, D]) for i in range(NX)]
    picked_t = [sb(f"f_picked_t{i}", [P, KD, P]) for i in range(2)]
    routed = [sb(f"f_routed{i}", [P, D]) for i in range(NY)]
    back = [sb(f"f_back{i}", [P, D]) for i in range(NK)]
    total = sb("f_total", [P, T, D])
    ps_turn = [ps(f"f_ps_turn{i}") for i in range(2)]
    ps_out = [ps(f"f_ps_out{i}") for i in range(2)]
    expert_in, now_set, rows_set = sem("f_expert_in"), sem("f_now_set"), sem("f_rows_set")
    picked_in = [sem(f"f_picked_in{i}") for i in range(NX)]
    routed_out = [sem(f"f_routed_out{i}") for i in range(NY)]
    back_in = [sem(f"f_back_in{i}") for i in range(NK)]
    turned, copied, product, scaled, added, x_in, out_stored = (
        sem(n) for n in ("f_turned", "f_copied", "f_product", "f_scaled", "f_added", "f_x_in", "f_out_stored"))
    x_v = x.rearrange("b (p t) d -> b p t d", t=T)
    out_v = out.rearrange("b (p t) d -> b p t d", t=T)
    routed_v = [table.rearrange("(m e) d -> e m d", e=E) for table in g.routed]
    block = ctx.enter_context(nc.Block())

    def pipeline(eng, slots, tokens):
        def two(i):
            slots(2 * i + 1, 1)
            tokens(2 * i, 0)
            slots(2 * i + 2, 0)
            tokens(2 * i + 1, 1)

        slots(0, 0)
        two(0)
        with eng.Fori(1, NB // 2 - 1) as i:
            two(i)
        slots(NB - 1, 1)
        tokens(NB - 2, 0)
        tokens(NB - 1, 1)

    def read_back(b):
        return count((b - 1) * 16 * (T // NK))

    @block.sync
    def _(sp):
        def slots(b, table):
            for s in range(SL):
                e, h = s // NH, s % NH
                sp.wait_ge(scaled, b * SL + s + 1)
                sp.sem_inc(g.passed_sp, 1)
                if s == 0:
                    for i in range(NK):
                        sp.wait_ge(back_in[i], read_back(b))
                sp.dma_start(routed_v[table][e, 1 + h * P:1 + (h + 1) * P, :],
                             routed[s % NY][:]).then_inc(routed_out[s % NY], 16)

        def tokens(b, table):
            sp.wait_ge(added, (b + 1) * T)
            sp.dma_start(out_v[bass.ds(b, 1)].rearrange("a p t d -> p (a t) d"), total[:]).then_inc(out_stored, 16)
            if isinstance(b, int) and b == NB - 1:
                return
            sp.wait_ge(out_stored, (b + 1) * 16)
            sp.dma_start(total[:], x_v[bass.ds(b + 1, 1)].rearrange("a p t d -> p (a t) d")).then_inc(x_in, 16)

        for e in range(E):
            sp.dma_start(expert[:, e, :, :], g.experts[e].rearrange("(k p) f -> p k f", p=P)).then_inc(expert_in, 16)
        sp.dma_start(total[:], x_v[0]).then_inc(x_in, 16)
        pipeline(sp, slots, tokens)
        sp.wait_ge(out_stored, NB * 16)

    @block.gpsimd
    def _(pool):
        def slots(b, table):
            pool.wait_ge(now_set, b + 1)
            for s in range(SL):
                pool.wait_ge(turned, b * SL + (s - NX + 1 if s >= NX else 0))
                pool.sem_inc(g.passed_pool, 1)
                nc.gpsimd.indirect_dma_start(
                    out=picked[s % NX][:], out_offset=None, in_=g.normed,
                    in_offset=bass.IndirectOffsetOnAxis(ap=slot_now[0][:, s:s + 1].bitcast(U32), axis=0)
                ).then_inc(picked_in[s % NX], 16)

        def tokens(b, table):
            pool.wait_ge(rows_set, b + 1)
            for i in range(NY):
                pool.wait_ge(routed_out[i], (b + 1) * 16 * (SL // NY))
            for t in range(T):
                pool.wait_ge(added, b * T + (t - NK + 1 if t >= NK else 0))
                pool.sem_inc(g.passed_pool, 1)
                nc.gpsimd.indirect_dma_start(
                    out=back[t % NK][:], out_offset=None, in_=g.routed[table],
                    in_offset=bass.IndirectOffsetOnAxis(ap=row_now[:, t:t + 1].bitcast(U32), axis=0)
                ).then_inc(back_in[t % NK], 16)

        pipeline(pool, slots, tokens)

    @block.vector
    def _(dve):
        def slots(b, table):
            for i in range(NX):
                dve.wait_ge(picked_in[i], b * 16 * (SL // NX))
            nc.vector.tensor_copy(slot_now[0][:], g.slot_token[:, bass.ds(b, 1), :].rearrange("p a s -> p (a s)")).then_inc(now_set, 1)
            for s in range(SL):
                dve.wait_ge(turned, b * SL + s + 1)
                dve.wait_ge(product, count(b * SL + s - 1 if s >= 2 else b * SL))
                nc.vector.tensor_copy(picked_t[s % 2][:].rearrange("p k n -> p (k n)"), ps_turn[s % 2][:, 0:KD * P]
                                      ).then_inc(copied, 1)

        def tokens(b, table):
            for i in range(NK):
                dve.wait_ge(back_in[i], b * 16 * (T // NK))
            nc.vector.tensor_copy(row_now[:], g.token_row[:, bass.ds(b, 1), :].rearrange("p a s -> p (a s)")).then_inc(rows_set, 1)
            dve.wait_ge(x_in, (b + 1) * 16)
            for t in range(T):
                dve.wait_ge(back_in[t % NK], (b * (T // NK) + t // NK + 1) * 16)
                nc.vector.tensor_tensor(total[:, t, :], total[:, t, :], back[t % NK][:], ALU.add).then_inc(added, 1)

        pipeline(dve, slots, tokens)

    @block.scalar
    def _(act):
        def slots(b):
            for s in range(SL):
                act.wait_ge(product, b * SL + s + 1)
                act.wait_ge(routed_out[s % NY], (b * (SL // NY) + s // NY) * 16)
                nc.scalar.activation(routed[s % NY][:], ps_out[s % 2][:, 0:D], ACT.Identity,
                                     scale=g.slot_gate[:, bass.ds(b, 1), s:s + 1].rearrange("p a s -> p (a s)")).then_inc(scaled, 1)

        slots(0)
        with act.Fori(1, NB) as b:
            slots(b)

    @block.tensor
    def _(pe):
        def turn(b, s):
            pe.wait_ge(picked_in[s % NX], (b * (SL // NX) + s // NX + 1) * 16)
            pe.wait_ge(copied, count(b * SL + s - 1 if s >= 2 else b * SL))
            for k in range(KD):
                mm = nc.tensor.transpose(ps_turn[s % 2][:, k * P:(k + 1) * P], picked[s % NX][:, k * P:(k + 1) * P], g.ident[:])
            mm.then_inc(turned, 1)

        def apply_expert(b, s):
            pe.wait_ge(copied, b * SL + s + 1)
            pe.wait_ge(scaled, count(b * SL + s - 1 if s >= 2 else b * SL))
            for k in range(KD):
                mm = nc.tensor.matmul(ps_out[s % 2][:, 0:D], picked_t[s % 2][:, k, :], expert[:, s // NH, k, :],
                                      start=(k == 0), stop=(k == KD - 1))
            mm.then_inc(product, 1)

        def slots(b):
            turn(b, 0)
            for s in range(SL):
                if s + 1 < SL:
                    turn(b, s + 1)
                apply_expert(b, s)

        pe.wait_ge(expert_in, E * 16)
        slots(0)
        with pe.Fori(1, NB) as b:
            slots(b)


def program(nc, w, g):
    with ExitStack() as ctx:
        constants(nc, g, w, ctx)
        route(nc, g, w.x, "in")
        with ExitStack() as c1:
            mixer(nc, g, w.x, c1)
        route(nc, g, g.x2, "mid")
        with ExitStack() as c1:
            ffn(nc, g, g.x2, w.out, c1)


def kernel(L0_attn_x, L0_attn_W_in, L0_attn_conv_w, L0_attn_conv_b, L0_attn_A_log, L0_attn_D, L0_attn_W_out,
           L0_ffn_gate_w, L0_ffn_experts):
    import concourse.bacc as bacc
    from concourse.bass_utils import run_bass_kernel_spmd

    nc = bacc.Bacc("TRN2", target_bir_lowering=False, num_devices=1)
    arrays = {}

    def given(name, a):
        a = np.ascontiguousarray(a)
        arrays[name] = a
        return nc.dram_tensor(name, a.shape, mybir.dt.from_np(a.dtype), kind="ExternalInput").ap()

    w, g = Bag(), Bag()
    w.x = given("in_x", L0_attn_x)
    w.A_log = given("in_a_log", L0_attn_A_log)
    w.w_in_t = given("in_w_in_t", L0_attn_W_in.T)
    w.w_out_t = given("in_w_out_t", L0_attn_W_out.T)
    w.conv_w = given("in_conv_w", L0_attn_conv_w.reshape(INNER, KC))
    w.conv_b_t = given("in_conv_b_t", L0_attn_conv_b.reshape(J, P).T)
    w.skip_t = given("in_skip_t", L0_attn_D.reshape(J, P).T)
    w.gate_w = given("in_gate_w", L0_ffn_gate_w)
    g.experts = given("in_experts", L0_ffn_experts)
    w.out = nc.dram_tensor("out", (NB, NT, D), F32, kind="ExternalOutput").ap()
    g.normed = nc.dram_tensor("normed_rows", (NB * NT, D), F32).ap()
    g.routed = [nc.dram_tensor(f"routed_rows{i}", (YR, D), F32).ap() for i in range(2)]
    g.x1 = nc.dram_tensor("x1_rows", (NB * NT, D), F32).ap()
    g.x2 = nc.dram_tensor("x2_rows", (NB, NT, D), F32).ap()
    program(nc, w, g)
    r = run_bass_kernel_spmd(nc, [arrays], core_ids=[0])
    return r.results[0]["out"]
```

```python
from contextlib import ExitStack

import numpy as np

import concourse.bass as bass
from concourse import mybir

ALU = mybir.AluOpType
ACT = mybir.ActivationFunctionType
F32 = mybir.dt.float32
BF16 = mybir.dt.bfloat16
I32 = mybir.dt.int32
U32 = mybir.dt.uint32
AX = mybir.AxisListType

P = 128
NB = 8
NT = 2048
D = 256
KD = D // P
T = NT // P
E = 8
M = NT // E
NH = M // P
SL = E * NH
R = NB * E
YR = E * (M + 1)
ITERS = 8
INNER = 512
J = INNER // P
N = 16
KC = 4
CH = 512
C = NT // CH
LN_EPS = 1e-5
CLIP = 1e-6


class Bag:
    pass


def count(value):
    return max(value, 0) if isinstance(value, int) else value


def constants(nc, g, w, ctx):

    def sb(name, shape, dt=F32):
        return ctx.enter_context(nc.sbuf_tensor(name, shape, dt))

    g.ident = sb("ident", [P, P])
    g.ones = sb("ones", [P, P])
    g.iota_col = sb("iota_col", [P, P])
    g.rank_of = sb("rank_of", [P, NH])
    g.expert_of = sb("expert_of", [P, R])
    g.token_base = sb("token_base", [P, NB])
    g.gate_w = sb("gate_w", [P, KD, E])
    g.w_in = sb("w_in", [P, KD, 2 * INNER])
    g.w_out = sb("w_out", [P, J, D])
    g.conv_w = sb("conv_w", [P, J, KC])
    g.conv_b = sb("conv_b", [P, J])
    g.skip = sb("skip", [P, J])
    g.neg_a = sb("neg_a", [P, J, N])
    g.slot_token = sb("slot_token", [P, NB, SL], I32)
    g.slot_gate = sb("slot_gate", [P, NB, SL])
    g.token_row = sb("token_row", [P, NB, T], I32)

    g.passed_dve, g.passed_pool, g.passed_sp = (
        ctx.enter_context(nc.semaphore(n)) for n in ("passed_dve", "passed_pool", "passed_sp"))

    with ExitStack() as c2:
        zrow = c2.enter_context(nc.sbuf_tensor("zero_row", [E, D], F32))
        zeroed = c2.enter_context(nc.semaphore("zeroed"))
        loaded = ctx.enter_context(nc.semaphore("weights_loaded"))
        a_loaded = c2.enter_context(nc.semaphore("a_log_loaded"))
        a_exp = c2.enter_context(nc.semaphore("a_exp_done"))
        zero_stored = c2.enter_context(nc.semaphore("zero_rows_stored"))
        block = c2.enter_context(nc.Block())

        @block.gpsimd
        def _(pool):
            nc.gpsimd.memset(zrow[:], 0.0).then_inc(zeroed, 1)
            nc.gpsimd.memset(g.ident[:], 0.0).then_inc(zeroed, 1)
            nc.gpsimd.memset(g.ones[:], 1.0)
            pool.wait_ge(zeroed, 2)
            nc.gpsimd.affine_select(out=g.ident[:], in_=g.ident[:], compare_op=ALU.not_equal, fill=1.0,
                                    base=0, pattern=[[-1, P]], channel_multiplier=1)
            for out, pattern, base, mult in (
                (g.iota_col[:], [[1, P]], 0, 0),
                (g.rank_of[:], [[P, NH]], 1, 1),
                (g.expert_of[:], [[0, NB], [1, E]], 0, 0),
                (g.token_base[:], [[NT, NB]], 0, 0),
            ):
                nc.gpsimd.iota(out, pattern, base=base, channel_multiplier=mult,
                               allow_small_or_imprecise_dtypes=True)

        @block.sync
        def _(sp):
            sp.dma_start(g.neg_a[:], w.A_log.rearrange("(j p) n -> p j n", p=P)).then_inc(a_loaded, 16)
            sp.dma_start(g.gate_w[:], w.gate_w.rearrange("(k p) e -> p k e", p=P)).then_inc(loaded, 16)
            sp.dma_start(g.w_in[:], w.w_in_t.rearrange("(k p) c -> p k c", p=P)).then_inc(loaded, 16)
            sp.dma_start(g.w_out[:], w.w_out_t.rearrange("(j p) d -> p j d", p=P)).then_inc(loaded, 16)
            sp.dma_start(g.conv_w[:], w.conv_w.rearrange("(j p) k -> p j k", p=P)).then_inc(loaded, 16)
            sp.dma_start(g.conv_b[:], w.conv_b_t).then_inc(loaded, 16)
            sp.dma_start(g.skip[:], w.skip_t).then_inc(loaded, 16)
            sp.wait_ge(zeroed, 1)
            for table in g.routed:
                sp.dma_start(table[0:E, :], zrow[:]).then_inc(zero_stored, 16)
            sp.wait_ge(loaded, 6 * 16)
            sp.wait_ge(zero_stored, 2 * 16)

        @block.scalar
        def _(act):
            act.wait_ge(a_loaded, 16)
            flat = g.neg_a[:].rearrange("p j n -> p (j n)")
            nc.scalar.activation(flat, flat, ACT.Exp).then_inc(a_exp, 1)
            act.wait_ge(a_exp, 1)
            nc.scalar.mul(flat, flat, -1.0)


def route(nc, g, x, tag):
    x_in = x.rearrange("b (p t) d -> b p t d", t=T)
    xn_out = g.normed.rearrange("(b p t) d -> b p t d", p=P, t=T)
    with ExitStack() as ctx:
        def sb(name, shape, dt=F32):
            return ctx.enter_context(nc.sbuf_tensor(f"{name}_{tag}", shape, dt))

        def sem(name):
            return nc.alloc_semaphore(f"{name}_{tag}")

        held = nc.snapshot_sems()
        probs = sb("probs", [P, T, NB, E])
        with ExitStack() as c1:
            logits_stage(nc, g, x_in, xn_out, probs, tag, c1)
        with ExitStack() as c1:
            rows = sinkhorn_stage(nc, g, probs, tag, ctx, c1)
        with ExitStack() as c1:
            top_stage(nc, g, rows, tag, c1)
        nc.clear_and_free_semaphores(nc.allocated_since(held))
        nc.all_engine_barrier()


def logits_stage(nc, g, x_in, xn_out, probs, tag, ctx):
    def sb(name, shape, dt=F32):
        return ctx.enter_context(nc.sbuf_tensor(f"{name}_{tag}", shape, dt))

    def sem(name):
        return nc.alloc_semaphore(f"{name}_{tag}")

    U = 4
    NB4 = 4
    HT = T // 2
    rows_ = [sb(f"rows{u}", [P, T, D]) for u in range(U)]
    stats = [sb(f"stats{u}", [P, T, 6]) for u in range(2)]
    moments = [sb(f"moments{u}", [P, T, 2]) for u in range(2)]
    std = [sb(f"std{u}", [P, T]) for u in range(2)]
    rstd = [sb(f"rstd{u}", [P, T]) for u in range(2)]
    shift = [sb(f"shift{u}", [P, T]) for u in range(2)]
    eps = sb("eps", [P, 1])
    turned = [sb(f"turned{i}", [P, KD, P]) for i in range(NB4)]
    ps_turn = [ctx.enter_context(nc.psum_tensor(f"ps_turn{i}_{tag}", [P, CH], F32)) for i in range(NB4)]
    ps_logit = [ctx.enter_context(nc.psum_tensor(f"ps_logit{u}_{tag}", [P, CH], F32)) for u in range(2)]

    def turns(eng, turn):
        turn(0)
        with eng.Fori(1, NB // U) as it:
            turn(it)

    row_in = [sem(f"row_in{u}") for u in range(U)]
    row_out = [sem(f"row_out{u}") for u in range(U)]
    eps_set, stats_done, moments_done, std_done, rstd_done, shift_done = (
        sem(n) for n in ("eps_set", "stats_done", "moments_done", "std_done", "rstd_done", "shift_done"))
    normed, turns_done, logits_done, probs_done = (
        sem(n) for n in ("normed", "turns_done", "logits_done", "probs_done"))
    turned_copied = [sem(n) for n in ("even_copied", "odd_copied")]
    block = ctx.enter_context(nc.Block())

    @block.sync
    def _(sp):
        def load(b, u):
            sp.dma_start(rows_[u][:], x_in[bass.ds(b, 1)].rearrange("a p t d -> p (a t) d")).then_inc(row_in[u], 16)

        def store(b, u):
            sp.wait_ge(normed, (b + 1) * T)
            sp.dma_start(xn_out[bass.ds(b, 1)].rearrange("a p t d -> p (a t) d"), rows_[u][:]
                         ).then_inc(row_out[u], 16)

        def load_over(b, u, turn):
            sp.wait_ge(row_out[u], turn * 16)
            sp.sem_inc(g.passed_sp, 1)
            sp.wait_ge(logits_done, (b - U + 1) * T)
            load(b, u)

        for u in range(U):
            load(u, u)
        with sp.Fori(1, NB // U) as it:
            for u in range(U):
                store((it - 1) * U + u, u)
                if u:
                    load_over(it * U + u - 1, u - 1, it)
            load_over(it * U + U - 1, U - 1, it)
        for u in range(U):
            store(NB - U + u, u)
        for u in range(U):
            sp.wait_ge(row_out[u], 16 * NB // U)

    @block.vector
    def _(dve):
        def copy(b, t):
            dve.wait_ge(turns_done, b * T + t + 1)
            dve.wait_ge(logits_done, count(b * T + t - NB4 + 1))
            nc.vector.tensor_copy(turned[t % NB4][:].rearrange("p k n -> p (k n)"),
                                  ps_turn[t % NB4][:, 0:KD * P]).then_inc(turned_copied[0], 1)

        def clip(b, i):
            dve.wait_ge(logits_done, (b + 1) * T)
            nc.vector.tensor_scalar(
                probs[:, :, bass.ds(b, 1), :].rearrange("p t a e -> p t (a e)"),
                ps_logit[i][:, 0:T * E].rearrange("p (t e) -> p t e", e=E),
                CLIP, None, ALU.max).then_inc(probs_done, 1)

        def turn(it):
            for u in range(U):
                b, i = it * U + u, u % 2
                first = isinstance(b, int) and b == 0
                for t in range(T):
                    if t == 0:
                        dve.wait_ge(row_in[u], (it + 1) * 16)
                    nc.vector.bn_stats(stats[i][:, t, :], rows_[u][:, t, :]).then_inc(stats_done, 1)
                    if not first and t % 2 == 0:
                        copy(b - 1, t)
                dve.wait_ge(stats_done, (b + 1) * T)
                dve.sem_inc(g.passed_dve, 1)
                for t in range(T):
                    nc.vector.bn_aggr(moments[i][:, t, :], stats[i][:, t, :]).then_inc(moments_done, 1)
                dve.wait_ge(std_done, b + 1)
                nc.vector.reciprocal(rstd[i][:], std[i][:]).then_inc(rstd_done, 1)
                dve.wait_ge(rstd_done, b + 1)
                nc.vector.scalar_tensor_tensor(shift[i][:], moments[i][:, :, 0], -1.0, rstd[i][:],
                                               ALU.mult, ALU.mult).then_inc(shift_done, 1)
                if not first:
                    clip(b - 1, 1 - i)

        nc.vector.memset(eps[:], LN_EPS).then_inc(eps_set, 1)
        turns(dve, turn)
        for t in range(0, T, 2):
            copy(NB - 1, t)
        clip(NB - 1, (NB - 1) % 2)

    @block.scalar
    def _(act):
        def copy(b, t):
            act.wait_ge(turns_done, b * T + t + 1)
            act.wait_ge(logits_done, count(b * T + t - NB4 + 1))
            nc.scalar.copy(turned[t % NB4][:].rearrange("p k n -> p (k n)"),
                           ps_turn[t % NB4][:, 0:KD * P]).then_inc(turned_copied[1], 1)

        def turn(it):
            for u in range(U):
                b, i = it * U + u, u % 2
                act.wait_ge(moments_done, (b + 1) * T)
                nc.scalar.activation(std[i][:], moments[i][:, :, 1], ACT.Sqrt, bias=eps[:, 0:1]
                                     ).then_inc(std_done, 1)
                act.wait_ge(shift_done, b + 1)
                for t in range(T):
                    nc.scalar.activation(rows_[u][:, t, :], rows_[u][:, t, :], ACT.Identity,
                                         bias=shift[i][:, t:t + 1], scale=rstd[i][:, t:t + 1]
                                         ).then_inc(normed, 1)
                    if t % 2 and t > 2:
                        copy(b, t - 2)
                copy(b, T - 1)

        act.wait_ge(eps_set, 1)
        turns(act, turn)

    @block.tensor
    def _(pe):
        def transpose(b, u, t):
            pe.wait_ge(normed, b * T + t + 1)
            pe.wait_ge(turned_copied[t % 2], count(b * HT + t // 2 - NB4 // 2 + 1))
            for k in range(KD):
                mm = nc.tensor.transpose(ps_turn[t % NB4][:, k * P:(k + 1) * P],
                                         rows_[u][:, t, k * P:(k + 1) * P], g.ident[:])
            mm.then_inc(turns_done, 1)

        def logit(b, u, t):
            pe.wait_ge(turned_copied[t % 2], b * HT + t // 2 + 1)
            if t == 0:
                pe.wait_ge(probs_done, count(b - 1))
            for k in range(KD):
                mm = nc.tensor.matmul(ps_logit[u % 2][:, t * E:(t + 1) * E], turned[t % NB4][:, k, :],
                                      g.gate_w[:, k, :], start=(k == 0), stop=(k == KD - 1))
            mm.then_inc(logits_done, 1)

        def turn(it):
            for u in range(U):
                b = it * U + u
                for t in range(T + 3):
                    if t < T:
                        transpose(b, u, t)
                    if t >= 3:
                        logit(b, u, t - 3)

        turns(pe, turn)


def sinkhorn_stage(nc, g, probs, tag, outer, ctx):
    def sb(name, shape, dt=F32, c=ctx):
        return c.enter_context(nc.sbuf_tensor(f"{name}_{tag}", shape, dt))

    def sem(name):
        return nc.alloc_semaphore(f"{name}_{tag}")

    rows = sb("gate_rows", [R, NT], c=outer)
    r = sb("token_scale", [P, T * NB])
    c_ = sb("expert_scale", [P, R])
    token_sum = sb("token_sum", [P, T * NB])
    scaled = sb("scaled", [P, T * NB, E])
    weighted = sb("weighted", [P, T, R])
    ps_sum = ctx.enter_context(nc.psum_tensor(f"ps_sum_{tag}", [P, CH], F32))
    ps_rows = [ctx.enter_context(nc.psum_tensor(f"ps_rows{i}_{tag}", [P, CH], F32)) for i in range(4)]
    weighted_done, sums_done, c_done, scaled_done, token_sums_done, r_done, gates_done, turned, copied = (
        sem(n) for n in ("weighted", "expert_sums", "expert_scale", "scaled", "token_sums", "token_scale",
                         "gates", "gates_turned", "gates_copied"))
    block = ctx.enter_context(nc.Block())
    flat = probs[:].rearrange("p t b e -> p (t b) e")

    @block.vector
    def _(dve):
        nc.vector.memset(r[:], 1.0).then_inc(r_done, 1)
        for i in range(ITERS):
            dve.wait_ge(r_done, i + 1)
            nc.vector.tensor_tensor(weighted[:].rearrange("p t (b e) -> p (t b) e", e=E), flat,
                                    r[:].unsqueeze(2).to_broadcast([P, T * NB, E]), ALU.mult
                                    ).then_inc(weighted_done, 1)
            dve.wait_ge(sums_done, i + 1)
            nc.vector.reciprocal(c_[:], ps_sum[:, 0:R]).then_inc(c_done, 1)
            dve.wait_ge(c_done, i + 1)
            nc.vector.tensor_tensor(scaled[:].rearrange("p (t b) e -> p t (b e)", b=NB),
                                    probs[:].rearrange("p t b e -> p t (b e)"),
                                    c_[:].unsqueeze(1).to_broadcast([P, T, R]), ALU.mult
                                    ).then_inc(scaled_done, 1)
            dve.wait_ge(scaled_done, i + 1)
            nc.vector.tensor_reduce(token_sum[:], scaled[:], AX.X, ALU.add).then_inc(token_sums_done, 1)
            dve.wait_ge(token_sums_done, i + 1)
            nc.vector.reciprocal(r[:], token_sum[:]).then_inc(r_done, 1)
        dve.wait_ge(r_done, ITERS + 1)
        nc.vector.tensor_tensor(weighted[:].rearrange("p t (b e) -> p (t b) e", e=E), scaled[:],
                                r[:].unsqueeze(2).to_broadcast([P, T * NB, E]), ALU.mult
                                ).then_inc(gates_done, 1)
        for i in range(4):
            dve.wait_ge(turned, 4 * (i + 1))
            nc.vector.tensor_copy(rows[:].rearrange("r (p t) -> r t p", t=T)[:, 4 * i:4 * i + 4, :],
                                  ps_rows[i][0:R, :].rearrange("r (t p) -> r t p", p=P)).then_inc(copied, 1)

    @block.tensor
    def _(pe):
        for i in range(ITERS):
            pe.wait_ge(weighted_done, i + 1)
            if i:
                pe.wait_ge(c_done, i)
            for t in range(T):
                mm = nc.tensor.matmul(ps_sum[:, 0:R], g.ones[:], weighted[:, t, :],
                                      start=(t == 0), stop=(t == T - 1))
            mm.then_inc(sums_done, 1)
        pe.wait_ge(gates_done, 1)
        for t in range(T):
            nc.tensor.transpose(ps_rows[t // 4][0:R, (t % 4) * P:(t % 4 + 1) * P], weighted[:, t, :],
                                g.ident[:]).then_inc(turned, 1)
    return rows


def top_stage(nc, g, rows, tag, ctx):
    def sb(name, shape, dt=F32):
        return ctx.enter_context(nc.sbuf_tensor(f"{name}_{tag}", shape, dt))

    def sem(name):
        return nc.alloc_semaphore(f"{name}_{tag}")

    vals = sb("top_vals", [R, M])
    idx = sb("top_idx", [R, M], U32)
    idx_f = sb("top_idx_f", [R, M])
    token_f = sb("token_f", [P, R, NH])
    token_i = sb("token_i", [P, R * NH], I32)
    part_i = sb("part_i", [P, R * NH], I32)
    tile_i = sb("tile_i", [P, R * NH], I32)
    part_f = sb("part_f", [P, R * NH])
    tile_f = sb("tile_f", [P, R * NH])
    at_tile = sb("at_tile", [P, R * NH, T], BF16)
    NU = 4
    at_part = [sb(f"at_part{i}", [P, P], BF16) for i in range(NU)]
    key = sb("key", [P, R, T])
    won = sb("won", [P, NB, T])
    ps_rank = ctx.enter_context(nc.psum_tensor(f"ps_rank_{tag}", [P, R * T], F32))
    ps_t = ctx.enter_context(nc.psum_tensor(f"ps_t_{tag}", [P, CH], F32))
    ps_v = ctx.enter_context(nc.psum_tensor(f"ps_v_{tag}", [P, CH], F32))
    maxed, indexed, replaced, idx_conv, moved, tok_copied, chain, gate_copied = (
        sem(n) for n in ("maxed", "indexed", "replaced", "idx_converted", "slots_turned",
                         "tokens_copied", "index_step", "gates_copied2"))
    part_built, part_used = sem("part_built"), sem("part_used")
    block = ctx.enter_context(nc.Block())

    @block.vector
    def _(dve):
        for k in range(M // 8):
            s = slice(8 * k, 8 * k + 8)
            if k:
                dve.wait_ge(replaced, k)
            nc.vector.max(vals[:, s], rows[:]).then_inc(maxed, 1)
            dve.wait_ge(maxed, k + 1)
            nc.vector.max_index(idx[:, s], vals[:, s], rows[:]).then_inc(indexed, 1)
            if k + 1 < M // 8:
                dve.wait_ge(indexed, k + 1)
                nc.vector.match_replace(rows[:], vals[:, s], rows[:], -1.0).then_inc(replaced, 1)
        dve.wait_ge(indexed, M // 8)
        nc.vector.tensor_copy(idx_f[:], idx[:]).then_inc(idx_conv, 1)
        dve.wait_ge(moved, 1)
        nc.vector.tensor_copy(token_f[:], ps_t[:, 0:R * NH].rearrange("p (h r) -> p r h", h=NH)
                              ).then_inc(tok_copied, 1)
        n_chain = [0]

        def step(ins):
            n_chain[0] += 1
            ins.then_inc(chain, 1)
            dve.wait_ge(chain, n_chain[0])

        dve.wait_ge(tok_copied, 1)
        flat = token_f[:].rearrange("p r h -> p (r h)")
        step(nc.vector.tensor_copy(token_i[:], flat))
        step(nc.vector.tensor_scalar(part_i[:], token_i[:], 4, None, ALU.logical_shift_right))
        step(nc.vector.tensor_scalar(tile_i[:], token_i[:], T - 1, None, ALU.bitwise_and))
        step(nc.vector.tensor_copy(part_f[:], part_i[:]))
        step(nc.vector.tensor_copy(tile_f[:], tile_i[:]))
        nc.vector.tensor_tensor(g.slot_token[:], token_f[:].rearrange("p (b e) h -> p b (e h)", b=NB),
                                g.token_base[:].unsqueeze(2).to_broadcast([P, NB, SL]), ALU.add)
        step(nc.vector.tensor_tensor(at_tile[:], tile_f[:].unsqueeze(2).to_broadcast([P, R * NH, T]),
                                     g.iota_col[:, 0:T].unsqueeze(1).to_broadcast([P, R * NH, T]),
                                     ALU.is_equal))
        for q in range(R * NH):
            if q >= NU:
                dve.wait_ge(part_used, count(q - NU + 1))
            nc.vector.tensor_scalar(at_part[q % NU][:], g.iota_col[:], part_f[:, q:q + 1],
                                    g.rank_of[:, q % NH:q % NH + 1], ALU.is_equal, ALU.mult
                                    ).then_inc(part_built, 1)
        dve.wait_ge(part_used, R * NH)
        ranks = ps_rank[:].rearrange("p (r t) -> p r t", t=T)
        step(nc.vector.scalar_tensor_tensor(key[:], ranks, float(E),
                                            g.expert_of[:].unsqueeze(2).to_broadcast([P, R, T]),
                                            ALU.mult, ALU.add))
        step(nc.vector.scalar_tensor_tensor(key[:], ranks, 0.0, key[:], ALU.is_gt, ALU.mult))
        step(nc.vector.tensor_reduce(won[:], key[:].rearrange("p (b e) t -> p b t e", e=E), AX.X, ALU.max))
        nc.vector.tensor_copy(g.token_row[:], won[:])

    @block.scalar
    def _(act):
        act.wait_ge(moved, 2)
        nc.scalar.mul(g.slot_gate[:].rearrange("p b (e h) -> p (b e) h", h=NH),
                      ps_v[:, 0:R * NH].rearrange("p (h r) -> p r h", h=NH), 0.5).then_inc(gate_copied, 1)

    @block.tensor
    def _(pe):
        pe.wait_ge(idx_conv, 1)
        for src, dst in ((idx_f, ps_t), (vals, ps_v)):
            for h in range(NH):
                mm = nc.tensor.transpose(dst[:, h * R:(h + 1) * R], src[:, h * P:(h + 1) * P],
                                         g.ident[0:R, 0:R])
            mm.then_inc(moved, 1)
        for q in range(R * NH):
            row = q // NH
            pe.wait_ge(part_built, q + 1)
            nc.tensor.matmul(ps_rank[:, row * T:(row + 1) * T], at_part[q % NU][:], at_tile[:, q, :],
                             start=(q % NH == 0), stop=(q % NH == NH - 1)).then_inc(part_used, 1)


def mixer(nc, g, x, ctx):
    def sb(name, shape, dt=F32):
        return ctx.enter_context(nc.sbuf_tensor(name, shape, dt))

    def sem(name):
        return ctx.enter_context(nc.semaphore(name))

    def ps(name):
        return ctx.enter_context(nc.psum_tensor(name, [P, CH], F32))

    NS, NX, NY, NK, NRES = 6, 3, 2, 4, 4
    LEAD = NS
    FFN = 6
    BACK = 22
    ADD = BACK + NK
    SCALES = ADD + T + 1
    TURN = SCALES + 5
    OUT = 5
    SQUARE = 9
    STEP = 3
    RES = 43
    state = [sb(f"state{i}", [P, NT]) for i in range(NS)]
    conv_in = sb("conv_in", [P, KC - 1 + NT])
    xc = [sb(f"xc{i}", [P, NT]) for i in range(J)]
    res = [sb(f"res{i}", [P, NT]) for i in range(2)]
    delta = [sb(f"delta{i}", [P, NT]) for i in range(2)]
    drive = [sb(f"drive{i}", [P, NT]) for i in range(2)]
    x1 = sb("x1", [P, T, D])
    x1t = sb("x1t", [P, KD, NT])
    resid = [sb(f"resid{i}", [P, 2, D]) for i in range(NRES)]
    picked = [sb(f"picked{i}", [P, D]) for i in range(NX)]
    picked_t = [sb(f"picked_t{i}", [P, KD, P]) for i in range(2)]
    routed = [sb(f"routed{i}", [P, D]) for i in range(NY)]
    back = [sb(f"back{i}", [P, D]) for i in range(NK)]
    expert = [sb(f"expert{i}", [P, KD, D]) for i in range(2)]
    slot_now = sb("slot_now", [P, SL], I32)
    gate_now = sb("gate_now", [P, SL])
    row_now = sb("row_now", [P, T], I32)
    stats = sb("m_stats", [P, T, 6])
    moments = sb("m_moments", [P, T, 2])
    rstd = sb("m_rstd", [P, T])
    shift = sb("m_shift", [P, T])
    eps = sb("m_eps", [P, 1])
    ps_sum = [ps(f"ps_states{c}") for c in range(C)]
    ps_proj = [ps(f"ps_proj{i}") for i in range(2)]
    ps_rows = [ps(f"ps_rows{i}") for i in range(2)]

    decay_ready = sem("decay_ready")
    state_ready = sem("state_ready")
    pair_added, pair_used = sem("pair_added"), sem("pair_used")
    setup = sem("m_setup")
    ssm_done, ssm_copied, conv_step, conv_done = (sem(n) for n in ("ssm_done", "ssm_copied", "conv_step", "conv_done"))
    res_done, res_copied, res_gated, xc_done, soft_step, soft_done, drive_done, delta_done = (
        sem(n) for n in ("res_done", "res_copied", "res_gated", "xc_done", "soft_step", "soft_done", "drive_done", "delta_done"))
    gated, y_done, out_done, out_added = (sem(n) for n in ("gated", "y_done", "out_done", "out_added"))
    now_set = sem("now_set")
    picked_in = [sem(f"picked_in{i}") for i in range(NX)]
    pick_turned, pick_copied, expert_done, routed_scaled = (
        sem(n) for n in ("pick_turned", "pick_copied", "expert_done", "routed_scaled"))
    expert_in = [sem(f"expert_in{i}") for i in range(2)]
    routed_out = [sem(f"routed_out{i}") for i in range(NY)]
    back_in = [sem(f"back_in{i}") for i in range(NK)]
    x_in, x1_added = sem("m_x_in"), sem("x1_added")
    x1_stored = [sem(f"x1_stored{i}") for i in range(2)]
    stats_done, moments_done, log_done, rstd_done, shift_done, normed, x1_turned, x1t_copied = (
        sem(n) for n in ("m_stats_done", "m_moments_done", "m_log_var_done", "m_rstd_done", "m_shift_done",
                         "m_normed", "x1_turned", "x1t_copied"))
    resid_in = [sem(f"resid_in{i}") for i in range(NRES)]
    x2_out = [sem(f"x2_out{i}") for i in range(NRES)]

    x_v = x.rearrange("b (p t) d -> b p t d", t=T)
    x1_v = g.x1.rearrange("(b p t) d -> b p t d", p=P, t=T)
    x2_v = g.x2.rearrange("b (p t) d -> b p t d", t=T)
    routed_v = g.routed[0].rearrange("(m e) d -> e m d", e=E)
    G2 = T // 2

    TH = T // 2
    x1_half = [x1[:, i * TH:(i + 1) * TH, :].rearrange("p t d -> p (t d)") for i in range(2)]
    xc_now = [x1_half[1], xc[3][:], xc[2][:], xc[3][:]]
    y_now = [xc[0][:], xc[1][:], xc[2][:], x1_half[0]]

    def projections(b, q, last):
        j, n = q // N, q % N
        if j in (1, 2) and 2 <= n < 2 + C:
            return "ssm", b, j + 1, n - 2
        if j in (1, 2) and 2 + C <= n < 2 + 2 * C:
            return "res", b, j, n - 2 - C
        if RES <= q < RES + C:
            return "res", b, J - 1, q - RES
        first = TURN + 4
        if not last and first <= q < first + 3 * C:
            branch, unit = (("ssm", 0), ("res", 0), ("ssm", 1))[(q - first) // C]
            return branch, b + 1, unit, (q - first) % C
        return None

    def silu_at(j):
        return 11 if j == J - 1 else 10

    def conv_at(j):
        return TURN - (J - 1) * N + 6 if j == J - 1 else 4


    def batches(eng, body):
        body(0, True, False)
        with eng.Fori(1, NB - 1) as b:
            body(b, False, False)
        body(NB - 1, False, True)

    block = ctx.enter_context(nc.Block())

    @block.sync
    def _(sp):
        def load_expert(nb, e):
            sp.wait_ge(expert_done, count(nb * SL + (e - 2) * NH + NH if e >= 2 else nb * SL))
            sp.dma_start(expert[e % 2][:], g.experts[e].rearrange("(k p) f -> p k f", p=P)
                         ).then_inc(expert_in[e % 2], 16)

        def load_x(nb):
            sp.dma_start(x1[:], x_v[bass.ds(nb, 1)].rearrange("a p t d -> p (a t) d")).then_inc(x_in, 16)

        def store_slots(nb, s):
            e, h = s // NH, s % NH
            sp.wait_ge(routed_scaled, nb * SL + s + 1)
            sp.dma_start(routed_v[e, 1 + h * P:1 + (h + 1) * P, :],
                         routed[s % NY][:]).then_inc(routed_out[s % NY], 16)
            if h == NH - 1 and e + 2 < E:
                load_expert(nb, e + 2)

        def store_x1(nb):
            for i in range(2):
                sp.wait_ge(x1_added, nb * T + (i + 1) * TH)
                sp.dma_start(x1_v[bass.ds(nb, 1), :, i * TH:(i + 1) * TH, :].rearrange("a p t d -> p (a t) d"),
                             x1[:, i * TH:(i + 1) * TH, :]).then_inc(x1_stored[i], 16)

        def load_resid(b, r):
            sp.dma_start(resid[r % NRES][:], x1_v[bass.ds(b, 1), :, 2 * r:2 * r + 2, :].rearrange("a p t d -> p (a t) d")
                         ).then_inc(resid_in[r % NRES], 16)

        def load_resids(b):
            for i in range(2):
                sp.wait_ge(x1_stored[i], (b + 1) * 16)
                sp.sem_inc(g.passed_sp, 1)
            for r in range(NRES):
                sp.wait_ge(x2_out[r], b * 16 * (G2 // NRES))
                load_resid(b, r)

        def store_result(b, r):
            sp.wait_ge(out_added, b * G2 + r + 1)
            sp.dma_start(x2_v[bass.ds(b, 1), :, 2 * r:2 * r + 2, :].rearrange("a p t d -> p (a t) d"), resid[r % NRES][:]
                         ).then_inc(x2_out[r % NRES], 16)
            if r >= 1 and r + NRES - 1 < G2:
                sp.wait_ge(x2_out[(r - 1) % NRES], (b * (G2 // NRES) + (r - 1) // NRES + 1) * 16)
                load_resid(b, r + NRES - 1)

        def body(b, first, last):
            if not last:
                for i in range(NK):
                    sp.wait_ge(back_in[i], (b + 1) * 16 * (T // NK))
                    sp.sem_inc(g.passed_sp, 1)
                load_expert(b + 1, 0)
                load_expert(b + 1, 1)
            for s in range(SL):
                if not first and s % 2:
                    store_result(b - 1, s // 2)
                if last:
                    continue
                if s == SL - 1:
                    sp.wait_ge(x1_turned, (b + 1) * G2)
                    sp.sem_inc(g.passed_sp, 1)
                    sp.wait_ge(y_done, b * J + 1)
                    sp.sem_inc(g.passed_sp, 1)
                    sp.wait_ge(out_done, count(b * G2))
                    sp.sem_inc(g.passed_sp, 1)
                    load_x(b + 1)
                store_slots(b + 1, s)
            if not last:
                store_x1(b + 1)
            load_resids(b)

        load_x(0)
        load_expert(0, 0)
        load_expert(0, 1)
        for s in range(SL):
            store_slots(0, s)
        store_x1(0)
        batches(sp, body)
        for r in range(G2):
            store_result(NB - 1, r)
        for r in range(NRES):
            sp.wait_ge(x2_out[r], NB * 16 * (G2 // NRES))

    @block.gpsimd
    def _(pool):
        def pick(nb, s):
            if s == 0:
                pool.wait_ge(now_set, (nb + 1) * 3)
            pool.wait_ge(pick_turned, nb * SL + (s - NX + 1 if s >= NX else 0))
            pool.sem_inc(g.passed_pool, 1)
            nc.gpsimd.indirect_dma_start(
                out=picked[s % NX][:], out_offset=None, in_=g.normed,
                in_offset=bass.IndirectOffsetOnAxis(ap=slot_now[:, s:s + 1].bitcast(U32), axis=0)
            ).then_inc(picked_in[s % NX], 16)

        def bring_back(nb, t):
            if t == 0:
                for i in range(NY):
                    pool.wait_ge(routed_out[i], (nb + 1) * 16 * (SL // NY))
            pool.wait_ge(x1_added, nb * T + (t - NK + 1 if t >= NK else 0))
            pool.sem_inc(g.passed_pool, 1)
            nc.gpsimd.indirect_dma_start(
                out=back[t % NK][:], out_offset=None, in_=g.routed[0],
                in_offset=bass.IndirectOffsetOnAxis(ap=row_now[:, t:t + 1].bitcast(U32), axis=0)
            ).then_inc(back_in[t % NK], 16)

        def square(b, j):
            u = b * J + j
            pool.wait_ge(xc_done, u + 1)
            pool.wait_ge(state_ready, count((u - 1) * N))
            nc.gpsimd.tensor_tensor(drive[j % 2][:], xc_now[j], xc_now[j], ALU.mult).then_inc(drive_done, 1)

        def body(b, first, last):
            if not last:
                for s in range(NX):
                    pick(b + 1, s)
            for q in range(1, J * N, 2):
                pool.wait_ge(state_ready, b * J * N + q + 1)
                nc.gpsimd.tensor_tensor(state[q % NS][:], state[q % NS - 1][:], state[q % NS][:], ALU.add
                                        ).then_inc(pair_added, 1)
                if q % N == SQUARE and q < (J - 1) * N:
                    square(b, q // N + 1)
                elif q % N == SQUARE and not last:
                    square(b + 1, 0)
                if last:
                    continue
                for v in (q, q + 1):
                    if NX <= v - 1 < SL:
                        pick(b + 1, v - 1)
                    if BACK <= v < BACK + T:
                        bring_back(b + 1, v - BACK)

        for s in range(SL):
            pick(0, s)
        for t in range(T):
            bring_back(0, t)
        square(0, 0)
        batches(pool, body)

    @block.vector
    def _(dve):
        def set_now(nb):
            for i in range(NK):
                dve.wait_ge(back_in[i], nb * 16 * (T // NK))
            nc.vector.tensor_copy(slot_now[:], g.slot_token[:, bass.ds(nb, 1), :].rearrange("p a s -> p (a s)")).then_inc(now_set, 1)
            dve.wait_ge(routed_scaled, nb * SL)
            nc.vector.tensor_copy(gate_now[:], g.slot_gate[:, bass.ds(nb, 1), :].rearrange("p a s -> p (a s)")).then_inc(now_set, 1)
            nc.vector.tensor_copy(row_now[:], g.token_row[:, bass.ds(nb, 1), :].rearrange("p a s -> p (a s)")).then_inc(now_set, 1)

        def add_routed(nb, t):
            if t == 0:
                dve.wait_ge(x_in, (nb + 1) * 16)
            dve.wait_ge(back_in[t % NK], (nb * (T // NK) + t // NK + 1) * 16)
            nc.vector.tensor_tensor(x1[:, t, :], x1[:, t, :], back[t % NK][:], ALU.add).then_inc(x1_added, 1)
            dve.wait_ge(x1_added, nb * T + t + 1)
            nc.vector.bn_stats(stats[:, t, :], x1[:, t, :]).then_inc(stats_done, 1)

        def aggregate(nb):
            dve.wait_ge(stats_done, (nb + 1) * T)
            dve.sem_inc(g.passed_dve, 1)
            for t in range(T):
                nc.vector.bn_aggr(moments[:, t, :], stats[:, t, :]).then_inc(moments_done, 1)

        def scales(nb):
            dve.wait_ge(rstd_done, nb + 1)
            dve.wait_ge(moments_done, (nb + 1) * T)
            nc.vector.scalar_tensor_tensor(shift[:], moments[:, :, 0], -1.0, rstd[:], ALU.mult, ALU.mult
                                           ).then_inc(shift_done, 1)

        def normalise(nb, t):
            if t == 0:
                dve.wait_ge(shift_done, nb + 1)
            if t % TH == 0:
                dve.wait_ge(x1_stored[t // TH], (nb + 1) * 16)
            nc.vector.tensor_scalar(x1[:, t, :], x1[:, t, :], rstd[:, t:t + 1], shift[:, t:t + 1],
                                    ALU.mult, ALU.add).then_inc(normed, 1)

        def conv(b, j, taps):
            u = b * J + j
            v = delta[j % 2]
            for i in taps:
                k = KC - 1 - i
                if i == 0:
                    dve.wait_ge(ssm_copied, (u + 1) * C)
                    ins = nc.vector.tensor_scalar(v[:], conv_in[:, k:k + NT], g.conv_w[:, j, k:k + 1], None, ALU.mult)
                else:
                    dve.wait_ge(conv_step, u * (KC - 1) + i)
                    ins = nc.vector.scalar_tensor_tensor(v[:], conv_in[:, k:k + NT], g.conv_w[:, j, k:k + 1], v[:],
                                                         ALU.mult, ALU.add)
                ins.then_inc(conv_step if i < KC - 1 else conv_done, 1)

        def step_size(b, j):
            u = b * J + j
            dve.wait_ge(soft_done, u + 1)
            nc.vector.scalar_tensor_tensor(delta[j % 2][:], xc_now[j], 0.0, delta[j % 2][:], ALU.max, ALU.add
                                           ).then_inc(delta_done, 1)

        def gate(b, j):
            u = b * J + j
            dve.wait_ge(pair_used, b * (J * N // 2) + (j + 1) * (N // 2))
            dve.wait_ge(res_gated, u + 1)
            for c in range(C):
                s = slice(c * CH, (c + 1) * CH)
                nc.vector.tensor_tensor(res[j % 2][:, s], ps_sum[c][:], res[j % 2][:, s], ALU.mult).then_inc(gated, 1)

        def combine(b, j):
            u = b * J + j
            dve.wait_ge(gated, (u + 1) * C)
            if j == 0:
                dve.wait_ge(out_done, b * G2)
            nc.vector.scalar_tensor_tensor(y_now[j], res[j % 2][:], g.skip[:, j:j + 1], xc_now[j], ALU.add, ALU.mult
                                           ).then_inc(y_done, 1)

        def add_out(b, r):
            dve.wait_ge(out_done, b * G2 + r + 1)
            dve.wait_ge(resid_in[r % NRES], (b * (G2 // NRES) + r // NRES + 1) * 16)
            nc.vector.tensor_tensor(resid[r % NRES][:].rearrange("p t d -> p (t d)"), ps_rows[1][:],
                                    resid[r % NRES][:].rearrange("p t d -> p (t d)"), ALU.add).then_inc(out_added, 1)

        def finish(b, q):
            if q == 2:
                gate(b, J - 1)
                combine(b, J - 1)
            if q in range(OUT, OUT + T, 2):
                add_out(b, (q - OUT) // 2)

        def body(b, first, last):
            if not last:
                set_now(b + 1)
            for j in range(J):
                for n in range(N):
                    q = j * N + n
                    if n == 0:
                        dve.wait_ge(drive_done, b * J + j + 1)
                    dve.wait_ge(decay_ready, b * J * N + q + 1)
                    nc.vector.tensor_tensor_scan(state[q % NS][:], state[q % NS][:], drive[j % 2][:], 0.0,
                                                 ALU.mult, ALU.add).then_inc(state_ready, 1)
                    if not first:
                        finish(b - 1, q)
                    if j and n == 2:
                        gate(b, j - 1)
                    if j and n == 4:
                        combine(b, j - 1)
                    if not (last and j == J - 1):
                        nb, nj = (b, j + 1) if j < J - 1 else (b + 1, 0)
                        if conv_at(j) <= n < conv_at(j) + KC:
                            conv(nb, nj, (n - conv_at(j),))
                        if n == silu_at(j) + STEP:
                            step_size(nb, nj)
                    if last:
                        continue
                    if ADD <= q < ADD + T:
                        add_routed(b + 1, q - ADD)
                    if q == ADD + T:
                        aggregate(b + 1)
                    if q == SCALES:
                        scales(b + 1)
                    if SCALES <= q < SCALES + 4:
                        for t in range(4 * (q - SCALES), 4 * (q - SCALES) + 4):
                            normalise(b + 1, t)

        nc.vector.memset(conv_in[:, 0:KC - 1], 0.0).then_inc(setup, 1)
        nc.vector.memset(eps[:], LN_EPS).then_inc(setup, 1)
        set_now(0)
        for t in range(T):
            add_routed(0, t)
        aggregate(0)
        scales(0)
        for t in range(T):
            normalise(0, t)
        dve.wait_ge(setup, 2)
        conv(0, 0, range(KC))
        step_size(0, 0)
        batches(dve, body)
        for q in range(OUT + T):
            finish(NB - 1, q)

    @block.scalar
    def _(act):
        def read_bank(nb, s):
            act.wait_ge(pick_turned, nb * SL + min(s + 1, SL))
            act.wait_ge(expert_done, nb * SL + s)
            if s < SL:
                nc.scalar.copy(picked_t[s % 2][:].rearrange("p k n -> p (k n)"), ps_rows[0][:, 0:KD * P]
                               ).then_inc(pick_copied, 1)
            if s == 1:
                act.wait_ge(now_set, (nb + 1) * 3)
            if s:
                act.wait_ge(routed_out[(s - 1) % NY], (nb * (SL // NY) + (s - 1) // NY) * 16)
                nc.scalar.activation(routed[(s - 1) % NY][:], ps_rows[0][:, CH - D:CH], ACT.Identity,
                                     scale=gate_now[:, s - 1:s]).then_inc(routed_scaled, 1)

        def deviation(nb):
            act.wait_ge(moments_done, (nb + 1) * T)
            act.wait_ge(normed, nb * T)
            nc.scalar.activation(rstd[:], moments[:, :, 1], ACT.Ln, bias=eps[:, 0:1]).then_inc(log_done, 1)
            act.wait_ge(log_done, nb + 1)
            nc.scalar.activation(rstd[:], rstd[:], ACT.Exp, scale=-0.5).then_inc(rstd_done, 1)

        def copy_turned(nb, i):
            act.wait_ge(x1_turned, nb * G2 + i + 1)
            nc.scalar.copy(x1t[:].rearrange("p k (n t) -> p t k n", t=T)[:, 2 * i:2 * i + 2],
                           ps_rows[i % 2][:].rearrange("p (t k n) -> p t k n", t=2, k=KD)).then_inc(x1t_copied, 1)

        def copy_ssm(b, j, c):
            u = b * J + j
            act.wait_ge(ssm_done, u * C + c + 1)
            if c == 0:
                act.wait_ge(conv_done, u)
            nc.scalar.copy(conv_in[:, KC - 1 + c * CH:KC - 1 + (c + 1) * CH], ps_proj[c % 2][:]).then_inc(ssm_copied, 1)

        def copy_res(b, j, c):
            u = b * J + j
            act.wait_ge(res_done, u * C + c + 1)
            if c == 0:
                act.wait_ge(y_done, count(u - 1))
            nc.scalar.copy(res[j % 2][:, c * CH:(c + 1) * CH], ps_proj[c % 2][:]).then_inc(res_copied, 1)

        def gate_res(b, j):
            u = b * J + j
            act.wait_ge(res_copied, (u + 1) * C)
            nc.scalar.activation(res[j % 2][:], res[j % 2][:], ACT.Silu).then_inc(res_gated, 1)

        def activate(b, j):
            u = b * J + j
            act.wait_ge(conv_done, u + 1)
            if j == 1:
                act.wait_ge(y_done, b * J)
            elif j == 2:
                act.wait_ge(out_done, b * G2)
            elif j == 3:
                act.wait_ge(y_done, b * J + 2)
            else:
                act.wait_ge(x1_turned, (b + 1) * G2)
            nc.scalar.activation(xc_now[j], delta[j % 2][:], ACT.Silu, bias=g.conv_b[:, j:j + 1]).then_inc(xc_done, 1)

        def magnitude(b, j):
            u = b * J + j
            act.wait_ge(xc_done, u + 1)
            nc.scalar.activation(delta[j % 2][:], xc_now[j], ACT.Abs).then_inc(soft_step, 1)

        def soft_exp(b, j):
            u = b * J + j
            act.wait_ge(soft_step, 2 * u + 1)
            nc.scalar.activation(delta[j % 2][:], delta[j % 2][:], ACT.Exp, scale=-1.0).then_inc(soft_step, 1)

        def soft_log(b, j):
            u = b * J + j
            act.wait_ge(soft_step, 2 * u + 2)
            nc.scalar.activation(delta[j % 2][:], delta[j % 2][:], ACT.Ln, bias=1.0).then_inc(soft_done, 1)

        def both_tables():
            nc.scalar.preload_act_table_set("natural_log_exp_and_others")

        def body(b, first, last):
            for j in range(J):
                for n in range(N):
                    q = j * N + n
                    if n == 0:
                        act.wait_ge(delta_done, b * J + j + 1)
                    before = q - NS if q >= NS else max(v for v in range(J * N) if v % NS == q) - J * N
                    act.wait_ge(pair_used if q % 2 else pair_added, count(b * (J * N // 2) + before // 2 + 1))
                    nc.scalar.activation(state[q % NS][:], delta[j % 2][:], ACT.Exp, scale=g.neg_a[:, j, n:n + 1]
                                         ).then_inc(decay_ready, 1)
                    if not last and FFN <= q <= FFN + SL:
                        read_bank(b + 1, q - FFN)
                    chunk = projections(b, q, last)
                    if chunk:
                        (copy_ssm if chunk[0] == "ssm" else copy_res)(*chunk[1:])
                    if not last and q == SCALES + 1:
                        deviation(b + 1)
                    if not last and TURN <= q < TURN + 4:
                        for i in range(2 * (q - TURN), 2 * (q - TURN) + 2):
                            copy_turned(b + 1, i)
                    if n == silu_at(j):
                        gate_res(b, j)
                    if not (last and j == J - 1):
                        nb, nj = (b, j + 1) if j < J - 1 else (b + 1, 0)
                        if n == silu_at(j):
                            activate(nb, nj)
                        if n == silu_at(j) + 1:
                            magnitude(nb, nj)
                        if n == silu_at(j) + 2:
                            soft_exp(nb, nj)
                        if n == silu_at(j) + 3:
                            soft_log(nb, nj)
                    if n == silu_at(j):
                        both_tables()

        for s in range(SL + 1):
            read_bank(0, s)
        act.wait_ge(setup, 2)
        both_tables()
        deviation(0)
        for i in range(G2):
            copy_turned(0, i)
        for c in range(C):
            copy_ssm(0, 0, c)
        for c in range(C):
            copy_res(0, 0, c)
        activate(0, 0)
        both_tables()
        magnitude(0, 0)
        soft_exp(0, 0)
        soft_log(0, 0)
        for c in range(C):
            copy_ssm(0, 1, c)
        batches(act, body)

    @block.tensor
    def _(pe):
        def fill_bank(nb, s):
            if s:
                pe.wait_ge(pick_copied, nb * SL + s)
                pe.wait_ge(routed_scaled, nb * SL + s - 1)
            else:
                pe.wait_ge(x1t_copied, nb * G2)
            if s:
                e = (s - 1) // NH
                pe.wait_ge(expert_in[e % 2], (nb * (E // 2) + e // 2 + 1) * 16)
                for k in range(KD):
                    mm = nc.tensor.matmul(ps_rows[0][:, CH - D:CH], picked_t[(s - 1) % 2][:, k, :], expert[e % 2][:, k, :],
                                          start=(k == 0), stop=(k == KD - 1))
                mm.then_inc(expert_done, 1)
            if s < SL:
                full = [len([v for v in range(SL) if v % NX == i]) for i in range(NX)]
                pe.wait_ge(picked_in[s % NX], (nb * full[s % NX] + s // NX + 1) * 16)
                for k in range(KD):
                    mm = nc.tensor.transpose(ps_rows[0][:, k * P:(k + 1) * P], picked[s % NX][:, k * P:(k + 1) * P], g.ident[:])
                mm.then_inc(pick_turned, 1)

        def turn_x1(nb, i):
            pe.wait_ge(normed, nb * T + 2 * i + 2)
            if i >= 2:
                pe.wait_ge(x1t_copied, count(nb * G2 + i - 1))
            elif i == 0:
                pe.wait_ge(routed_scaled, (nb + 1) * SL)
            else:
                pe.wait_ge(out_added, count((nb - 1) * G2))
            for t in (2 * i, 2 * i + 1):
                for k in range(KD):
                    c = (t % 2) * KD + k
                    mm = nc.tensor.transpose(ps_rows[i % 2][:, c * P:(c + 1) * P], x1[:, t, k * P:(k + 1) * P], g.ident[:])
            mm.then_inc(x1_turned, 1)

        def project(bank, col, c):
            for k in range(KD):
                mm = nc.tensor.matmul(ps_proj[bank][:], g.w_in[:, k, col:col + P], x1t[:, k, c * CH:(c + 1) * CH],
                                      start=(k == 0), stop=(k == KD - 1))
            return mm

        def project_ssm(b, j, c):
            u = b * J + j
            if c == 0:
                pe.wait_ge(x1t_copied, (b + 1) * G2)
            if c >= 2:
                pe.wait_ge(ssm_copied, count(u * C + c - 1))
            elif j == 2:
                pe.wait_ge(ssm_copied, u * C)
            else:
                pe.wait_ge(res_copied, count((u, u, None, u - 1)[j] * C))
            project(c % 2, j * P, c).then_inc(ssm_done, 1)

        def project_res(b, j, c):
            u = b * J + j
            if c >= 2:
                pe.wait_ge(res_copied, count(u * C + c - 1))
            elif j < J - 1:
                pe.wait_ge(ssm_copied, (u + (2 if j else 1)) * C)
            else:
                pe.wait_ge(res_copied, u * C)
            project(c % 2, INNER + j * P, c).then_inc(res_done, 1)

        def project_out(b, r, last):
            if r:
                pe.wait_ge(out_added, b * G2 + r)
            else:
                pe.wait_ge(y_done, (b + 1) * J)
                pe.wait_ge(x1t_copied, NB * G2 if last else (b + 2) * G2)
            for t in (2 * r, 2 * r + 1):
                for j in range(J):
                    mm = nc.tensor.matmul(ps_rows[1][:, (t % 2) * D:(t % 2 + 1) * D],
                                          y_now[j].rearrange("p (n t) -> p n t", t=T)[:, :, t],
                                          g.w_out[:, j, :], start=(j == 0), stop=(j == J - 1))
            mm.then_inc(out_done, 1)

        def beside(b, v, last):
            j, n = v // N, v % N
            if not last and FFN <= v <= FFN + SL:
                fill_bank(b + 1, v - FFN)
            chunk = projections(b, v, last)
            if chunk:
                (project_ssm if chunk[0] == "ssm" else project_res)(*chunk[1:])
            if not last and TURN <= v < TURN + 4:
                for i in range(2 * (v - TURN), 2 * (v - TURN) + 2):
                    turn_x1(b + 1, i)

        def body(b, first, last):
            for v in range(LEAD):
                beside(b, v, last)
            for j in range(J):
                for n in range(1, N, 2):
                    q = j * N + n
                    for c in range(C):
                        if c == 0:
                            pe.wait_ge(pair_added, b * (J * N // 2) + q // 2 + 1)
                        if n == 1:
                            pe.wait_ge(gated, count((b * J + j - 1) * C + c + 1))
                        mm = nc.tensor.matmul(ps_sum[c][:], g.ident[:], state[q % NS][:, c * CH:(c + 1) * CH],
                                              start=(n == 1), stop=(n == N - 1))
                    mm.then_inc(pair_used, 1)
                    if q + LEAD - 1 < J * N:
                        beside(b, q + LEAD - 1, last)
                    if not first and q < T:
                        project_out(b - 1, q // 2, False)
                    if q + LEAD < J * N:
                        beside(b, q + LEAD, last)

        for s in range(SL + 1):
            fill_bank(0, s)
        for i in range(G2):
            turn_x1(0, i)
        for c in range(C):
            project_ssm(0, 0, c)
        for c in range(C):
            project_res(0, 0, c)
        for c in range(C):
            project_ssm(0, 1, c)
        batches(pe, body)
        for r in range(G2):
            project_out(NB - 1, r, True)


def ffn(nc, g, x, out, ctx):
    def sb(name, shape, dt=F32):
        return ctx.enter_context(nc.sbuf_tensor(name, shape, dt))

    def sem(name):
        return ctx.enter_context(nc.semaphore(name))

    def ps(name):
        return ctx.enter_context(nc.psum_tensor(name, [P, CH], F32))

    NX = NY = NK = 8
    NT4 = 4
    BRING, JOIN = SL + 6, SL + 10
    expert = sb("f_expert", [P, E, KD, D])
    slot_now = [sb(f"f_slot_now{i}", [P, SL], I32) for i in range(2)]
    row_now = [sb(f"f_row_now{i}", [P, T], I32) for i in range(2)]
    picked = [sb(f"f_picked{i}", [P, D]) for i in range(NX)]
    picked_t = [sb(f"f_picked_t{i}", [P, KD, P]) for i in range(NT4)]
    routed = [sb(f"f_routed{i}", [P, D]) for i in range(NY)]
    back = [sb(f"f_back{i}", [P, D]) for i in range(NK)]
    total = [sb(f"f_total{i}", [P, T, D]) for i in range(2)]
    ps_turn = [ps(f"f_ps_turn{i}") for i in range(NT4)]
    ps_out = [ps(f"f_ps_out{i}") for i in range(NT4)]
    expert_in, now_set, rows_set = sem("f_expert_in"), sem("f_now_set"), sem("f_rows_set")
    picked_in = [sem(f"f_picked_in{i}") for i in range(NX)]
    routed_out = [sem(f"f_routed_out{i}") for i in range(NY)]
    back_in = [sem(f"f_back_in{i}") for i in range(NK)]
    x_in = [sem(f"f_x_in{i}") for i in range(2)]
    out_stored = [sem(f"f_out_stored{i}") for i in range(2)]
    turned, copied, product, scaled, added = (
        sem(n) for n in ("f_turned", "f_copied", "f_product", "f_scaled", "f_added"))
    x_v = x.rearrange("b (p t) d -> b p t d", t=T)
    out_v = out.rearrange("b (p t) d -> b p t d", t=T)
    routed_v = [table.rearrange("(m e) d -> e m d", e=E) for table in g.routed]
    block = ctx.enter_context(nc.Block())

    def rounds(eng, turn):
        turn(0, 0)
        turn(0, 1)
        with eng.Fori(1, NB // 2 - 1) as i:
            turn(i, 0)
            turn(i, 1)
        for i in range(NB // 2 - 1, NB // 2 + 1):
            turn(i, 0)
            turn(i, 1)

    def there(b):
        return not isinstance(b, int) or 0 <= b < NB

    def behind(i, odd, s, lag):
        k = (lag - s + SL - 1) // SL
        return 2 * i + odd - k, s - lag + SL * k, (odd - k) % 2, i + (odd - k) // 2

    @block.sync
    def _(sp):
        def load_x(b, odd):
            sp.dma_start(total[odd][:], x_v[bass.ds(b, 1)].rearrange("a p t d -> p (a t) d")).then_inc(x_in[odd], 16)

        def turn(i, odd):
            b = 2 * i + odd
            for s in range(SL):
                e, h = s // NH, s % NH
                if there(b):
                    if s == 0:
                        for k in range(NK):
                            sp.wait_ge(back_in[k], count((b - 1) * 16 * (T // NK)))
                            sp.sem_inc(g.passed_sp, 1)
                    sp.wait_ge(scaled, b * SL + s + 1)
                    sp.dma_start(routed_v[odd][e, 1 + h * P:1 + (h + 1) * P, :],
                                 routed[s % NY][:]).then_inc(routed_out[s % NY], 16)
                if s == JOIN - SL + 2 and there(b - 2):
                    sp.wait_ge(added, (b - 1) * T)
                    sp.dma_start(out_v[bass.ds(b - 2, 1)].rearrange("a p t d -> p (a t) d"), total[odd][:]
                                 ).then_inc(out_stored[odd], 16)
            if there(b) and there(b - 2):
                sp.wait_ge(out_stored[odd], i * 16)
                load_x(b, odd)

        for e in range(E):
            sp.dma_start(expert[:, e, :, :], g.experts[e].rearrange("(k p) f -> p k f", p=P)).then_inc(expert_in, 16)
        load_x(0, 0)
        load_x(1, 1)
        rounds(sp, turn)
        for odd in range(2):
            sp.wait_ge(out_stored[odd], NB // 2 * 16)

    @block.gpsimd
    def _(pool):
        def turn(i, odd):
            b = 2 * i + odd
            for s in range(SL):
                if there(b):
                    if s == 0:
                        pool.wait_ge(now_set, b + 1)
                    pool.wait_ge(turned, count(b * SL + s - NX + 1))
                    pool.sem_inc(g.passed_pool, 1)
                    nc.gpsimd.indirect_dma_start(
                        out=picked[s % NX][:], out_offset=None, in_=g.normed,
                        in_offset=bass.IndirectOffsetOnAxis(ap=slot_now[odd][:, s:s + 1].bitcast(U32), axis=0)
                    ).then_inc(picked_in[s % NX], 16)
                m, t, table, _ = behind(i, odd, s, BRING)
                if there(m):
                    if t == 0:
                        pool.wait_ge(rows_set, m + 1)
                        for k in range(NY):
                            pool.wait_ge(routed_out[k], (m + 1) * 16 * (SL // NY))
                    pool.wait_ge(added, count(m * T + t - NK + 1))
                    pool.sem_inc(g.passed_pool, 1)
                    nc.gpsimd.indirect_dma_start(
                        out=back[t % NK][:], out_offset=None, in_=g.routed[table],
                        in_offset=bass.IndirectOffsetOnAxis(ap=row_now[table][:, t:t + 1].bitcast(U32), axis=0)
                    ).then_inc(back_in[t % NK], 16)

        rounds(pool, turn)

    @block.vector
    def _(dve):
        def set_slots(b, odd):
            for k in range(NX):
                dve.wait_ge(picked_in[k], count((b - 1) * 16 * (SL // NX)))
            nc.vector.tensor_copy(slot_now[odd][:], g.slot_token[:, bass.ds(b, 1), :].rearrange("p a s -> p (a s)")
                                  ).then_inc(now_set, 1)

        def set_rows(b, odd):
            for k in range(NK):
                dve.wait_ge(back_in[k], count((b - 1) * 16 * (T // NK)))
            nc.vector.tensor_copy(row_now[odd][:], g.token_row[:, bass.ds(b, 1), :].rearrange("p a s -> p (a s)")
                                  ).then_inc(rows_set, 1)

        def turn(i, odd):
            b = 2 * i + odd
            for s in range(SL):
                if there(b):
                    dve.wait_ge(turned, b * SL + s + 1)
                    dve.wait_ge(product, count(b * SL + s - NT4 + 1))
                    nc.vector.tensor_copy(picked_t[s % NT4][:].rearrange("p k n -> p (k n)"),
                                          ps_turn[s % NT4][:, 0:KD * P]).then_inc(copied, 1)
                if s == 2 and there(b + 1) and not (isinstance(b, int) and b < 0):
                    set_slots(b + 1, 1 - odd)
                m, t, table, turn_of = behind(i, odd, s, JOIN)
                if there(m):
                    if t == 0:
                        dve.wait_ge(x_in[table], (turn_of + 1) * 16)
                    dve.wait_ge(back_in[t % NK], (m * (T // NK) + t // NK + 1) * 16)
                    nc.vector.tensor_tensor(total[table][:, t, :], total[table][:, t, :], back[t % NK][:], ALU.add
                                            ).then_inc(added, 1)
                if s == JOIN - SL and there(b):
                    set_rows(b, odd)

        set_slots(0, 0)
        rounds(dve, turn)

    @block.scalar
    def _(act):
        def slots(b):
            for s in range(SL):
                act.wait_ge(product, b * SL + s + 1)
                act.wait_ge(routed_out[s % NY], (b * (SL // NY) + s // NY) * 16)
                nc.scalar.activation(routed[s % NY][:], ps_out[s % NT4][:, 0:D], ACT.Identity,
                                     scale=g.slot_gate[:, bass.ds(b, 1), s:s + 1].rearrange("p a s -> p (a s)")).then_inc(scaled, 1)

        slots(0)
        with act.Fori(1, NB) as b:
            slots(b)

    @block.tensor
    def _(pe):
        def turn(b, s):
            pe.wait_ge(picked_in[s % NX], (b * (SL // NX) + s // NX + 1) * 16)
            pe.wait_ge(copied, count(b * SL + s - NT4 + 1))
            for k in range(KD):
                mm = nc.tensor.transpose(ps_turn[s % NT4][:, k * P:(k + 1) * P], picked[s % NX][:, k * P:(k + 1) * P], g.ident[:])
            mm.then_inc(turned, 1)

        def apply_expert(b, s):
            pe.wait_ge(copied, b * SL + s + 1)
            pe.wait_ge(scaled, count(b * SL + s - NT4 + 1))
            for k in range(KD):
                mm = nc.tensor.matmul(ps_out[s % NT4][:, 0:D], picked_t[s % NT4][:, k, :], expert[:, s // NH, k, :],
                                      start=(k == 0), stop=(k == KD - 1))
            mm.then_inc(product, 1)

        def slots(b):
            for s in range(SL + 1):
                if s < SL:
                    turn(b, s)
                if s:
                    apply_expert(b, s - 1)

        pe.wait_ge(expert_in, E * 16)
        slots(0)
        with pe.Fori(1, NB) as b:
            slots(b)


def program(nc, w, g):
    with ExitStack() as ctx:
        constants(nc, g, w, ctx)
        route(nc, g, w.x, "in")
        with ExitStack() as c1:
            mixer(nc, g, w.x, c1)
        route(nc, g, g.x2, "mid")
        with ExitStack() as c1:
            ffn(nc, g, g.x2, w.out, c1)


def kernel(L0_attn_x, L0_attn_W_in, L0_attn_conv_w, L0_attn_conv_b, L0_attn_A_log, L0_attn_D, L0_attn_W_out,
           L0_ffn_gate_w, L0_ffn_experts):
    import concourse.bacc as bacc
    from concourse.bass_utils import run_bass_kernel_spmd

    nc = bacc.Bacc("TRN2", target_bir_lowering=False, num_devices=1)
    arrays = {}

    def given(name, a):
        a = np.ascontiguousarray(a)
        arrays[name] = a
        return nc.dram_tensor(name, a.shape, mybir.dt.from_np(a.dtype), kind="ExternalInput").ap()

    w, g = Bag(), Bag()
    w.x = given("in_x", L0_attn_x)
    w.A_log = given("in_a_log", L0_attn_A_log)
    w.w_in_t = given("in_w_in_t", L0_attn_W_in.T)
    w.w_out_t = given("in_w_out_t", L0_attn_W_out.T)
    w.conv_w = given("in_conv_w", L0_attn_conv_w.reshape(INNER, KC))
    w.conv_b_t = given("in_conv_b_t", L0_attn_conv_b.reshape(J, P).T)
    w.skip_t = given("in_skip_t", L0_attn_D.reshape(J, P).T)
    w.gate_w = given("in_gate_w", L0_ffn_gate_w)
    g.experts = given("in_experts", L0_ffn_experts)
    w.out = nc.dram_tensor("out", (NB, NT, D), F32, kind="ExternalOutput").ap()
    g.normed = nc.dram_tensor("normed_rows", (NB * NT, D), F32).ap()
    g.routed = [nc.dram_tensor(f"routed_rows{i}", (YR, D), F32).ap() for i in range(2)]
    g.x1 = nc.dram_tensor("x1_rows", (NB * NT, D), F32).ap()
    g.x2 = nc.dram_tensor("x2_rows", (NB, NT, D), F32).ap()
    program(nc, w, g)
    r = run_bass_kernel_spmd(nc, [arrays], core_ids=[0])
    return r.results[0]["out"]
```

```python
from contextlib import ExitStack

import numpy as np

import concourse.bass as bass
from concourse import mybir

ALU = mybir.AluOpType
ACT = mybir.ActivationFunctionType
F32 = mybir.dt.float32
BF16 = mybir.dt.bfloat16
I32 = mybir.dt.int32
U32 = mybir.dt.uint32
AX = mybir.AxisListType

P = 128
NB = 8
NT = 2048
D = 256
KD = D // P
T = NT // P
E = 8
M = NT // E
NH = M // P
SL = E * NH
R = NB * E
YR = E * (M + 1)
ITERS = 8
INNER = 512
J = INNER // P
N = 16
KC = 4
CH = 512
C = NT // CH
LN_EPS = 1e-5
CLIP = 1e-6


class Bag:
    pass


def count(value):
    return max(value, 0) if isinstance(value, int) else value


def constants(nc, g, w, ctx):

    def sb(name, shape, dt=F32):
        return ctx.enter_context(nc.sbuf_tensor(name, shape, dt))

    g.ident = sb("ident", [P, P])
    g.ones = sb("ones", [P, P])
    g.iota_col = sb("iota_col", [P, P])
    g.rank_of = sb("rank_of", [P, NH])
    g.expert_of = sb("expert_of", [P, R])
    g.token_base = sb("token_base", [P, NB])
    g.gate_w = sb("gate_w", [P, KD, E])
    g.w_in = sb("w_in", [P, KD, 2 * INNER])
    g.w_out = sb("w_out", [P, J, D])
    g.conv_w = sb("conv_w", [P, J, KC])
    g.conv_b = sb("conv_b", [P, J])
    g.skip = sb("skip", [P, J])
    g.neg_a = sb("neg_a", [P, J, N])
    g.slot_token = sb("slot_token", [P, NB, SL], I32)
    g.slot_gate = sb("slot_gate", [P, NB, SL])
    g.token_row = sb("token_row", [P, NB, T], I32)

    g.passed_dve, g.passed_pool, g.passed_sp = (
        ctx.enter_context(nc.semaphore(n)) for n in ("passed_dve", "passed_pool", "passed_sp"))

    with ExitStack() as c2:
        zrow = c2.enter_context(nc.sbuf_tensor("zero_row", [E, D], F32))
        zeroed = c2.enter_context(nc.semaphore("zeroed"))
        loaded = ctx.enter_context(nc.semaphore("weights_loaded"))
        a_loaded = c2.enter_context(nc.semaphore("a_log_loaded"))
        a_exp = c2.enter_context(nc.semaphore("a_exp_done"))
        zero_stored = c2.enter_context(nc.semaphore("zero_rows_stored"))
        block = c2.enter_context(nc.Block())

        @block.gpsimd
        def _(pool):
            nc.gpsimd.memset(zrow[:], 0.0).then_inc(zeroed, 1)
            nc.gpsimd.memset(g.ident[:], 0.0).then_inc(zeroed, 1)
            nc.gpsimd.memset(g.ones[:], 1.0)
            pool.wait_ge(zeroed, 2)
            nc.gpsimd.affine_select(out=g.ident[:], in_=g.ident[:], compare_op=ALU.not_equal, fill=1.0,
                                    base=0, pattern=[[-1, P]], channel_multiplier=1)
            for out, pattern, base, mult in (
                (g.iota_col[:], [[1, P]], 0, 0),
                (g.rank_of[:], [[P, NH]], 1, 1),
                (g.expert_of[:], [[0, NB], [1, E]], 0, 0),
                (g.token_base[:], [[NT, NB]], 0, 0),
            ):
                nc.gpsimd.iota(out, pattern, base=base, channel_multiplier=mult,
                               allow_small_or_imprecise_dtypes=True)

        @block.sync
        def _(sp):
            sp.dma_start(g.neg_a[:], w.A_log.rearrange("(j p) n -> p j n", p=P)).then_inc(a_loaded, 16)
            sp.dma_start(g.gate_w[:], w.gate_w.rearrange("(k p) e -> p k e", p=P)).then_inc(loaded, 16)
            sp.dma_start(g.w_in[:], w.w_in_t.rearrange("(k p) c -> p k c", p=P)).then_inc(loaded, 16)
            sp.dma_start(g.w_out[:], w.w_out_t.rearrange("(j p) d -> p j d", p=P)).then_inc(loaded, 16)
            sp.dma_start(g.conv_w[:], w.conv_w.rearrange("(j p) k -> p j k", p=P)).then_inc(loaded, 16)
            sp.dma_start(g.conv_b[:], w.conv_b_t).then_inc(loaded, 16)
            sp.dma_start(g.skip[:], w.skip_t).then_inc(loaded, 16)
            sp.wait_ge(zeroed, 1)
            for table in g.routed:
                sp.dma_start(table[0:E, :], zrow[:]).then_inc(zero_stored, 16)
            sp.wait_ge(loaded, 6 * 16)
            sp.wait_ge(zero_stored, 2 * 16)

        @block.scalar
        def _(act):
            act.wait_ge(a_loaded, 16)
            flat = g.neg_a[:].rearrange("p j n -> p (j n)")
            nc.scalar.activation(flat, flat, ACT.Exp).then_inc(a_exp, 1)
            act.wait_ge(a_exp, 1)
            nc.scalar.mul(flat, flat, -1.0)


def route(nc, g, x, tag):
    x_in = x.rearrange("b (p t) d -> b p t d", t=T)
    xn_out = g.normed.rearrange("(b p t) d -> b p t d", p=P, t=T)
    with ExitStack() as ctx:
        def sb(name, shape, dt=F32):
            return ctx.enter_context(nc.sbuf_tensor(f"{name}_{tag}", shape, dt))

        def sem(name):
            return nc.alloc_semaphore(f"{name}_{tag}")

        held = nc.snapshot_sems()
        probs = sb("probs", [P, T, NB, E])
        with ExitStack() as c1:
            logits_stage(nc, g, x_in, xn_out, probs, tag, c1)
        with ExitStack() as c1:
            rows = sinkhorn_stage(nc, g, probs, tag, ctx, c1)
        with ExitStack() as c1:
            top_stage(nc, g, rows, tag, c1)
        nc.clear_and_free_semaphores(nc.allocated_since(held))
        nc.all_engine_barrier()


def logits_stage(nc, g, x_in, xn_out, probs, tag, ctx):
    def sb(name, shape, dt=F32):
        return ctx.enter_context(nc.sbuf_tensor(f"{name}_{tag}", shape, dt))

    def sem(name):
        return nc.alloc_semaphore(f"{name}_{tag}")

    U = 4
    NB4 = 4
    G2 = T // 2
    WHEN, LAG = 3, 2
    rows_ = [sb(f"rows{u}", [P, T, D]) for u in range(U)]
    stats = [sb(f"stats{u}", [P, T, 6]) for u in range(2)]
    moments = [sb(f"moments{u}", [P, T, 2]) for u in range(2)]
    std = [sb(f"std{u}", [P, T]) for u in range(2)]
    rstd = [sb(f"rstd{u}", [P, T]) for u in range(2)]
    shift = [sb(f"shift{u}", [P, T]) for u in range(2)]
    eps = sb("eps", [P, 1])
    turned = [sb(f"turned{i}", [P, 2, KD, P]) for i in range(NB4)]
    ps_turn = [ctx.enter_context(nc.psum_tensor(f"ps_turn{i}_{tag}", [P, CH], F32)) for i in range(NB4)]
    ps_logit = [ctx.enter_context(nc.psum_tensor(f"ps_logit{u}_{tag}", [P, CH], F32)) for u in range(2)]

    def turns(eng, turn):
        turn(0)
        with eng.Fori(1, NB // U) as it:
            turn(it)

    row_in = [sem(f"row_in{u}") for u in range(U)]
    row_out = [sem(f"row_out{u}") for u in range(U)]
    eps_set, stats_done, moments_done, std_done, rstd_done, shift_done = (
        sem(n) for n in ("eps_set", "stats_done", "moments_done", "std_done", "rstd_done", "shift_done"))
    normed, turns_done, logits_done, probs_done = (
        sem(n) for n in ("normed", "turns_done", "logits_done", "probs_done"))
    turned_copied = [sem(n) for n in ("even_copied", "odd_copied")]
    block = ctx.enter_context(nc.Block())

    @block.sync
    def _(sp):
        def load(b, u):
            sp.dma_start(rows_[u][:], x_in[bass.ds(b, 1)].rearrange("a p t d -> p (a t) d")).then_inc(row_in[u], 16)

        def store(b, u):
            sp.wait_ge(normed, (b + 1) * T)
            sp.dma_start(xn_out[bass.ds(b, 1)].rearrange("a p t d -> p (a t) d"), rows_[u][:]
                         ).then_inc(row_out[u], 16)

        def load_over(b, u, turn):
            sp.wait_ge(row_out[u], turn * 16)
            sp.sem_inc(g.passed_sp, 1)
            sp.wait_ge(logits_done, (b - U + 1) * G2)
            load(b, u)

        for u in range(U):
            load(u, u)
        with sp.Fori(1, NB // U) as it:
            for u in range(U):
                store((it - 1) * U + u, u)
                if u:
                    load_over(it * U + u - 1, u - 1, it)
            load_over(it * U + U - 1, U - 1, it)
        for u in range(U):
            store(NB - U + u, u)
        for u in range(U):
            sp.wait_ge(row_out[u], 16 * NB // U)

    @block.vector
    def _(dve):
        def copy(b, i):
            dve.wait_ge(turns_done, b * G2 + i + 1)
            dve.wait_ge(logits_done, count(b * G2 + i - NB4 + 1))
            nc.vector.tensor_copy(turned[i % NB4][:].rearrange("p t k n -> p (t k n)"),
                                  ps_turn[i % NB4][:]).then_inc(turned_copied[0], 1)

        def clip(b, i):
            dve.wait_ge(logits_done, (b + 1) * G2)
            nc.vector.tensor_scalar(
                probs[:, :, bass.ds(b, 1), :].rearrange("p t a e -> p t (a e)"),
                ps_logit[i][:, 0:T * E].rearrange("p (t e) -> p t e", e=E),
                CLIP, None, ALU.max).then_inc(probs_done, 1)

        def turn(it):
            for u in range(U):
                b, i = it * U + u, u % 2
                first = isinstance(b, int) and b == 0
                for t in range(T):
                    if t == 0:
                        dve.wait_ge(row_in[u], (it + 1) * 16)
                    nc.vector.bn_stats(stats[i][:, t, :], rows_[u][:, t, :]).then_inc(stats_done, 1)
                    if not first and t % 4 == WHEN:
                        copy(b - 1, t // 4 * 2)
                dve.wait_ge(stats_done, (b + 1) * T)
                dve.sem_inc(g.passed_dve, 1)
                for t in range(T):
                    nc.vector.bn_aggr(moments[i][:, t, :], stats[i][:, t, :]).then_inc(moments_done, 1)
                dve.wait_ge(std_done, b + 1)
                nc.vector.reciprocal(rstd[i][:], std[i][:]).then_inc(rstd_done, 1)
                dve.wait_ge(rstd_done, b + 1)
                nc.vector.scalar_tensor_tensor(shift[i][:], moments[i][:, :, 0], -1.0, rstd[i][:],
                                               ALU.mult, ALU.mult).then_inc(shift_done, 1)
                if not first:
                    clip(b - 1, 1 - i)

        nc.vector.memset(eps[:], LN_EPS).then_inc(eps_set, 1)
        turns(dve, turn)
        for i in range(0, G2, 2):
            copy(NB - 1, i)
        clip(NB - 1, (NB - 1) % 2)

    @block.scalar
    def _(act):
        def copy(b, i):
            act.wait_ge(turns_done, b * G2 + i + 1)
            act.wait_ge(logits_done, count(b * G2 + i - NB4 + 1))
            nc.scalar.copy(turned[i % NB4][:].rearrange("p t k n -> p (t k n)"),
                           ps_turn[i % NB4][:]).then_inc(turned_copied[1], 1)

        def turn(it):
            for u in range(U):
                b, i = it * U + u, u % 2
                act.wait_ge(moments_done, (b + 1) * T)
                nc.scalar.activation(std[i][:], moments[i][:, :, 1], ACT.Sqrt, bias=eps[:, 0:1]
                                     ).then_inc(std_done, 1)
                act.wait_ge(shift_done, b + 1)
                for t in range(T):
                    nc.scalar.activation(rows_[u][:, t, :], rows_[u][:, t, :], ACT.Identity,
                                         bias=shift[i][:, t:t + 1], scale=rstd[i][:, t:t + 1]
                                         ).then_inc(normed, 1)
                    if t % 4 == 2 and t > 4:
                        copy(b, t // 4 * 2 - 1)
                copy(b, G2 - 1)

        act.wait_ge(eps_set, 1)
        turns(act, turn)

    @block.tensor
    def _(pe):
        def transpose(b, u, i):
            pe.wait_ge(normed, b * T + 2 * i + 2)
            pe.wait_ge(turned_copied[i % 2], count(b * (G2 // 2) + i // 2 - NB4 // 2 + 1))
            for t in (2 * i, 2 * i + 1):
                for k in range(KD):
                    c = (t % 2) * KD + k
                    mm = nc.tensor.transpose(ps_turn[i % NB4][:, c * P:(c + 1) * P],
                                             rows_[u][:, t, k * P:(k + 1) * P], g.ident[:])
            mm.then_inc(turns_done, 1)

        def logit(b, u, i):
            pe.wait_ge(turned_copied[i % 2], b * (G2 // 2) + i // 2 + 1)
            if i == 0:
                pe.wait_ge(probs_done, count(b - 1))
            for t in (2 * i, 2 * i + 1):
                for k in range(KD):
                    mm = nc.tensor.matmul(ps_logit[u % 2][:, t * E:(t + 1) * E], turned[i % NB4][:, t % 2, k, :],
                                          g.gate_w[:, k, :], start=(k == 0), stop=(k == KD - 1))
            mm.then_inc(logits_done, 1)

        def turn(it):
            for u in range(U):
                b = it * U + u
                for i in range(G2 + LAG):
                    if i < G2:
                        transpose(b, u, i)
                    if i >= LAG:
                        logit(b, u, i - LAG)

        turns(pe, turn)


def sinkhorn_stage(nc, g, probs, tag, outer, ctx):
    def sb(name, shape, dt=F32, c=ctx):
        return c.enter_context(nc.sbuf_tensor(f"{name}_{tag}", shape, dt))

    def sem(name):
        return nc.alloc_semaphore(f"{name}_{tag}")

    rows = sb("gate_rows", [P, NT // 2], c=outer)
    second = sb("second_halves", [R, NT // 2])
    HP = P // 2
    r = sb("token_scale", [P, T * NB])
    c_ = sb("expert_scale", [P, R])
    token_sum = sb("token_sum", [P, T * NB])
    tile_sum = sb("tile_sum", [P, R])
    tile_sums_done = sem("tile_sums")
    scaled = sb("scaled", [P, T * NB, E])
    weighted = sb("weighted", [P, T, R])
    ps_sum = ctx.enter_context(nc.psum_tensor(f"ps_sum_{tag}", [P, CH], F32))
    ps_rows = [ctx.enter_context(nc.psum_tensor(f"ps_rows{i}_{tag}", [P, CH], F32)) for i in range(4)]
    weighted_done, sums_done, c_done, scaled_done, token_sums_done, r_done, gates_done, turned, copied, half_moved = (
        sem(n) for n in ("weighted", "expert_sums", "expert_scale", "scaled", "token_sums", "token_scale",
                         "gates", "gates_turned", "gates_copied", "half_moved"))
    block = ctx.enter_context(nc.Block())
    flat = probs[:].rearrange("p t b e -> p (t b) e")

    @block.vector
    def _(dve):
        nc.vector.memset(r[:], 1.0).then_inc(r_done, 1)
        for i in range(ITERS):
            dve.wait_ge(r_done, i + 1)
            nc.vector.tensor_tensor(weighted[:].rearrange("p t (b e) -> p (t b) e", e=E), flat,
                                    r[:].unsqueeze(2).to_broadcast([P, T * NB, E]), ALU.mult
                                    ).then_inc(weighted_done, 1)
            dve.wait_ge(weighted_done, i + 1)
            nc.vector.tensor_reduce(tile_sum[:], weighted[:].rearrange("p t r -> p r t"), AX.X, ALU.add
                                    ).then_inc(tile_sums_done, 1)
            dve.wait_ge(sums_done, i + 1)
            nc.vector.reciprocal(c_[:], ps_sum[:, 0:R]).then_inc(c_done, 1)
            dve.wait_ge(c_done, i + 1)
            nc.vector.tensor_tensor(scaled[:].rearrange("p (t b) e -> p t (b e)", b=NB),
                                    probs[:].rearrange("p t b e -> p t (b e)"),
                                    c_[:].unsqueeze(1).to_broadcast([P, T, R]), ALU.mult
                                    ).then_inc(scaled_done, 1)
            dve.wait_ge(scaled_done, i + 1)
            nc.vector.tensor_reduce(token_sum[:], scaled[:], AX.X, ALU.add).then_inc(token_sums_done, 1)
            dve.wait_ge(token_sums_done, i + 1)
            nc.vector.reciprocal(r[:], token_sum[:]).then_inc(r_done, 1)
        dve.wait_ge(r_done, ITERS + 1)
        nc.vector.tensor_tensor(weighted[:].rearrange("p t (b e) -> p (t b) e", e=E), scaled[:],
                                r[:].unsqueeze(2).to_broadcast([P, T * NB, E]), ALU.mult
                                ).then_inc(gates_done, 1)
        for i in range(4):
            dve.wait_ge(turned, 4 * (i + 1))
            for h, half in ((1, second), (0, rows)):
                nc.vector.tensor_copy(half[0:R, :].rearrange("r (p t) -> r t p", t=T)[:, 4 * i:4 * i + 4, :],
                                      ps_rows[i][0:R, :].rearrange("r (t p) -> r t p", p=P)[:, :, h * HP:(h + 1) * HP]
                                      ).then_inc(copied, 1)

    @block.sync
    def _(sp):
        sp.wait_ge(copied, 8)
        sp.dma_start(rows[R:P, :], second[:]).then_inc(half_moved, 16)
        sp.wait_ge(half_moved, 16)

    @block.tensor
    def _(pe):
        for i in range(ITERS):
            pe.wait_ge(tile_sums_done, i + 1)
            if i:
                pe.wait_ge(c_done, i)
            nc.tensor.matmul(ps_sum[:, 0:R], g.ones[:], tile_sum[:], start=True, stop=True).then_inc(sums_done, 1)
        pe.wait_ge(gates_done, 1)
        for t in range(T):
            nc.tensor.transpose(ps_rows[t // 4][0:R, (t % 4) * P:(t % 4 + 1) * P], weighted[:, t, :],
                                g.ident[:]).then_inc(turned, 1)
    return rows


def top_stage(nc, g, rows, tag, ctx):
    def sb(name, shape, dt=F32):
        return ctx.enter_context(nc.sbuf_tensor(f"{name}_{tag}", shape, dt))

    def sem(name):
        return nc.alloc_semaphore(f"{name}_{tag}")

    vals = sb("top_vals", [P, M])
    idx = sb("top_idx", [P, M], U32)
    idx_f = sb("top_idx_f", [P, M])
    half_t = [[sb(f"half_t{q}_{h}", [P, P]) for h in range(NH)] for q in range(2)]
    mirror = sb("mirror", [P, P])
    mirror_made = sem("mirror_made")
    ps_half = ctx.enter_context(nc.psum_tensor(f"ps_half_{tag}", [P, 2 * NH * P], F32))
    merged_v = [sb(f"merged_v{i}", [R, M]) for i in range(2)]
    merged_i = [sb(f"merged_i{i}", [R, M]) for i in range(2)]
    above, equal, swap, gap = (sb(n, [R, M]) for n in ("above", "equal", "swap", "gap"))
    half_turned, half_copied, mirrored, merge_step = (
        sem(n) for n in ("half_turned", "half_copied", "mirrored", "merge_step"))
    token_f = sb("token_f", [P, R, NH])
    token_i = sb("token_i", [P, R * NH], I32)
    part_i = sb("part_i", [P, R * NH], I32)
    tile_i = sb("tile_i", [P, R * NH], I32)
    part_f = sb("part_f", [P, R * NH])
    tile_f = sb("tile_f", [P, R * NH])
    at_tile = sb("at_tile", [P, R * NH, T], BF16)
    NU, GQ = 3, 8
    at_part = [sb(f"at_part{i}", [P, GQ, P], BF16) for i in range(NU)]
    key = sb("key", [P, R, T])
    won = sb("won", [P, NB, T])
    ps_rank = ctx.enter_context(nc.psum_tensor(f"ps_rank_{tag}", [P, R * T], F32))
    ps_t = ctx.enter_context(nc.psum_tensor(f"ps_t_{tag}", [P, CH], F32))
    ps_v = ctx.enter_context(nc.psum_tensor(f"ps_v_{tag}", [P, CH], F32))
    maxed, indexed, replaced, idx_conv, moved, tok_copied, chain, gate_copied = (
        sem(n) for n in ("maxed", "indexed", "replaced", "idx_converted", "slots_turned",
                         "tokens_copied", "index_step", "gates_copied2"))
    part_built, part_used, merged = sem("part_built"), sem("part_used"), sem("merged")
    ps_mirror = ctx.enter_context(nc.psum_tensor(f"ps_mirror_{tag}", [P, 2 * M], F32))
    FINAL = (M.bit_length() - 1) % 2
    block = ctx.enter_context(nc.Block())

    @block.gpsimd
    def _(pool):
        nc.gpsimd.memset(mirror[:], 0.0).then_inc(mirror_made, 1)
        pool.wait_ge(mirror_made, 1)
        nc.gpsimd.affine_select(out=mirror[:], in_=mirror[:], compare_op=ALU.not_equal, fill=1.0,
                                base=1 - P, pattern=[[1, P]], channel_multiplier=1).then_inc(mirror_made, 1)

    @block.vector
    def _(dve):
        for k in range(M // 8):
            s = slice(8 * k, 8 * k + 8)
            if k:
                dve.wait_ge(replaced, k)
            nc.vector.max(vals[:, s], rows[:]).then_inc(maxed, 1)
            dve.wait_ge(maxed, k + 1)
            nc.vector.max_index(idx[:, s], vals[:, s], rows[:]).then_inc(indexed, 1)
            if k + 1 < M // 8:
                dve.wait_ge(indexed, k + 1)
                nc.vector.match_replace(rows[:], vals[:, s], rows[:], -1.0).then_inc(replaced, 1)
        dve.wait_ge(indexed, M // 8)
        nc.vector.tensor_copy(idx_f[:], idx[:]).then_inc(idx_conv, 1)
        for q in range(2):
            for h in range(NH):
                dve.wait_ge(half_turned, 2 * NH)
                nc.vector.tensor_copy(half_t[q][h][:], ps_half[:, (q * NH + h) * P:(q * NH + h + 1) * P]).then_inc(half_copied, 1)

        n_merge = [0]

        def merge(*steps):
            for ins in steps:
                ins.then_inc(merge_step, 1)
            n_merge[0] += len(steps)
            dve.wait_ge(merge_step, n_merge[0])

        def exchange(xv, xi, yv, yi, high, low, shape):
            ab, eq, sw, gp = (shape(buf) for buf in (above, equal, swap, gap))
            steps = [nc.vector.tensor_tensor(ab, yv, xv, ALU.is_gt), nc.vector.tensor_tensor(eq, yv, xv, ALU.is_equal),
                     nc.vector.tensor_tensor(gp, yi, xi, ALU.subtract),
                     nc.vector.tensor_tensor(high[0], xv, yv, ALU.max)]
            if low:
                steps.append(nc.vector.tensor_tensor(low[0], xv, yv, ALU.min))
            merge(*steps)
            merge(nc.vector.scalar_tensor_tensor(sw, gp, 0.0, eq, ALU.is_lt, ALU.mult))
            merge(nc.vector.tensor_tensor(sw, sw, ab, ALU.add))
            merge(nc.vector.tensor_tensor(gp, gp, sw, ALU.mult))
            steps = [nc.vector.tensor_tensor(high[1], xi, gp, ALU.add)]
            if low:
                steps.append(nc.vector.tensor_tensor(low[1], yi, gp, ALU.subtract))
            merge(*steps)

        dve.wait_ge(mirrored, 1)
        merge(nc.vector.tensor_scalar(merged_i[1][:], ps_mirror[0:R, M:2 * M], float(NT // 2), None, ALU.add))
        dve.wait_ge(idx_conv, 1)
        exchange(vals[0:R, :], idx_f[0:R, :], ps_mirror[0:R, 0:M], merged_i[1][:],
                 (merged_v[0][:], merged_i[0][:]), None, lambda buf: buf[:])
        now, d = 0, M // 2
        while d:
            def pairs(buf, k):
                return buf[:].rearrange("r (a k d) -> r a k d", k=2, d=d)[:, :, k, :]

            v, i, v2, i2 = merged_v[now], merged_i[now], merged_v[1 - now], merged_i[1 - now]
            exchange(pairs(v, 0), pairs(i, 0), pairs(v, 1), pairs(i, 1), (pairs(v2, 0), pairs(i2, 0)),
                     (pairs(v2, 1), pairs(i2, 1)), lambda buf: pairs(buf, 0))
            now, d = 1 - now, d // 2
        assert now == FINAL
        dve.sem_inc(merged, 1)
        dve.wait_ge(moved, 1)
        nc.vector.tensor_copy(token_f[:], ps_t[:, 0:R * NH].rearrange("p (h r) -> p r h", h=NH)
                              ).then_inc(tok_copied, 1)
        n_chain = [0]

        def step(ins):
            n_chain[0] += 1
            ins.then_inc(chain, 1)
            dve.wait_ge(chain, n_chain[0])

        dve.wait_ge(tok_copied, 1)
        flat = token_f[:].rearrange("p r h -> p (r h)")
        step(nc.vector.tensor_copy(token_i[:], flat))
        step(nc.vector.tensor_scalar(part_i[:], token_i[:], 4, None, ALU.logical_shift_right))
        step(nc.vector.tensor_scalar(tile_i[:], token_i[:], T - 1, None, ALU.bitwise_and))
        step(nc.vector.tensor_copy(part_f[:], part_i[:]))
        step(nc.vector.tensor_copy(tile_f[:], tile_i[:]))
        nc.vector.tensor_tensor(g.slot_token[:], token_f[:].rearrange("p (b e) h -> p b (e h)", b=NB),
                                g.token_base[:].unsqueeze(2).to_broadcast([P, NB, SL]), ALU.add)
        step(nc.vector.tensor_tensor(at_tile[:], tile_f[:].unsqueeze(2).to_broadcast([P, R * NH, T]),
                                     g.iota_col[:, 0:T].unsqueeze(1).to_broadcast([P, R * NH, T]),
                                     ALU.is_equal))
        step(nc.vector.tensor_tensor(at_tile[:].rearrange("p (r h) t -> p r h t", h=NH),
                                     at_tile[:].rearrange("p (r h) t -> p r h t", h=NH),
                                     g.rank_of[:].unsqueeze(1).unsqueeze(3).to_broadcast([P, R, NH, T]), ALU.mult))
        for i in range(R * NH // GQ):
            if i >= NU:
                dve.wait_ge(part_used, (i - NU + 1) * GQ)
            nc.vector.tensor_tensor(at_part[i % NU][:], part_f[:, i * GQ:(i + 1) * GQ].unsqueeze(2).to_broadcast([P, GQ, P]),
                                    g.iota_col[:].unsqueeze(1).to_broadcast([P, GQ, P]), ALU.is_equal
                                    ).then_inc(part_built, 1)
        dve.wait_ge(part_used, R * NH)
        ranks = ps_rank[:].rearrange("p (r t) -> p r t", t=T)
        step(nc.vector.scalar_tensor_tensor(key[:], ranks, float(E),
                                            g.expert_of[:].unsqueeze(2).to_broadcast([P, R, T]),
                                            ALU.mult, ALU.add))
        step(nc.vector.scalar_tensor_tensor(key[:], ranks, 0.0, key[:], ALU.is_gt, ALU.mult))
        step(nc.vector.tensor_reduce(won[:], key[:].rearrange("p (b e) t -> p b t e", e=E), AX.X, ALU.max))
        nc.vector.tensor_copy(g.token_row[:], won[:])

    @block.scalar
    def _(act):
        act.wait_ge(moved, 2)
        nc.scalar.mul(g.slot_gate[:].rearrange("p b (e h) -> p (b e) h", h=NH),
                      ps_v[:, 0:R * NH].rearrange("p (h r) -> p r h", h=NH), 0.5).then_inc(gate_copied, 1)

    @block.tensor
    def _(pe):
        pe.wait_ge(mirror_made, 2)
        pe.wait_ge(idx_conv, 1)
        for q, src in enumerate((vals, idx_f)):
            for h in range(NH):
                nc.tensor.transpose(ps_half[:, (q * NH + h) * P:(q * NH + h + 1) * P], src[:, h * P:(h + 1) * P], g.ident[:]).then_inc(half_turned, 1)
        for q in range(2):
            for h in range(NH):
                pe.wait_ge(half_copied, q * NH + h + 1)
                first = q * M + (NH - 1 - h) * P
                mm = nc.tensor.matmul(ps_mirror[0:R, first:first + P], half_t[q][h][:, R:P], mirror[:],
                                      start=True, stop=True)
        mm.then_inc(mirrored, 1)
        pe.wait_ge(merged, 1)
        for src, dst in ((merged_i[FINAL], ps_t), (merged_v[FINAL], ps_v)):
            for h in range(NH):
                mm = nc.tensor.transpose(dst[:, h * R:(h + 1) * R], src[:, h * P:(h + 1) * P],
                                         g.ident[0:R, 0:R])
            mm.then_inc(moved, 1)
        for q in range(R * NH):
            row = q // NH
            pe.wait_ge(part_built, q // GQ + 1)
            nc.tensor.matmul(ps_rank[:, row * T:(row + 1) * T], at_part[q // GQ % NU][:, q % GQ, :], at_tile[:, q, :],
                             start=(q % NH == 0), stop=(q % NH == NH - 1)).then_inc(part_used, 1)


def mixer(nc, g, x, ctx):
    def sb(name, shape, dt=F32):
        return ctx.enter_context(nc.sbuf_tensor(name, shape, dt))

    def sem(name):
        return ctx.enter_context(nc.semaphore(name))

    def ps(name):
        return ctx.enter_context(nc.psum_tensor(name, [P, CH], F32))

    NS, NX, NY, NK, NRES = 6, 3, 2, 4, 4
    LEAD = NS
    FFN = 6
    BACK = 22
    ADD = BACK + NK
    SCALES = ADD + T + 1
    TURN = SCALES + 5
    OUT = 5
    SQUARE = 9
    STEP = 3
    RES = 43
    state = [sb(f"state{i}", [P, NT]) for i in range(NS)]
    conv_in = sb("conv_in", [P, KC - 1 + NT])
    xc = [sb(f"xc{i}", [P, NT]) for i in range(J)]
    res = [sb(f"res{i}", [P, NT]) for i in range(2)]
    delta = [sb(f"delta{i}", [P, NT]) for i in range(2)]
    drive = [sb(f"drive{i}", [P, NT]) for i in range(2)]
    x1 = sb("x1", [P, T, D])
    x1t = sb("x1t", [P, KD, NT])
    resid = [sb(f"resid{i}", [P, 2, D]) for i in range(NRES)]
    picked = [sb(f"picked{i}", [P, D]) for i in range(NX)]
    picked_t = [sb(f"picked_t{i}", [P, KD, P]) for i in range(2)]
    routed = [sb(f"routed{i}", [P, D]) for i in range(NY)]
    back = [sb(f"back{i}", [P, D]) for i in range(NK)]
    expert = [sb(f"expert{i}", [P, KD, D]) for i in range(2)]
    slot_now = sb("slot_now", [P, SL], I32)
    gate_now = sb("gate_now", [P, SL])
    row_now = sb("row_now", [P, T], I32)
    stats = sb("m_stats", [P, T, 6])
    moments = sb("m_moments", [P, T, 2])
    rstd = sb("m_rstd", [P, T])
    shift = sb("m_shift", [P, T])
    eps = sb("m_eps", [P, 1])
    ps_sum = [ps(f"ps_states{c}") for c in range(C)]
    ps_proj = [ps(f"ps_proj{i}") for i in range(2)]
    def out_bank(r, last):
        return ps_rows[1 - r % 2 if last else 1]

    ps_rows = [ps(f"ps_rows{i}") for i in range(2)]

    decay_ready = sem("decay_ready")
    state_ready = sem("state_ready")
    pair_added, pair_used = sem("pair_added"), sem("pair_used")
    setup = sem("m_setup")
    ssm_done, ssm_copied, conv_step, conv_done = (sem(n) for n in ("ssm_done", "ssm_copied", "conv_step", "conv_done"))
    res_done, res_copied, res_gated, xc_done, soft_step, soft_done, drive_done, delta_done = (
        sem(n) for n in ("res_done", "res_copied", "res_gated", "xc_done", "soft_step", "soft_done", "drive_done", "delta_done"))
    gated, y_done, out_done, out_added = (sem(n) for n in ("gated", "y_done", "out_done", "out_added"))
    now_set = sem("now_set")
    picked_in = [sem(f"picked_in{i}") for i in range(NX)]
    pick_turned, pick_copied, expert_done, routed_scaled = (
        sem(n) for n in ("pick_turned", "pick_copied", "expert_done", "routed_scaled"))
    expert_in = [sem(f"expert_in{i}") for i in range(2)]
    routed_out = [sem(f"routed_out{i}") for i in range(NY)]
    back_in = [sem(f"back_in{i}") for i in range(NK)]
    x_in, x1_added = sem("m_x_in"), sem("x1_added")
    x1_stored = [sem(f"x1_stored{i}") for i in range(2)]
    stats_done, moments_done, log_done, rstd_done, shift_done, normed, x1_turned, x1t_copied = (
        sem(n) for n in ("m_stats_done", "m_moments_done", "m_log_var_done", "m_rstd_done", "m_shift_done",
                         "m_normed", "x1_turned", "x1t_copied"))
    resid_in = [sem(f"resid_in{i}") for i in range(NRES)]
    x2_out = [sem(f"x2_out{i}") for i in range(NRES)]

    x_v = x.rearrange("b (p t) d -> b p t d", t=T)
    x1_v = g.x1.rearrange("(b p t) d -> b p t d", p=P, t=T)
    x2_v = g.x2.rearrange("b (p t) d -> b p t d", t=T)
    routed_v = g.routed[0].rearrange("(m e) d -> e m d", e=E)
    G2 = T // 2

    TH = T // 2
    x1_half = [x1[:, i * TH:(i + 1) * TH, :].rearrange("p t d -> p (t d)") for i in range(2)]
    xc_now = [x1_half[1], xc[3][:], xc[2][:], xc[3][:]]
    y_now = [xc[0][:], xc[1][:], xc[2][:], x1_half[0]]

    def projections(b, q, last):
        j, n = q // N, q % N
        if j in (1, 2) and 2 <= n < 2 + C:
            return "ssm", b, j + 1, n - 2
        if j in (1, 2) and 2 + C <= n < 2 + 2 * C:
            return "res", b, j, n - 2 - C
        if RES <= q < RES + C:
            return "res", b, J - 1, q - RES
        first = TURN + 4
        if not last and first <= q < first + 3 * C:
            branch, unit = (("ssm", 0), ("res", 0), ("ssm", 1))[(q - first) // C]
            return branch, b + 1, unit, (q - first) % C
        return None

    def silu_at(j):
        return 11 if j == J - 1 else 10

    def conv_at(j):
        return TURN - (J - 1) * N + 5 if j == J - 1 else 4


    def batches(eng, body):
        body(0, True, False)
        with eng.Fori(1, NB - 1) as b:
            body(b, False, False)
        body(NB - 1, False, True)

    block = ctx.enter_context(nc.Block())

    @block.sync
    def _(sp):
        def load_expert(nb, e):
            sp.wait_ge(expert_done, count(nb * SL + (e - 2) * NH + NH if e >= 2 else nb * SL))
            sp.dma_start(expert[e % 2][:], g.experts[e].rearrange("(k p) f -> p k f", p=P)
                         ).then_inc(expert_in[e % 2], 16)

        def load_x(nb):
            sp.dma_start(x1[:], x_v[bass.ds(nb, 1)].rearrange("a p t d -> p (a t) d")).then_inc(x_in, 16)

        def store_slots(nb, s):
            e, h = s // NH, s % NH
            sp.wait_ge(routed_scaled, nb * SL + s + 1)
            sp.dma_start(routed_v[e, 1 + h * P:1 + (h + 1) * P, :],
                         routed[s % NY][:]).then_inc(routed_out[s % NY], 16)
            if h == NH - 1 and e + 2 < E:
                load_expert(nb, e + 2)

        def store_x1(nb):
            for i in range(2):
                sp.wait_ge(x1_added, nb * T + (i + 1) * TH)
                sp.dma_start(x1_v[bass.ds(nb, 1), :, i * TH:(i + 1) * TH, :].rearrange("a p t d -> p (a t) d"),
                             x1[:, i * TH:(i + 1) * TH, :]).then_inc(x1_stored[i], 16)

        def load_resid(b, r):
            sp.dma_start(resid[r % NRES][:], x1_v[bass.ds(b, 1), :, 2 * r:2 * r + 2, :].rearrange("a p t d -> p (a t) d")
                         ).then_inc(resid_in[r % NRES], 16)

        def load_resids(b):
            for i in range(2):
                sp.wait_ge(x1_stored[i], (b + 1) * 16)
                sp.sem_inc(g.passed_sp, 1)
            for r in range(NRES):
                sp.wait_ge(x2_out[r], b * 16 * (G2 // NRES))
                load_resid(b, r)

        def store_result(b, r):
            sp.wait_ge(out_added, b * G2 + r + 1)
            sp.dma_start(x2_v[bass.ds(b, 1), :, 2 * r:2 * r + 2, :].rearrange("a p t d -> p (a t) d"), resid[r % NRES][:]
                         ).then_inc(x2_out[r % NRES], 16)
            if r >= 1 and r + NRES - 1 < G2:
                sp.wait_ge(x2_out[(r - 1) % NRES], (b * (G2 // NRES) + (r - 1) // NRES + 1) * 16)
                load_resid(b, r + NRES - 1)

        def body(b, first, last):
            if not last:
                for i in range(NK):
                    sp.wait_ge(back_in[i], (b + 1) * 16 * (T // NK))
                    sp.sem_inc(g.passed_sp, 1)
                load_expert(b + 1, 0)
                load_expert(b + 1, 1)
            for s in range(SL):
                if not first and s % 2:
                    store_result(b - 1, s // 2)
                if last:
                    continue
                if s == SL - 1:
                    sp.wait_ge(x1_turned, (b + 1) * G2)
                    sp.sem_inc(g.passed_sp, 1)
                    sp.wait_ge(y_done, b * J + 1)
                    sp.sem_inc(g.passed_sp, 1)
                    sp.wait_ge(out_done, count(b * G2))
                    sp.sem_inc(g.passed_sp, 1)
                    load_x(b + 1)
                store_slots(b + 1, s)
            if not last:
                store_x1(b + 1)
            load_resids(b)

        load_expert(0, 0)
        load_expert(0, 1)
        for s in range(SL):
            store_slots(0, s)
            if s == SL - 4:
                load_x(0)
        store_x1(0)
        batches(sp, body)
        for r in range(G2):
            store_result(NB - 1, r)
        for r in range(NRES):
            sp.wait_ge(x2_out[r], NB * 16 * (G2 // NRES))

    @block.gpsimd
    def _(pool):
        def pick(nb, s):
            if s == 0:
                pool.wait_ge(now_set, (nb + 1) * 3)
            pool.wait_ge(pick_turned, nb * SL + (s - NX + 1 if s >= NX else 0))
            pool.sem_inc(g.passed_pool, 1)
            nc.gpsimd.indirect_dma_start(
                out=picked[s % NX][:], out_offset=None, in_=g.normed,
                in_offset=bass.IndirectOffsetOnAxis(ap=slot_now[:, s:s + 1].bitcast(U32), axis=0)
            ).then_inc(picked_in[s % NX], 16)

        def bring_back(nb, t):
            if t == 0:
                for i in range(NY):
                    pool.wait_ge(routed_out[i], (nb + 1) * 16 * (SL // NY))
            pool.wait_ge(x1_added, nb * T + (t - NK + 1 if t >= NK else 0))
            pool.sem_inc(g.passed_pool, 1)
            nc.gpsimd.indirect_dma_start(
                out=back[t % NK][:], out_offset=None, in_=g.routed[0],
                in_offset=bass.IndirectOffsetOnAxis(ap=row_now[:, t:t + 1].bitcast(U32), axis=0)
            ).then_inc(back_in[t % NK], 16)

        def square(b, j):
            u = b * J + j
            pool.wait_ge(xc_done, u + 1)
            pool.wait_ge(state_ready, count((u - 1) * N))
            nc.gpsimd.tensor_tensor(drive[j % 2][:], xc_now[j], xc_now[j], ALU.mult).then_inc(drive_done, 1)

        def body(b, first, last):
            if not last:
                for s in range(NX):
                    pick(b + 1, s)
            for q in range(1, J * N, 2):
                pool.wait_ge(state_ready, b * J * N + q + 1)
                nc.gpsimd.tensor_tensor(state[q % NS][:], state[q % NS - 1][:], state[q % NS][:], ALU.add
                                        ).then_inc(pair_added, 1)
                if q % N == SQUARE and q < (J - 1) * N:
                    square(b, q // N + 1)
                elif q % N == SQUARE and not last:
                    square(b + 1, 0)
                if last:
                    continue
                for v in (q, q + 1):
                    if NX <= v - 1 < SL:
                        pick(b + 1, v - 1)
                    if BACK <= v < BACK + T:
                        bring_back(b + 1, v - BACK)

        for s in range(SL):
            pick(0, s)
        for t in range(T):
            bring_back(0, t)
        square(0, 0)
        batches(pool, body)

    @block.vector
    def _(dve):
        def set_now(nb):
            for i in range(NK):
                dve.wait_ge(back_in[i], nb * 16 * (T // NK))
            nc.vector.tensor_copy(slot_now[:], g.slot_token[:, bass.ds(nb, 1), :].rearrange("p a s -> p (a s)")).then_inc(now_set, 1)
            dve.wait_ge(routed_scaled, nb * SL)
            nc.vector.tensor_copy(gate_now[:], g.slot_gate[:, bass.ds(nb, 1), :].rearrange("p a s -> p (a s)")).then_inc(now_set, 1)
            nc.vector.tensor_copy(row_now[:], g.token_row[:, bass.ds(nb, 1), :].rearrange("p a s -> p (a s)")).then_inc(now_set, 1)

        def add_routed(nb, t):
            if t == 0:
                dve.wait_ge(x_in, (nb + 1) * 16)
            dve.wait_ge(back_in[t % NK], (nb * (T // NK) + t // NK + 1) * 16)
            nc.vector.tensor_tensor(x1[:, t, :], x1[:, t, :], back[t % NK][:], ALU.add).then_inc(x1_added, 1)
            dve.wait_ge(x1_added, nb * T + t + 1)
            nc.vector.bn_stats(stats[:, t, :], x1[:, t, :]).then_inc(stats_done, 1)

        def aggregate(nb):
            dve.wait_ge(stats_done, (nb + 1) * T)
            dve.sem_inc(g.passed_dve, 1)
            for t in range(T):
                nc.vector.bn_aggr(moments[:, t, :], stats[:, t, :]).then_inc(moments_done, 1)

        def scales(nb):
            dve.wait_ge(rstd_done, nb + 1)
            dve.wait_ge(moments_done, (nb + 1) * T)
            nc.vector.scalar_tensor_tensor(shift[:], moments[:, :, 0], -1.0, rstd[:], ALU.mult, ALU.mult
                                           ).then_inc(shift_done, 1)

        def normalise(nb, t):
            if t == 0:
                dve.wait_ge(shift_done, nb + 1)
            if t % TH == 0:
                dve.wait_ge(x1_stored[t // TH], (nb + 1) * 16)
            nc.vector.tensor_scalar(x1[:, t, :], x1[:, t, :], rstd[:, t:t + 1], shift[:, t:t + 1],
                                    ALU.mult, ALU.add).then_inc(normed, 1)

        def conv(b, j, taps):
            u = b * J + j
            v = delta[j % 2]
            for i in taps:
                k = KC - 1 - i
                if i == 0:
                    dve.wait_ge(ssm_copied, (u + 1) * C)
                    ins = nc.vector.tensor_scalar(v[:], conv_in[:, k:k + NT], g.conv_w[:, j, k:k + 1], None, ALU.mult)
                else:
                    dve.wait_ge(conv_step, u * (KC - 1) + i)
                    ins = nc.vector.scalar_tensor_tensor(v[:], conv_in[:, k:k + NT], g.conv_w[:, j, k:k + 1], v[:],
                                                         ALU.mult, ALU.add)
                ins.then_inc(conv_step if i < KC - 1 else conv_done, 1)

        def step_size(b, j):
            u = b * J + j
            dve.wait_ge(soft_done, u + 1)
            nc.vector.scalar_tensor_tensor(delta[j % 2][:], xc_now[j], 0.0, delta[j % 2][:], ALU.max, ALU.add
                                           ).then_inc(delta_done, 1)

        def gate(b, j):
            u = b * J + j
            dve.wait_ge(pair_used, b * (J * N // 2) + (j + 1) * (N // 2))
            dve.wait_ge(res_gated, u + 1)
            for c in range(C):
                s = slice(c * CH, (c + 1) * CH)
                nc.vector.tensor_tensor(res[j % 2][:, s], ps_sum[c][:], res[j % 2][:, s], ALU.mult).then_inc(gated, 1)

        def combine(b, j):
            u = b * J + j
            dve.wait_ge(gated, (u + 1) * C)
            if j == 0:
                dve.wait_ge(out_done, b * G2)
            nc.vector.scalar_tensor_tensor(y_now[j], res[j % 2][:], g.skip[:, j:j + 1], xc_now[j], ALU.add, ALU.mult
                                           ).then_inc(y_done, 1)

        def add_out(b, r, last):
            dve.wait_ge(out_done, b * G2 + r + 1)
            dve.wait_ge(resid_in[r % NRES], (b * (G2 // NRES) + r // NRES + 1) * 16)
            nc.vector.tensor_tensor(resid[r % NRES][:].rearrange("p t d -> p (t d)"), out_bank(r, last)[:],
                                    resid[r % NRES][:].rearrange("p t d -> p (t d)"), ALU.add).then_inc(out_added, 1)

        def finish(b, q, last):
            if q == 2:
                gate(b, J - 1)
                combine(b, J - 1)
            if q in range(OUT, OUT + T, 2):
                add_out(b, (q - OUT) // 2, last)

        def body(b, first, last):
            if not last:
                set_now(b + 1)
            for j in range(J):
                for n in range(N):
                    q = j * N + n
                    if n == 0:
                        dve.wait_ge(drive_done, b * J + j + 1)
                    dve.wait_ge(decay_ready, b * J * N + q + 1)
                    nc.vector.tensor_tensor_scan(state[q % NS][:], state[q % NS][:], drive[j % 2][:], 0.0,
                                                 ALU.mult, ALU.add).then_inc(state_ready, 1)
                    if not first:
                        finish(b - 1, q, False)
                    if j and n == 2:
                        gate(b, j - 1)
                    if j and n == 4:
                        combine(b, j - 1)
                    if not (last and j == J - 1):
                        nb, nj = (b, j + 1) if j < J - 1 else (b + 1, 0)
                        if conv_at(j) <= n < conv_at(j) + KC:
                            conv(nb, nj, (n - conv_at(j),))
                        if n == silu_at(j) + STEP:
                            step_size(nb, nj)
                    if last:
                        continue
                    if ADD <= q < ADD + T:
                        add_routed(b + 1, q - ADD)
                    if q == ADD + T:
                        aggregate(b + 1)
                    if q == SCALES:
                        scales(b + 1)
                    if SCALES <= q < SCALES + 4:
                        for t in range(4 * (q - SCALES), 4 * (q - SCALES) + 4):
                            normalise(b + 1, t)

        nc.vector.memset(conv_in[:, 0:KC - 1], 0.0).then_inc(setup, 1)
        nc.vector.memset(eps[:], LN_EPS).then_inc(setup, 1)
        set_now(0)
        for t in range(T):
            add_routed(0, t)
        aggregate(0)
        scales(0)
        for t in range(T):
            normalise(0, t)
        dve.wait_ge(setup, 2)
        conv(0, 0, range(KC))
        step_size(0, 0)
        batches(dve, body)
        for q in range(OUT + T):
            finish(NB - 1, q, True)

    @block.scalar
    def _(act):
        def read_bank(nb, s):
            act.wait_ge(pick_turned, nb * SL + min(s + 1, SL))
            act.wait_ge(expert_done, nb * SL + s)
            if s < SL:
                nc.scalar.copy(picked_t[s % 2][:].rearrange("p k n -> p (k n)"), ps_rows[0][:, 0:KD * P]
                               ).then_inc(pick_copied, 1)
            if s == 1:
                act.wait_ge(now_set, (nb + 1) * 3)
            if s:
                act.wait_ge(routed_out[(s - 1) % NY], (nb * (SL // NY) + (s - 1) // NY) * 16)
                nc.scalar.activation(routed[(s - 1) % NY][:], ps_rows[0][:, CH - D:CH], ACT.Identity,
                                     scale=gate_now[:, s - 1:s]).then_inc(routed_scaled, 1)

        def deviation(nb):
            act.wait_ge(moments_done, (nb + 1) * T)
            act.wait_ge(normed, nb * T)
            nc.scalar.activation(rstd[:], moments[:, :, 1], ACT.Ln, bias=eps[:, 0:1]).then_inc(log_done, 1)
            act.wait_ge(log_done, nb + 1)
            nc.scalar.activation(rstd[:], rstd[:], ACT.Exp, scale=-0.5).then_inc(rstd_done, 1)

        def copy_turned(nb, i):
            act.wait_ge(x1_turned, nb * G2 + i + 1)
            nc.scalar.copy(x1t[:].rearrange("p k (n t) -> p t k n", t=T)[:, 2 * i:2 * i + 2],
                           ps_rows[i % 2][:].rearrange("p (t k n) -> p t k n", t=2, k=KD)).then_inc(x1t_copied, 1)

        def copy_ssm(b, j, c):
            u = b * J + j
            act.wait_ge(ssm_done, u * C + c + 1)
            if c == 0:
                act.wait_ge(conv_done, u)
            nc.scalar.copy(conv_in[:, KC - 1 + c * CH:KC - 1 + (c + 1) * CH], ps_proj[c % 2][:]).then_inc(ssm_copied, 1)

        def copy_res(b, j, c):
            u = b * J + j
            act.wait_ge(res_done, u * C + c + 1)
            if c == 0:
                act.wait_ge(y_done, count(u - 1))
            nc.scalar.copy(res[j % 2][:, c * CH:(c + 1) * CH], ps_proj[c % 2][:]).then_inc(res_copied, 1)

        def gate_res(b, j):
            u = b * J + j
            act.wait_ge(res_copied, (u + 1) * C)
            nc.scalar.activation(res[j % 2][:], res[j % 2][:], ACT.Silu).then_inc(res_gated, 1)

        def activate(b, j):
            u = b * J + j
            act.wait_ge(conv_done, u + 1)
            if j == 1:
                act.wait_ge(y_done, b * J)
            elif j == 2:
                act.wait_ge(out_done, b * G2)
            elif j == 3:
                act.wait_ge(y_done, b * J + 2)
            else:
                act.wait_ge(x1_turned, (b + 1) * G2)
            nc.scalar.activation(xc_now[j], delta[j % 2][:], ACT.Silu, bias=g.conv_b[:, j:j + 1]).then_inc(xc_done, 1)

        def magnitude(b, j):
            u = b * J + j
            act.wait_ge(xc_done, u + 1)
            nc.scalar.activation(delta[j % 2][:], xc_now[j], ACT.Abs).then_inc(soft_step, 1)

        def soft_exp(b, j):
            u = b * J + j
            act.wait_ge(soft_step, 2 * u + 1)
            nc.scalar.activation(delta[j % 2][:], delta[j % 2][:], ACT.Exp, scale=-1.0).then_inc(soft_step, 1)

        def soft_log(b, j):
            u = b * J + j
            act.wait_ge(soft_step, 2 * u + 2)
            nc.scalar.activation(delta[j % 2][:], delta[j % 2][:], ACT.Ln, bias=1.0).then_inc(soft_done, 1)

        def both_tables():
            nc.scalar.preload_act_table_set("natural_log_exp_and_others")

        def body(b, first, last):
            for j in range(J):
                for n in range(N):
                    q = j * N + n
                    if n == 0:
                        act.wait_ge(delta_done, b * J + j + 1)
                    before = q - NS if q >= NS else max(v for v in range(J * N) if v % NS == q) - J * N
                    act.wait_ge(pair_used if q % 2 else pair_added, count(b * (J * N // 2) + before // 2 + 1))
                    nc.scalar.activation(state[q % NS][:], delta[j % 2][:], ACT.Exp, scale=g.neg_a[:, j, n:n + 1]
                                         ).then_inc(decay_ready, 1)
                    if not last and FFN <= q <= FFN + SL:
                        read_bank(b + 1, q - FFN)
                    chunk = projections(b, q, last)
                    if chunk:
                        (copy_ssm if chunk[0] == "ssm" else copy_res)(*chunk[1:])
                    if not last and q == SCALES + 1:
                        deviation(b + 1)
                    if not last and TURN <= q < TURN + 4:
                        for i in range(2 * (q - TURN), 2 * (q - TURN) + 2):
                            copy_turned(b + 1, i)
                    if n == silu_at(j):
                        gate_res(b, j)
                    if not (last and j == J - 1):
                        nb, nj = (b, j + 1) if j < J - 1 else (b + 1, 0)
                        if n == silu_at(j):
                            activate(nb, nj)
                        if n == silu_at(j) + 1:
                            magnitude(nb, nj)
                        if n == silu_at(j) + 2:
                            soft_exp(nb, nj)
                        if n == silu_at(j) + 3:
                            soft_log(nb, nj)
                    if n == silu_at(j):
                        both_tables()

        for s in range(SL + 1):
            if s < SL:
                act.wait_ge(pick_turned, s + 1)
                act.wait_ge(expert_done, count(s - 1))
                nc.scalar.copy(picked_t[s % 2][:].rearrange("p k n -> p (k n)"), ps_sum[s % 2][:, 0:KD * P]
                               ).then_inc(pick_copied, 1)
            if s:
                act.wait_ge(expert_done, s)
                act.wait_ge(now_set, 3)
                act.wait_ge(routed_out[(s - 1) % NY], (s - 1) // NY * 16)
                nc.scalar.activation(routed[(s - 1) % NY][:], ps_sum[2 + (s - 1) % 2][:, 0:D], ACT.Identity,
                                     scale=gate_now[:, s - 1:s]).then_inc(routed_scaled, 1)
        act.wait_ge(setup, 2)
        both_tables()
        deviation(0)
        for i in range(G2):
            copy_turned(0, i)
        for c in range(C):
            copy_ssm(0, 0, c)
        for c in range(C):
            copy_res(0, 0, c)
        activate(0, 0)
        both_tables()
        magnitude(0, 0)
        soft_exp(0, 0)
        soft_log(0, 0)
        for c in range(C):
            copy_ssm(0, 1, c)
        batches(act, body)

    @block.tensor
    def _(pe):
        def fill_bank(nb, s):
            if s:
                pe.wait_ge(pick_copied, nb * SL + s)
                pe.wait_ge(routed_scaled, nb * SL + s - 1)
            else:
                pe.wait_ge(x1t_copied, nb * G2)
            if s:
                e = (s - 1) // NH
                pe.wait_ge(expert_in[e % 2], (nb * (E // 2) + e // 2 + 1) * 16)
                for k in range(KD):
                    mm = nc.tensor.matmul(ps_rows[0][:, CH - D:CH], picked_t[(s - 1) % 2][:, k, :], expert[e % 2][:, k, :],
                                          start=(k == 0), stop=(k == KD - 1))
                mm.then_inc(expert_done, 1)
            if s < SL:
                full = [len([v for v in range(SL) if v % NX == i]) for i in range(NX)]
                pe.wait_ge(picked_in[s % NX], (nb * full[s % NX] + s // NX + 1) * 16)
                for k in range(KD):
                    mm = nc.tensor.transpose(ps_rows[0][:, k * P:(k + 1) * P], picked[s % NX][:, k * P:(k + 1) * P], g.ident[:])
                mm.then_inc(pick_turned, 1)

        def turn_x1(nb, i):
            pe.wait_ge(normed, nb * T + 2 * i + 2)
            if i >= 2:
                pe.wait_ge(x1t_copied, count(nb * G2 + i - 1))
            elif i == 0:
                pe.wait_ge(routed_scaled, (nb + 1) * SL)
            else:
                pe.wait_ge(out_added, count((nb - 1) * G2))
            for t in (2 * i, 2 * i + 1):
                for k in range(KD):
                    c = (t % 2) * KD + k
                    mm = nc.tensor.transpose(ps_rows[i % 2][:, c * P:(c + 1) * P], x1[:, t, k * P:(k + 1) * P], g.ident[:])
            mm.then_inc(x1_turned, 1)

        def project(bank, col, c):
            for k in range(KD):
                mm = nc.tensor.matmul(ps_proj[bank][:], g.w_in[:, k, col:col + P], x1t[:, k, c * CH:(c + 1) * CH],
                                      start=(k == 0), stop=(k == KD - 1))
            return mm

        def project_ssm(b, j, c):
            u = b * J + j
            if c == 0:
                pe.wait_ge(x1t_copied, (b + 1) * G2)
            if c >= 2:
                pe.wait_ge(ssm_copied, count(u * C + c - 1))
            elif j == 2:
                pe.wait_ge(ssm_copied, u * C)
            else:
                pe.wait_ge(res_copied, count((u, u, None, u - 1)[j] * C))
            project(c % 2, j * P, c).then_inc(ssm_done, 1)

        def project_res(b, j, c):
            u = b * J + j
            if c >= 2:
                pe.wait_ge(res_copied, count(u * C + c - 1))
            elif j < J - 1:
                pe.wait_ge(ssm_copied, (u + (2 if j else 1)) * C)
            else:
                pe.wait_ge(res_copied, u * C)
            project(c % 2, INNER + j * P, c).then_inc(res_done, 1)

        def project_out(b, r, last):
            if r:
                pe.wait_ge(out_added, b * G2 + (r - 1 if last else r))
            else:
                pe.wait_ge(y_done, (b + 1) * J)
                pe.wait_ge(x1t_copied, NB * G2 if last else (b + 2) * G2)
            for t in (2 * r, 2 * r + 1):
                for j in range(J):
                    mm = nc.tensor.matmul(out_bank(r, last)[:, (t % 2) * D:(t % 2 + 1) * D],
                                          y_now[j].rearrange("p (n t) -> p n t", t=T)[:, :, t],
                                          g.w_out[:, j, :], start=(j == 0), stop=(j == J - 1))
            mm.then_inc(out_done, 1)

        def beside(b, v, last):
            j, n = v // N, v % N
            if not last and FFN <= v <= FFN + SL:
                fill_bank(b + 1, v - FFN)
            chunk = projections(b, v, last)
            if chunk:
                (project_ssm if chunk[0] == "ssm" else project_res)(*chunk[1:])
            if not last and TURN <= v < TURN + 4:
                for i in range(2 * (v - TURN), 2 * (v - TURN) + 2):
                    turn_x1(b + 1, i)

        def body(b, first, last):
            for v in range(LEAD):
                beside(b, v, last)
            for j in range(J):
                for n in range(1, N, 2):
                    q = j * N + n
                    for c in range(C):
                        if c == 0:
                            pe.wait_ge(pair_added, b * (J * N // 2) + q // 2 + 1)
                        if n == 1:
                            pe.wait_ge(gated, count((b * J + j - 1) * C + c + 1))
                        mm = nc.tensor.matmul(ps_sum[c][:], g.ident[:], state[q % NS][:, c * CH:(c + 1) * CH],
                                              start=(n == 1), stop=(n == N - 1))
                    mm.then_inc(pair_used, 1)
                    if q + LEAD - 1 < J * N:
                        beside(b, q + LEAD - 1, last)
                    if not first and q < T:
                        project_out(b - 1, q // 2, False)
                    if q + LEAD < J * N:
                        beside(b, q + LEAD, last)

        for s in range(SL + 1):
            if s < SL:
                pe.wait_ge(picked_in[s % NX], (s // NX + 1) * 16)
                pe.wait_ge(pick_copied, count(s - 1))
                for k in range(KD):
                    mm = nc.tensor.transpose(ps_sum[s % 2][:, k * P:(k + 1) * P], picked[s % NX][:, k * P:(k + 1) * P], g.ident[:])
                mm.then_inc(pick_turned, 1)
            if s:
                e = (s - 1) // NH
                pe.wait_ge(pick_copied, s)
                pe.wait_ge(routed_scaled, count(s - 2))
                pe.wait_ge(expert_in[e % 2], (e // 2 + 1) * 16)
                for k in range(KD):
                    mm = nc.tensor.matmul(ps_sum[2 + (s - 1) % 2][:, 0:D], picked_t[(s - 1) % 2][:, k, :], expert[e % 2][:, k, :],
                                          start=(k == 0), stop=(k == KD - 1))
                mm.then_inc(expert_done, 1)
        for i in range(G2):
            turn_x1(0, i)
        for c in range(C):
            project_ssm(0, 0, c)
        for c in range(C):
            project_res(0, 0, c)
        for c in range(C):
            project_ssm(0, 1, c)
        batches(pe, body)
        for r in range(G2):
            project_out(NB - 1, r, True)


def ffn(nc, g, x, out, ctx):
    def sb(name, shape, dt=F32):
        return ctx.enter_context(nc.sbuf_tensor(name, shape, dt))

    def sem(name):
        return ctx.enter_context(nc.semaphore(name))

    def ps(name):
        return ctx.enter_context(nc.psum_tensor(name, [P, CH], F32))

    NX = NY = NK = 8
    NT4 = 4
    BRING, JOIN = SL + 6, SL + 10
    expert = sb("f_expert", [P, E, KD, D])
    slot_now = [sb(f"f_slot_now{i}", [P, SL], I32) for i in range(2)]
    row_now = [sb(f"f_row_now{i}", [P, T], I32) for i in range(2)]
    picked = [sb(f"f_picked{i}", [P, D]) for i in range(NX)]
    picked_t = [sb(f"f_picked_t{i}", [P, KD, P]) for i in range(NT4)]
    routed = [sb(f"f_routed{i}", [P, D]) for i in range(NY)]
    back = [sb(f"f_back{i}", [P, D]) for i in range(NK)]
    total = [sb(f"f_total{i}", [P, T, D]) for i in range(2)]
    ps_turn = [ps(f"f_ps_turn{i}") for i in range(NT4)]
    ps_out = [ps(f"f_ps_out{i}") for i in range(NT4)]
    expert_in, now_set, rows_set = sem("f_expert_in"), sem("f_now_set"), sem("f_rows_set")
    picked_in = [sem(f"f_picked_in{i}") for i in range(NX)]
    routed_out = [sem(f"f_routed_out{i}") for i in range(NY)]
    back_in = [sem(f"f_back_in{i}") for i in range(NK)]
    x_in = [sem(f"f_x_in{i}") for i in range(2)]
    out_stored = [sem(f"f_out_stored{i}") for i in range(2)]
    turned, copied, product, scaled, added = (
        sem(n) for n in ("f_turned", "f_copied", "f_product", "f_scaled", "f_added"))
    x_v = x.rearrange("b (p t) d -> b p t d", t=T)
    out_v = out.rearrange("b (p t) d -> b p t d", t=T)
    routed_v = [table.rearrange("(m e) d -> e m d", e=E) for table in g.routed]
    block = ctx.enter_context(nc.Block())

    def rounds(eng, turn):
        turn(0, 0)
        turn(0, 1)
        with eng.Fori(1, NB // 2 - 1) as i:
            turn(i, 0)
            turn(i, 1)
        for i in range(NB // 2 - 1, NB // 2 + 1):
            turn(i, 0)
            turn(i, 1)

    def there(b):
        return not isinstance(b, int) or 0 <= b < NB

    def behind(i, odd, s, lag):
        k = (lag - s + SL - 1) // SL
        return 2 * i + odd - k, s - lag + SL * k, (odd - k) % 2, i + (odd - k) // 2

    @block.sync
    def _(sp):
        def load_x(b, odd):
            sp.dma_start(total[odd][:], x_v[bass.ds(b, 1)].rearrange("a p t d -> p (a t) d")).then_inc(x_in[odd], 16)

        def turn(i, odd):
            b = 2 * i + odd
            for s in range(SL):
                e, h = s // NH, s % NH
                if there(b):
                    if s == 0:
                        for k in range(NK):
                            sp.wait_ge(back_in[k], count((b - 1) * 16 * (T // NK)))
                            sp.sem_inc(g.passed_sp, 1)
                    sp.wait_ge(scaled, b * SL + s + 1)
                    sp.dma_start(routed_v[odd][e, 1 + h * P:1 + (h + 1) * P, :],
                                 routed[s % NY][:]).then_inc(routed_out[s % NY], 16)
                if s == JOIN - SL + 2 and there(b - 2):
                    sp.wait_ge(added, (b - 1) * T)
                    sp.dma_start(out_v[bass.ds(b - 2, 1)].rearrange("a p t d -> p (a t) d"), total[odd][:]
                                 ).then_inc(out_stored[odd], 16)
            if there(b) and there(b - 2):
                sp.wait_ge(out_stored[odd], i * 16)
                load_x(b, odd)

        for e in range(E):
            sp.dma_start(expert[:, e, :, :], g.experts[e].rearrange("(k p) f -> p k f", p=P)).then_inc(expert_in, 16)
        load_x(0, 0)
        load_x(1, 1)
        rounds(sp, turn)
        for odd in range(2):
            sp.wait_ge(out_stored[odd], NB // 2 * 16)

    @block.gpsimd
    def _(pool):
        def turn(i, odd):
            b = 2 * i + odd
            for s in range(SL):
                if there(b):
                    if s == 0:
                        pool.wait_ge(now_set, b + 1)
                    pool.wait_ge(turned, count(b * SL + s - NX + 1))
                    pool.sem_inc(g.passed_pool, 1)
                    nc.gpsimd.indirect_dma_start(
                        out=picked[s % NX][:], out_offset=None, in_=g.normed,
                        in_offset=bass.IndirectOffsetOnAxis(ap=slot_now[odd][:, s:s + 1].bitcast(U32), axis=0)
                    ).then_inc(picked_in[s % NX], 16)
                m, t, table, _ = behind(i, odd, s, BRING)
                if there(m):
                    if t == 0:
                        pool.wait_ge(rows_set, m + 1)
                        for k in range(NY):
                            pool.wait_ge(routed_out[k], (m + 1) * 16 * (SL // NY))
                    pool.wait_ge(added, count(m * T + t - NK + 1))
                    pool.sem_inc(g.passed_pool, 1)
                    nc.gpsimd.indirect_dma_start(
                        out=back[t % NK][:], out_offset=None, in_=g.routed[table],
                        in_offset=bass.IndirectOffsetOnAxis(ap=row_now[table][:, t:t + 1].bitcast(U32), axis=0)
                    ).then_inc(back_in[t % NK], 16)

        rounds(pool, turn)

    @block.vector
    def _(dve):
        def set_slots(b, odd):
            for k in range(NX):
                dve.wait_ge(picked_in[k], count((b - 1) * 16 * (SL // NX)))
            nc.vector.tensor_copy(slot_now[odd][:], g.slot_token[:, bass.ds(b, 1), :].rearrange("p a s -> p (a s)")
                                  ).then_inc(now_set, 1)

        def set_rows(b, odd):
            for k in range(NK):
                dve.wait_ge(back_in[k], count((b - 1) * 16 * (T // NK)))
            nc.vector.tensor_copy(row_now[odd][:], g.token_row[:, bass.ds(b, 1), :].rearrange("p a s -> p (a s)")
                                  ).then_inc(rows_set, 1)

        def turn(i, odd):
            b = 2 * i + odd
            for s in range(SL):
                if there(b):
                    dve.wait_ge(turned, b * SL + s + 1)
                    dve.wait_ge(product, count(b * SL + s - NT4 + 1))
                    nc.vector.tensor_copy(picked_t[s % NT4][:].rearrange("p k n -> p (k n)"),
                                          ps_turn[s % NT4][:, 0:KD * P]).then_inc(copied, 1)
                if s == 2 and there(b + 1) and not (isinstance(b, int) and b < 0):
                    set_slots(b + 1, 1 - odd)
                m, t, table, turn_of = behind(i, odd, s, JOIN)
                if there(m):
                    if t == 0:
                        dve.wait_ge(x_in[table], (turn_of + 1) * 16)
                    dve.wait_ge(back_in[t % NK], (m * (T // NK) + t // NK + 1) * 16)
                    nc.vector.tensor_tensor(total[table][:, t, :], total[table][:, t, :], back[t % NK][:], ALU.add
                                            ).then_inc(added, 1)
                if s == JOIN - SL and there(b):
                    set_rows(b, odd)

        set_slots(0, 0)
        rounds(dve, turn)

    @block.scalar
    def _(act):
        def slots(b):
            for s in range(SL):
                act.wait_ge(product, b * SL + s + 1)
                act.wait_ge(routed_out[s % NY], (b * (SL // NY) + s // NY) * 16)
                nc.scalar.activation(routed[s % NY][:], ps_out[s % NT4][:, 0:D], ACT.Identity,
                                     scale=g.slot_gate[:, bass.ds(b, 1), s:s + 1].rearrange("p a s -> p (a s)")).then_inc(scaled, 1)

        slots(0)
        with act.Fori(1, NB) as b:
            slots(b)

    @block.tensor
    def _(pe):
        def turn(b, s):
            pe.wait_ge(picked_in[s % NX], (b * (SL // NX) + s // NX + 1) * 16)
            pe.wait_ge(copied, count(b * SL + s - NT4 + 1))
            for k in range(KD):
                mm = nc.tensor.transpose(ps_turn[s % NT4][:, k * P:(k + 1) * P], picked[s % NX][:, k * P:(k + 1) * P], g.ident[:])
            mm.then_inc(turned, 1)

        def apply_expert(b, s):
            pe.wait_ge(copied, b * SL + s + 1)
            pe.wait_ge(scaled, count(b * SL + s - NT4 + 1))
            for k in range(KD):
                mm = nc.tensor.matmul(ps_out[s % NT4][:, 0:D], picked_t[s % NT4][:, k, :], expert[:, s // NH, k, :],
                                      start=(k == 0), stop=(k == KD - 1))
            mm.then_inc(product, 1)

        def slots(b):
            for s in range(SL + 1):
                if s < SL:
                    turn(b, s)
                if s == 1 and isinstance(b, int):
                    pe.wait_ge(expert_in, E * 16)
                if s:
                    apply_expert(b, s - 1)

        slots(0)
        with pe.Fori(1, NB) as b:
            slots(b)


def program(nc, w, g):
    with ExitStack() as ctx:
        constants(nc, g, w, ctx)
        route(nc, g, w.x, "in")
        with ExitStack() as c1:
            mixer(nc, g, w.x, c1)
        route(nc, g, g.x2, "mid")
        with ExitStack() as c1:
            ffn(nc, g, g.x2, w.out, c1)


def kernel(L0_attn_x, L0_attn_W_in, L0_attn_conv_w, L0_attn_conv_b, L0_attn_A_log, L0_attn_D, L0_attn_W_out,
           L0_ffn_gate_w, L0_ffn_experts):
    import concourse.bacc as bacc
    from concourse.bass_utils import run_bass_kernel_spmd

    nc = bacc.Bacc("TRN2", target_bir_lowering=False, num_devices=1)
    arrays = {}

    def given(name, a):
        a = np.ascontiguousarray(a)
        arrays[name] = a
        return nc.dram_tensor(name, a.shape, mybir.dt.from_np(a.dtype), kind="ExternalInput").ap()

    w, g = Bag(), Bag()
    w.x = given("in_x", L0_attn_x)
    w.A_log = given("in_a_log", L0_attn_A_log)
    w.w_in_t = given("in_w_in_t", L0_attn_W_in.T)
    w.w_out_t = given("in_w_out_t", L0_attn_W_out.T)
    w.conv_w = given("in_conv_w", L0_attn_conv_w.reshape(INNER, KC))
    w.conv_b_t = given("in_conv_b_t", L0_attn_conv_b.reshape(J, P).T)
    w.skip_t = given("in_skip_t", L0_attn_D.reshape(J, P).T)
    w.gate_w = given("in_gate_w", L0_ffn_gate_w)
    g.experts = given("in_experts", L0_ffn_experts)
    w.out = nc.dram_tensor("out", (NB, NT, D), F32, kind="ExternalOutput").ap()
    g.normed = nc.dram_tensor("normed_rows", (NB * NT, D), F32).ap()
    g.routed = [nc.dram_tensor(f"routed_rows{i}", (YR, D), F32).ap() for i in range(2)]
    g.x1 = nc.dram_tensor("x1_rows", (NB * NT, D), F32).ap()
    g.x2 = nc.dram_tensor("x2_rows", (NB, NT, D), F32).ap()
    program(nc, w, g)
    r = run_bass_kernel_spmd(nc, [arrays], core_ids=[0])
    return r.results[0]["out"]
```
